# Optimizing a Trainium2 kernel written in Bass

```python
import numpy as np
import jax
import jax.numpy as jnp

def _softmax(x, axis=-1):
    return jax.nn.softmax(x, axis=axis)

def _gelu(x):
    return jax.nn.gelu(x, approximate=True)

def _silu(x):
    return jax.nn.silu(x)

def _sigmoid(x):
    return jax.nn.sigmoid(x)

def _layernorm(x, axis=-1, eps=1e-05):
    m = jnp.mean(x, axis=axis, keepdims=True)
    v = jnp.var(x, axis=axis, keepdims=True)
    return (x - m) / jnp.sqrt(v + eps)

def _scatter_add(tgt, idx, src, axis=0):
    return tgt.at[idx].add(src)

def _segment_sum(src, seg, n):
    return jax.ops.segment_sum(src, seg, n)
kernel_name = 'mk_seq_postln_d2_jaxref_r4_33772b'

def setup_inputs(seed: int=0):
    np.random.seed(seed)
    _w = jnp.asarray

    def _L0_attn_setup():
        import jax, jax.numpy as jnp
        import numpy as np
        from jax import lax

        def _silu(x):
            return x * jax.nn.sigmoid(x)

        def _selective_scan(u, delta, A, B, C):
            b, l, d = u.shape
            n = A.shape[1]
            deltaA = jnp.exp(delta[..., None] * A)
            deltaBu = (delta * u)[..., None] * B[:, :, None, :]

            def step(h, inp):
                dA, dBu, c = inp
                h = dA * h + dBu
                y = jnp.einsum('bdn,bn->bd', h, c)
                return (h, y)
            h0 = jnp.zeros((b, d, n), u.dtype)
            xs = (jnp.moveaxis(deltaA, 1, 0), jnp.moveaxis(deltaBu, 1, 0), jnp.moveaxis(C, 1, 0))
            _, ys = lax.scan(step, h0, xs)
            return jnp.moveaxis(ys, 0, 1)
        key = jax.random.key(seed)
        ks = jax.random.split(key, 9)
        b, l, h = (2, 512, 256)
        d, n, r, k = (512, 16, 64, 4)
        s = lambda *sh: 1.0 / np.sqrt(sh[-1])
        return {'x': jax.random.normal(ks[0], (b, l, h), jnp.float32), 'W_in': jax.random.normal(ks[1], (2 * d, h), jnp.float32) * s(h), 'conv_w': jax.random.normal(ks[2], (d, 1, k), jnp.float32) * s(k), 'conv_b': jax.random.normal(ks[3], (d,), jnp.float32) * 0.02, 'W_x': jax.random.normal(ks[4], (r + 2 * n, d), jnp.float32) * s(d), 'W_dt': jax.random.normal(ks[5], (d, r), jnp.float32) * s(r), 'b_dt': jax.random.normal(ks[6], (d,), jnp.float32) * 0.02, 'A_log': jax.random.normal(ks[7], (d, n), jnp.float32) * 0.1, 'W_out': jax.random.normal(ks[8], (h, d), jnp.float32) * s(d)}
    _L0_attn_in = _L0_attn_setup()

    def _L0_ffn_setup():
        import jax, jax.numpy as jnp
        import numpy as np

        def _binarize(w):
            alpha = jax.lax.stop_gradient(jnp.mean(jnp.abs(w), axis=1, keepdims=True))
            bw = alpha * jnp.sign(w)
            return w + jax.lax.stop_gradient(bw - w)
        key = jax.random.key(seed)
        k1, k2, k3, k4, k5 = jax.random.split(key, 5)
        D, H = (256, 1024)
        x = jax.random.normal(k1, (64, 196, D), dtype=jnp.float32)
        w1 = jax.random.normal(k2, (H, D), dtype=jnp.float32) * 0.02
        b1 = jax.random.normal(k3, (H,), dtype=jnp.float32) * 0.02
        w2 = jax.random.normal(k4, (D, H), dtype=jnp.float32) * 0.02
        b2 = jax.random.normal(k5, (D,), dtype=jnp.float32) * 0.02
        return {'x': x, 'w1': w1, 'b1': b1, 'w2': w2, 'b2': b2}
    _L0_ffn_in = _L0_ffn_setup()

    def _L1_attn_setup():
        import math
        import jax, jax.numpy as jnp
        import numpy as np
        N_HEADS = 16
        LOCAL_HEADS = 8
        GLOBAL_HEADS = N_HEADS - LOCAL_HEADS
        WINDOW = 64
        NEG_INF = -1e+30
        key = jax.random.key(seed)
        ks = jax.random.split(key, 6)
        B, S, E = (1, 1024, 256)
        inp = {'hidden_states': jax.random.normal(ks[0], (B, S, E), dtype=jnp.float32), 'Wq': jax.random.normal(ks[1], (E, E), dtype=jnp.float32) * (1.0 / math.sqrt(E)), 'Wk': jax.random.normal(ks[2], (E, E), dtype=jnp.float32) * (1.0 / math.sqrt(E)), 'Wv': jax.random.normal(ks[3], (E, E), dtype=jnp.float32) * (1.0 / math.sqrt(E)), 'Wo': jax.random.normal(ks[4], (E, E), dtype=jnp.float32) * (1.0 / math.sqrt(E)), 'bo': jnp.zeros((E,), dtype=jnp.float32)}
        return inp
    _L1_attn_in = _L1_attn_setup()

    def _L1_ffn_setup():
        import jax, jax.numpy as jnp
        import numpy as np
        B, L, D = (2, 512, 256)
        E = 15
        H = D * 1
        K = 3
        T = 1.0
        key = jax.random.key(seed)
        ks = jax.random.split(key, 12)
        s = 0.02
        return {'x': jax.random.normal(ks[0], (B, L, D), dtype=jnp.float32), 'router_W': jax.random.normal(ks[1], (D, E), dtype=jnp.float32) * s, 'router_b': jnp.zeros((E,), dtype=jnp.float32), 'sW1': jax.random.normal(ks[2], (D, H), dtype=jnp.float32) * s, 'sb1': jnp.zeros((H,), dtype=jnp.float32), 'sW2': jax.random.normal(ks[3], (H, D), dtype=jnp.float32) * s, 'sb2': jnp.zeros((D,), dtype=jnp.float32), 'eW1': jax.random.normal(ks[4], (E, D, H), dtype=jnp.float32) * s, 'eb1': jnp.zeros((E, H), dtype=jnp.float32), 'eW2': jax.random.normal(ks[5], (E, H, D), dtype=jnp.float32) * s, 'eb2': jnp.zeros((E, D), dtype=jnp.float32)}
    _L1_ffn_in = _L1_ffn_setup()
    _d = {'L0_attn_x': _L0_attn_in['x'], 'L0_attn_W_in': _L0_attn_in['W_in'], 'L0_attn_conv_w': _L0_attn_in['conv_w'], 'L0_attn_conv_b': _L0_attn_in['conv_b'], 'L0_attn_W_x': _L0_attn_in['W_x'], 'L0_attn_W_dt': _L0_attn_in['W_dt'], 'L0_attn_b_dt': _L0_attn_in['b_dt'], 'L0_attn_A_log': _L0_attn_in['A_log'], 'L0_attn_W_out': _L0_attn_in['W_out'], 'L0_ffn_w1': _L0_ffn_in['w1'], 'L0_ffn_b1': _L0_ffn_in['b1'], 'L0_ffn_w2': _L0_ffn_in['w2'], 'L0_ffn_b2': _L0_ffn_in['b2'], 'L1_attn_Wq': _L1_attn_in['Wq'], 'L1_attn_Wk': _L1_attn_in['Wk'], 'L1_attn_Wv': _L1_attn_in['Wv'], 'L1_attn_Wo': _L1_attn_in['Wo'], 'L1_attn_bo': _L1_attn_in['bo'], 'L1_ffn_router_W': _L1_ffn_in['router_W'], 'L1_ffn_router_b': _L1_ffn_in['router_b'], 'L1_ffn_sW1': _L1_ffn_in['sW1'], 'L1_ffn_sb1': _L1_ffn_in['sb1'], 'L1_ffn_sW2': _L1_ffn_in['sW2'], 'L1_ffn_sb2': _L1_ffn_in['sb2'], 'L1_ffn_eW1': _L1_ffn_in['eW1'], 'L1_ffn_eb1': _L1_ffn_in['eb1'], 'L1_ffn_eW2': _L1_ffn_in['eW2'], 'L1_ffn_eb2': _L1_ffn_in['eb2']}
    _x0 = _d['L0_attn_x']
    _d['L0_attn_x'] = jax.random.normal(jax.random.fold_in(jax.random.key(seed), 1), (4, 1024, 256), dtype=_x0.dtype)
    del _x0
    return _d

def reference(L0_attn_x, L0_attn_W_in, L0_attn_conv_w, L0_attn_conv_b, L0_attn_W_x, L0_attn_W_dt, L0_attn_b_dt, L0_attn_A_log, L0_attn_W_out, L0_ffn_w1, L0_ffn_b1, L0_ffn_w2, L0_ffn_b2, L1_attn_Wq, L1_attn_Wk, L1_attn_Wv, L1_attn_Wo, L1_attn_bo, L1_ffn_router_W, L1_ffn_router_b, L1_ffn_sW1, L1_ffn_sb1, L1_ffn_sW2, L1_ffn_sb2, L1_ffn_eW1, L1_ffn_eb1, L1_ffn_eW2, L1_ffn_eb2):

    def _L0_attn_ref(x, W_in, conv_w, conv_b, W_x, W_dt, b_dt, A_log, W_out):
        import jax, jax.numpy as jnp
        import numpy as np
        from jax import lax

        def _silu(x):
            return x * jax.nn.sigmoid(x)

        def _selective_scan(u, delta, A, B, C):
            b, l, d = u.shape
            n = A.shape[1]
            deltaA = jnp.exp(delta[..., None] * A)
            deltaBu = (delta * u)[..., None] * B[:, :, None, :]

            def step(h, inp):
                dA, dBu, c = inp
                h = dA * h + dBu
                y = jnp.einsum('bdn,bn->bd', h, c)
                return (h, y)
            h0 = jnp.zeros((b, d, n), u.dtype)
            xs = (jnp.moveaxis(deltaA, 1, 0), jnp.moveaxis(deltaBu, 1, 0), jnp.moveaxis(C, 1, 0))
            _, ys = lax.scan(step, h0, xs)
            return jnp.moveaxis(ys, 0, 1)
        b, l, _ = x.shape
        d, n = A_log.shape
        r = W_dt.shape[1]
        k = conv_w.shape[-1]
        xr = jnp.einsum('blh,eh->ble', x, W_in)
        xs, res = (xr[..., :d], xr[..., d:])
        xp = jnp.pad(xs, ((0, 0), (k - 1, 0), (0, 0)))
        xc = lax.conv_general_dilated(jnp.transpose(xp, (0, 2, 1)), conv_w, (1,), 'VALID', dimension_numbers=('NCH', 'OIH', 'NCH'), feature_group_count=d)
        xc = jnp.transpose(xc, (0, 2, 1)) + conv_b
        xc = _silu(xc)
        x_dbl = jnp.einsum('bld,ed->ble', xc, W_x)
        dt, B, C = (x_dbl[..., :r], x_dbl[..., r:r + n], x_dbl[..., r + n:])
        delta = jax.nn.softplus(jnp.einsum('blr,dr->bld', dt, W_dt) + b_dt)
        A = -jnp.exp(A_log.astype(jnp.float32))
        y = lax.stop_gradient(_selective_scan(xc, delta, A, B, C))
        return jnp.einsum('bld,hd->blh', y * _silu(res), W_out)

    def _L0_ffn_ref(x, w1, b1, w2, b2):
        import jax, jax.numpy as jnp
        import numpy as np

        def _binarize(w):
            alpha = jax.lax.stop_gradient(jnp.mean(jnp.abs(w), axis=1, keepdims=True))
            bw = alpha * jnp.sign(w)
            return w + jax.lax.stop_gradient(bw - w)
        bw1 = _binarize(w1)
        h = jnp.einsum('bsd,hd->bsh', x, bw1) + b1
        h = jax.nn.gelu(h, approximate=False)
        bw2 = _binarize(w2)
        out = jnp.einsum('bsh,dh->bsd', h, bw2) + b2
        return out

    def _L1_attn_ref(hidden_states, Wq, Wk, Wv, Wo, bo):
        import math
        import jax, jax.numpy as jnp
        import numpy as np
        N_HEADS = 16
        LOCAL_HEADS = 8
        GLOBAL_HEADS = N_HEADS - LOCAL_HEADS
        WINDOW = 64
        NEG_INF = -1e+30
        B, S, E = hidden_states.shape
        H, D = (N_HEADS, E // N_HEADS)
        scale = 1.0 / math.sqrt(D)

        def proj(W):
            y = jnp.einsum('bse,fe->bsf', hidden_states, W)
            return y.reshape(B, S, H, D).transpose(0, 2, 1, 3)
        q = proj(Wq) * scale
        k = proj(Wk)
        v = proj(Wv)
        i = jnp.arange(S)[:, None]
        j = jnp.arange(S)[None, :]
        causal = j <= i
        local = causal & (j >= i - WINDOW)

        def attend(qh, kh, vh, mask):
            scores = jnp.einsum('bhsd,bhtd->bhst', qh, kh)
            scores = jnp.where(mask, scores, NEG_INF)
            w = jax.nn.softmax(scores, axis=-1)
            return jnp.einsum('bhst,bhtd->bhsd', w, vh)
        out_g = attend(q[:, :GLOBAL_HEADS], k[:, :GLOBAL_HEADS], v[:, :GLOBAL_HEADS], causal)
        out_l = attend(q[:, GLOBAL_HEADS:], k[:, GLOBAL_HEADS:], v[:, GLOBAL_HEADS:], local)
        attn = jnp.concatenate([out_g, out_l], axis=1)
        attn = attn.transpose(0, 2, 1, 3).reshape(B, S, E)
        return jnp.einsum('bse,fe->bsf', attn, Wo) + bo

    def _L1_ffn_ref(x, router_W, router_b, sW1, sb1, sW2, sb2, eW1, eb1, eW2, eb2):
        import jax, jax.numpy as jnp
        import numpy as np
        B, L, D = (2, 512, 256)
        E = 15
        H = D * 1
        K = 3
        T = 1.0
        b, l, d = x.shape
        n = b * l
        xt = x.reshape(n, d)
        shared = jax.nn.relu(xt @ sW1 + sb1) @ sW2 + sb2
        logits = xt @ router_W + router_b
        probs = jax.nn.softmax(logits / T, axis=-1)
        top_p, top_i = jax.lax.top_k(probs, K)
        cw = jnp.zeros((n, E), dtype=probs.dtype)
        cw = cw.at[jnp.arange(n)[:, None], top_i].set(top_p)
        h = jax.nn.relu(jnp.einsum('nd,edh->neh', xt, eW1) + eb1)
        ye = jnp.einsum('neh,ehd->ned', h, eW2) + eb2
        routed = jnp.einsum('ned,ne->nd', ye, cw)
        return (shared + routed).reshape(b, l, d)
    x = L0_attn_x
    x = _layernorm(x + _L0_attn_ref(x, L0_attn_W_in, L0_attn_conv_w, L0_attn_conv_b, L0_attn_W_x, L0_attn_W_dt, L0_attn_b_dt, L0_attn_A_log, L0_attn_W_out), axis=-1)
    x = _layernorm(x + _L0_ffn_ref(x, L0_ffn_w1, L0_ffn_b1, L0_ffn_w2, L0_ffn_b2), axis=-1)
    x = _layernorm(x + _L1_attn_ref(x, L1_attn_Wq, L1_attn_Wk, L1_attn_Wv, L1_attn_Wo, L1_attn_bo), axis=-1)
    x = _layernorm(x + _L1_ffn_ref(x, L1_ffn_router_W, L1_ffn_router_b, L1_ffn_sW1, L1_ffn_sb1, L1_ffn_sW2, L1_ffn_sb2, L1_ffn_eW1, L1_ffn_eb1, L1_ffn_eW2, L1_ffn_eb2), axis=-1)
    return x

_drawn_inputs = setup_inputs


def setup_inputs(seed=0):
    import zlib

    import numpy as np

    out = dict(_drawn_inputs(seed))
    spreads = {'L1_attn_bo': (0.0, 0.1),
     'L1_ffn_router_b': (0.0, 0.735),
     'L1_ffn_sb1': (0.0, 0.39),
     'L1_ffn_sb2': (0.0, 0.1),
     'L1_ffn_eb1': (0.0, 0.8),
     'L1_ffn_eb2': (0.0, 0.468)}
    factors = {'L0_attn_conv_b': 3.755,
     'L0_attn_b_dt': 8.0,
     'L0_ffn_b1': 8.0,
     'L1_ffn_router_W': 2.942,
     'L1_ffn_eW1': 5.378,
     'L1_ffn_eW2': 4.311}
    for name, (base, spread) in spreads.items():
        noise = np.random.default_rng([zlib.crc32(name.encode()), seed]).standard_normal(out[name].shape)
        drawn = base * np.exp(spread * noise) if base else spread * noise
        out[name] = jnp.asarray(drawn.astype(out[name].dtype))
    for name, factor in factors.items():
        out[name] = (out[name] * factor).astype(out[name].dtype)
    return out
```

```python
import numpy as np
import concourse.bass as bass
from concourse import mybir
from contextlib import ExitStack

FP32 = mybir.dt.float32
BF16 = mybir.dt.bfloat16
ALU = mybir.AluOpType
ACT = mybir.ActivationFunctionType
AX = mybir.AxisListType

NB = 4
SEQ = 1024
TOK = NB * SEQ
D = 256
CH = 512
NCH = TOK // CH
DT = 4
NS = 16
EPS = 1e-5


class LnTiles:

    def __init__(self, sb, p, res=None, nrm=None):
        self.res = sb(p + "_ln_res", [128, 4, D]) if res is None else res
        self.nrm = sb(p + "_ln_nrm", [128, 4, D]) if nrm is None else nrm
        self.stats = sb(p + "_ln_stats", [128, 4, 6])
        self.mean = sb(p + "_ln_mean", [128, 4])
        self.diff = sb(p + "_ln_diff", [128, 4])
        self.var = sb(p + "_ln_var", [128, 4])
        self.rstd = sb(p + "_ln_rstd", [128, 4])
        self.minus_half = sb(p + "_ln_minus_half", [128, 4])


class LnSems:

    def __init__(self, sem, p):
        self.steps = sem(p + "_ln_steps")
        self.rstd = sem(p + "_ln_rstd_ready")
        self.done = sem(p + "_ln_done")
        self.half = sem(p + "_ln_half_ready")
        self.turned = sem(p + "_ln_turned")
        self.stored = sem(p + "_ln_stored")


LN_STEPS = 11


def two_banks(P, at):
    return P[:, at:at + 2, :].rearrange("p b (t d) -> p (b t) d", d=D)


def over_tiles(row):
    return row[:, :].unsqueeze(1).to_broadcast([128, 4, D])


def ln_start(nc, ln, lns):
    nc.vector.memset(ln.minus_half[:, :], -0.5).then_inc(lns.half, 1)
    nc.vector.memset(ln.diff[:, :], 0.0).then_inc(lns.stored, 1)
    nc.vector.memset(ln.mean[:, :], 0.0).then_inc(lns.done, 4)


def ln_dve(nc, dve, ln, lns, c, stored=None, each=1):
    count = [c * LN_STEPS]

    def step(ins):
        ins.then_inc(lns.steps, 1)
        count[0] = count[0] + 1

    for t in range(4):
        step(nc.vector.bn_stats(ln.stats[:, t, :], ln.res[:, t, :]))
    dve.wait_ge(lns.steps, count[0])
    step(nc.vector.tensor_tensor(ln.mean[:, :], ln.stats[:, :, 1], ln.stats[:, :, 4], ALU.add))
    step(nc.vector.tensor_tensor(ln.diff[:, :], ln.stats[:, :, 1], ln.stats[:, :, 4], ALU.subtract))
    step(nc.vector.tensor_tensor(ln.var[:, :], ln.stats[:, :, 2], ln.stats[:, :, 5], ALU.add))
    dve.wait_ge(lns.steps, count[0])
    step(nc.vector.tensor_tensor(ln.diff[:, :], ln.diff[:, :], ln.diff[:, :], ALU.mult))
    step(nc.vector.tensor_scalar(ln.var[:, :], ln.var[:, :], 1.0 / D, EPS, ALU.mult, ALU.add))
    step(nc.vector.tensor_scalar(ln.mean[:, :], ln.mean[:, :], 0.5, None, ALU.mult))
    dve.wait_ge(lns.steps, count[0])
    step(nc.vector.scalar_tensor_tensor(ln.var[:, :], ln.diff[:, :], 0.25, ln.var[:, :], ALU.mult, ALU.add))
    dve.wait_ge(lns.rstd, c + 1)
    dve.wait_ge(lns.stored if stored is None else stored, (c + 1) * each)
    for t in range(4):
        nc.vector.tensor_scalar(ln.nrm[:, t, :], ln.res[:, t, :], ln.mean[:, t:t + 1],
                                ln.rstd[:, t:t + 1], ALU.subtract, ALU.mult).then_inc(lns.done, 1)


def ln_pool(nc, pool, ln, lns, c):
    pool.wait_ge(lns.steps, (c + 1) * LN_STEPS)
    nc.gpsimd.tensor_tensor(ln.rstd[:, :], ln.var[:, :], ln.minus_half[:, :], ALU.pow).then_inc(lns.rstd, 1)


def ln_pe(nc, pe, ln, lns, P, bank, ident, c):
    pe.wait_ge(lns.done, (c + 2) * 4)
    for k in range(2):
        for t in range(4):
            last = nc.tensor.transpose(P[:, bank + k, t * 128:(t + 1) * 128], ln.nrm[:, t, k * 128:(k + 1) * 128],
                                       ident[:, :])
    last.then_inc(lns.turned, 1)


def ln_act(nc, act, ln, lns, P, bank, XN, XT, c):
    act.wait_ge(lns.done, (c + 2) * 4)
    nc.scalar.copy(XN[:, bass.ds(c * 4, 4), :], ln.nrm[:, :, :])
    act.wait_ge(lns.turned, c + 1)
    nc.scalar.copy(XT[:, :, bass.ds(c * CH, CH)], P[:, bank:bank + 2, :]).then_inc(lns.stored, 1)
def mamba_phase(nc, XN, XT, P, ident, x_tok, x_feat, w_in, conv_w, conv_b, w_x, w_dt, b_dt, a_log, w_out, bc_scratch):
    ctx = ExitStack()
    with ctx:
        def sb(name, shape, dt=FP32):
            return ctx.enter_context(nc.sbuf_tensor(name, shape, dt))

        def sem(name):
            return ctx.enter_context(nc.semaphore(name))

        w_in_sb = sb("w_in_sb", [128, 2, 1024])
        w_x_sb = sb("w_x_sb", [128, DT, 96])
        w_dt_sb = sb("w_dt_sb", [64, 512])
        w_out_sb = sb("w_out_sb", [128, DT, 256])
        conv_w_sb = sb("conv_w_sb", [128, DT, 4])
        conv_b_sb = sb("conv_b_sb", [128, DT])
        b_dt_sb = sb("b_dt_sb", [128, DT])
        a_neg = sb("a_neg", [128, DT, NS])
        a_exp = sb("a_exp", [128, DT, NS])
        xT = sb("m_xT", [128, 2, CH])
        xres = sb("m_xres", [128, 4, 256])
        xs = sb("m_xs", [128, DT, CH + 3])
        conv = sb("m_conv", [128, DT, CH])
        gate = sb("m_gate", [128, DT, CH])
        u = sb("m_u", [128, DT, CH])
        z = sb("m_z", [128, DT, CH])
        delta = z
        du = conv
        low = sb("m_low", [64, CH])
        bc_own = sb("m_bc_own", [96, CH])
        bc = sb("m_bc", [128, 2 * NS, CH])
        dbu = sb("m_dbu", [128, 4, CH])
        sp = dbu
        h3 = sb("m_h3", [128, CH])
        g = u
        state = sb("m_state", [128, DT, NS])
        ln = LnTiles(sb, "m", g[:, 0:2, :].rearrange("p a (t d) -> p (a t) d", d=D),
                     g[:, 2:4, :].rearrange("p a (t d) -> p (a t) d", d=D))

        w_loaded = sem("m_w_loaded")
        xT_loaded = sem("m_xT_loaded")
        xres_loaded = sem("m_xres_loaded")
        scratch_written = sem("m_scratch_written")
        bc_loaded = [sem(f"m_bc_loaded{k}") for k in range(4)]
        a_ready = sem("m_a_ready")
        xr_ready = sem("m_xr_ready")
        xs_ready = sem("m_xs_ready")
        conv_step = sem("m_conv_step")
        xs_head = sem("m_xs_head")
        gate_ready = sem("m_gate_ready")
        u_ready = sem("m_u_ready")
        xdbl_ready = sem("m_xdbl_ready")
        low_ready = sem("m_low_ready")
        bc_own_ready = sem("m_bc_own_ready")
        dlow_ready = sem("m_dlow_ready")
        z_step = sem("m_z_step")
        delta_ready = sem("m_delta_ready")
        du_ready = sem("m_du_ready")
        dA_ready = sem("m_dA_ready")
        dbu_ready = sem("m_dbu_ready")
        h_ready = sem("m_h_ready")
        g_dve = sem("m_g_dve")
        g_pool = sem("m_g_pool")
        summed = sem("m_summed")
        state_pool = sem("m_state_pool")
        state_dve = sem("m_state_dve")
        gated = sem("m_gated")
        proj_ready = sem("m_proj_ready")
        res_added = sem("m_res_added")
        lns = LnSems(sem, "m")

        DA, H, Y = (0, 1), (2, 3, 4), (5, 6)
        block = ctx.enter_context(nc.Block())

        @block.sync
        def _(sync):
            for dst, src in ((w_in_sb, w_in), (w_x_sb, w_x), (w_out_sb, w_out), (conv_w_sb, conv_w)):
                sync.dma_start(dst[:, :, :], src).then_inc(w_loaded, 16)
            for dst, src in ((w_dt_sb, w_dt), (conv_b_sb, conv_b), (b_dt_sb, b_dt)):
                sync.dma_start(dst[:, :], src).then_inc(w_loaded, 16)
            sync.dma_start(a_exp[:, :, :], a_log).then_inc(w_loaded, 16)
            with nc.sync.Fori(0, NB) as b:
                for half in range(2):
                    c = b * 2 + half
                    first_token, first_tile = nc.sync.snap(c * CH), nc.sync.snap(c * 4)
                    sync.wait_ge(gate_ready, (c + 1) * DT)
                    sync.dma_start(xT[:, :, :], x_feat[:, :, bass.ds(first_token, CH)]).then_inc(xT_loaded, 16)
                    sync.wait_ge(lns.stored, c + 1)
                    sync.dma_start(xres[:, :, :], x_tok[:, bass.ds(first_tile, 4), :]).then_inc(xres_loaded, 16)
                    sync.wait_ge(bc_own_ready, c + 1)
                    sync.dma_start(bc_scratch, bc_own[64:96, :]).then_inc(scratch_written, 16)
                    sync.wait_ge(scratch_written, (c + 1) * 16)
                    for k in range(4):
                        for s in (0, NS):
                            rows = slice(s + 4 * k, s + 4 * k + 4)
                            sync.dma_start(bc[:, rows, :],
                                           bc_scratch[rows, :].partition_broadcast(128)).then_inc(bc_loaded[k], 16)

        @block.tensor
        def _(pe):
            pe.wait_ge(w_loaded, 16 * 8)
            with nc.tensor.Fori(0, NB) as b:
                for half in range(2):
                    c = b * 2 + half
                    pe.wait_ge(xT_loaded, (c + 1) * 16)
                    pe.wait_ge(lns.stored, c + 1)
                    for m in range(8):
                        for k in range(2):
                            last = nc.tensor.matmul(P[:, m, :], w_in_sb[:, k, m * 128:(m + 1) * 128], xT[:, k, :],
                                                    start=(k == 0), stop=(k == 1))
                        last.then_inc(xr_ready, 1)
                    pe.wait_ge(u_ready, (c + 1) * DT)
                    for k in range(DT):
                        last = nc.tensor.matmul(P[0:96, 0, :], w_x_sb[:, k, :], u[:, k, :],
                                                start=(k == 0), stop=(k == DT - 1))
                    last.then_inc(xdbl_ready, 1)
                    pe.wait_ge(low_ready, c + 1)
                    for m in range(DT):
                        nc.tensor.matmul(P[:, 1 + m, :], w_dt_sb[:, m * 128:(m + 1) * 128], low[:, :],
                                         start=True, stop=True).then_inc(dlow_ready, 1)
                    for dt in range(DT):
                        def units(q, first, last_q):
                            for r in range(4):
                                if r < 3:
                                    pe.wait_ge(g_dve, c * 48 + 12 * dt + q * 3 + r + 1)
                                else:
                                    pe.wait_ge(g_pool, c * 16 + 4 * dt + q + 1)
                                nc.tensor.matmul(P[:, Y[dt % 2], :], ident[:, :], g[:, r, :],
                                                 start=(first and r == 0),
                                                 stop=(last_q and r == 3)).then_inc(summed, 1)
                        if dt >= 2:
                            pe.wait_ge(gated, c * DT + dt - 1)
                        units(0, True, False)
                        with nc.tensor.Fori(1, 3) as q:
                            units(q, False, False)
                        units(3, False, True)
                    pe.wait_ge(gated, (c + 1) * DT)
                    for t in range(4):
                        for k in range(DT):
                            last = nc.tensor.matmul(P[:, t // 2, (t % 2) * 256:(t % 2) * 256 + 256],
                                                    gate[:, k, t * 128:(t + 1) * 128], w_out_sb[:, k, :],
                                                    start=(k == 0), stop=(k == DT - 1))
                    last.then_inc(proj_ready, 1)
                    ln_pe(nc, pe, ln, lns, P, 2, ident, c)

        @block.scalar
        def _(act):
            act.wait_ge(w_loaded, 16 * 8)
            nc.scalar.activation(a_exp[:, :, :], a_exp[:, :, :], ACT.Exp).then_inc(a_ready, 1)
            act.wait_ge(a_ready, 1)
            nc.scalar.mul(a_neg[:, :, :], a_exp[:, :, :], -1.0).then_inc(a_ready, 1)
            act.wait_ge(a_ready, 2)
            with nc.scalar.Fori(0, NB) as b:
                for half in range(2):
                    c = b * 2 + half
                    act.wait_ge(xs_head, c + 1)
                    for m in range(DT):
                        act.wait_ge(xr_ready, c * 8 + m + 1)
                        nc.scalar.copy(xs[:, m, 3:CH + 3], P[:, m, :]).then_inc(xs_ready, 1)
                    for m in range(DT):
                        act.wait_ge(xr_ready, c * 8 + 4 + m + 1)
                        nc.scalar.activation(gate[:, m, :], P[:, 4 + m, :], ACT.Silu).then_inc(gate_ready, 1)
                    for m in range(DT):
                        act.wait_ge(conv_step, c * 16 + 12 + m + 1)
                        nc.scalar.activation(u[:, m, :], conv[:, m, :], ACT.Silu,
                                             bias=conv_b_sb[:, m:m + 1]).then_inc(u_ready, 1)
                    act.wait_ge(xdbl_ready, c + 1)
                    nc.scalar.copy(low[:, :], P[0:64, 0, :]).then_inc(low_ready, 1)
                    nc.scalar.copy(bc_own[64:96, :], P[64:96, 0, :]).then_inc(bc_own_ready, 1)
                    for m in range(DT):
                        act.wait_ge(dlow_ready, c * DT + m + 1)
                        last = nc.scalar.activation(z[:, m, :], P[:, 1 + m, :], ACT.Identity,
                                                    bias=b_dt_sb[:, m:m + 1])
                    last.then_inc(z_step, 1)
                    act.wait_ge(z_step, c * 4 + 1)
                    nc.scalar.activation(sp[:, :, :], z[:, :, :], ACT.Abs).then_inc(z_step, 1)
                    act.wait_ge(z_step, c * 4 + 2)
                    nc.scalar.activation(sp[:, :, :], sp[:, :, :], ACT.Exp, scale=-1.0).then_inc(z_step, 1)
                    act.wait_ge(z_step, c * 4 + 3)
                    nc.scalar.activation(sp[:, :, :], sp[:, :, :], ACT.Ln, bias=1.0).then_inc(z_step, 1)
                    act.wait_ge(delta_ready, c + 1)
                    for dt in range(DT):
                        def decays(q, first):
                            for r in range(4):
                                unit = c * 64 + 16 * dt + q * 4 + r
                                if not (first and dt == 0 and r < 2):
                                    act.wait_ge(h_ready, unit - 1)
                                nc.scalar.activation(P[:, DA[r % 2], :], delta[:, dt, :], ACT.Exp,
                                                     scale=a_neg[:, dt, bass.ds(q * 4 + r, 1)]).then_inc(dA_ready, 1)
                        decays(0, True)
                        with nc.scalar.Fori(1, 4) as q:
                            decays(q, False)
                    ln_act(nc, act, ln, lns, P, 2, XN, XT, c)

        @block.gpsimd
        def _(pool):
            pool.wait_ge(lns.half, 1)
            with nc.gpsimd.Fori(0, NB) as b:
                for half in range(2):
                    c = b * 2 + half
                    pool.wait_ge(du_ready, c + 1)

                    def last_product(dt, q):
                        unit = c * 64 + 16 * dt + q * 4 + 3
                        pool.wait_ge(h_ready, unit + 1)
                        if not (dt == 0 and isinstance(q, int) and q == 0):
                            pool.wait_ge(summed, unit - 3)
                        nc.gpsimd.tensor_tensor(g[:, 3, :], h3[:, :], bc[:, NS + q * 4 + 3, :],
                                                ALU.mult).then_inc(g_pool, 1)
                        if half == 0:
                            nc.gpsimd.tensor_copy(state[:, dt, bass.ds(q * 4 + 3, 1)],
                                                  h3[:, CH - 1:CH]).then_inc(state_pool, 1)

                    for dt in range(DT):
                        def inputs(q, first):
                            for r in range(4):
                                unit = c * 64 + 16 * dt + q * 4 + r
                                if dt == 0 and r == 0:
                                    if first:
                                        pool.wait_ge(bc_loaded[0], (c + 1) * 32)
                                if not (first and dt == 0):
                                    pool.wait_ge(h_ready, unit - 3)
                                nc.gpsimd.tensor_tensor(dbu[:, r, :], du[:, dt, :], bc[:, q * 4 + r, :],
                                                        ALU.mult).then_inc(dbu_ready, 1)
                                if r == 1:
                                    if not first:
                                        last_product(dt, q - 1)
                                    elif dt:
                                        last_product(dt - 1, 3)
                        inputs(0, True)
                        if dt == 0:
                            for q in range(1, 4):
                                pool.wait_ge(bc_loaded[q], (c + 1) * 32)
                                inputs(q, False)
                        else:
                            with nc.gpsimd.Fori(1, 4) as q:
                                inputs(q, False)
                    last_product(DT - 1, 3)
                    ln_pool(nc, pool, ln, lns, c)

        @block.vector
        def _(dve):
            ln_start(nc, ln, lns)
            nc.vector.memset(xs[:, :, 0:3], 0.0).then_inc(xs_head, 1)
            nc.vector.memset(state[:, :, :], 0.0).then_inc(gate_ready, DT)
            dve.wait_ge(w_loaded, 16 * 8)
            with nc.vector.Fori(0, NB) as b:
                for half in range(2):
                    c = b * 2 + half
                    for tap in range(4):
                        for m in range(DT):
                            if tap == 0:
                                dve.wait_ge(xs_ready, c * DT + m + 1)
                                nc.vector.tensor_scalar(conv[:, m, :], xs[:, m, 0:CH], conv_w_sb[:, m, 0:1], None,
                                                        ALU.mult).then_inc(conv_step, 1)
                            else:
                                dve.wait_ge(conv_step, c * 16 + 4 * (tap - 1) + m + 1)
                                nc.vector.scalar_tensor_tensor(conv[:, m, :], xs[:, m, tap:CH + tap],
                                                               conv_w_sb[:, m, tap:tap + 1], conv[:, m, :],
                                                               ALU.mult, ALU.add).then_inc(conv_step, 1)
                    if half == 0:
                        nc.vector.tensor_copy(xs[:, :, 0:3], xs[:, :, CH:CH + 3]).then_inc(xs_head, 1)
                    else:
                        nc.vector.memset(xs[:, :, 0:3], 0.0).then_inc(xs_head, 1)
                    dve.wait_ge(z_step, (c + 1) * 4)
                    nc.vector.scalar_tensor_tensor(delta[:, :, :], z[:, :, :], 0.0, sp[:, :, :],
                                                   ALU.max, ALU.add).then_inc(delta_ready, 1)
                    dve.wait_ge(delta_ready, c + 1)
                    dve.wait_ge(u_ready, (c + 1) * DT)
                    nc.vector.tensor_tensor(du[:, :, :], delta[:, :, :], u[:, :, :], ALU.mult).then_inc(du_ready, 1)
                    if half == 1:
                        dve.wait_ge(state_pool, (b + 1) * 16)
                        dve.wait_ge(state_dve, (b + 1) * 16)
                    for dt in range(DT):
                        def scan(q, r, first):
                            unit = c * 64 + 16 * dt + q * 4 + r
                            dve.wait_ge(dA_ready, unit + 1)
                            dve.wait_ge(dbu_ready, unit + 1)
                            if half == 0 and r == 0 and not (first and dt == 0):
                                dve.wait_ge(state_dve, b * 16 + 4 * dt + q)
                            if half == 1 and r < 3 and not (first and dt == 0):
                                dve.wait_ge(g_dve, c * 48 + 12 * dt + q * 3 - 3 + r + 1)
                            if r == 3 and not (first and dt == 0):
                                dve.wait_ge(g_pool, c * 16 + 4 * dt + q)
                                if half == 0:
                                    dve.wait_ge(state_pool, b * 16 + 4 * dt + q)
                            out = P[:, H[r], :] if r < 3 else h3[:, :]
                            initial = state[:, dt, bass.ds(q * 4 + r, 1)] if half else 0.0
                            nc.vector.tensor_tensor_scan(out, P[:, DA[r % 2], :], dbu[:, r, :], initial,
                                                         ALU.mult, ALU.add).then_inc(h_ready, 1)

                        def product(q, r, first):
                            unit = c * 64 + 16 * dt + q * 4 + r
                            dve.wait_ge(h_ready, unit + 1)
                            if not (first and dt == 0):
                                dve.wait_ge(summed, unit - 3)
                            nc.vector.tensor_tensor(g[:, r, :], P[:, H[r], :], bc[:, NS + q * 4 + r, :],
                                                    ALU.mult).then_inc(g_dve, 1)

                        def units(q, first):
                            scan(q, 0, first)
                            scan(q, 1, first)
                            product(q, 0, first)
                            scan(q, 2, first)
                            product(q, 1, first)
                            scan(q, 3, first)
                            product(q, 2, first)
                            if half == 0:
                                nc.vector.tensor_copy(state[:, dt, bass.ds(q * 4, 3)],
                                                      P[:, H[0]:H[2] + 1, CH - 1]).then_inc(state_dve, 1)

                        def gate_tile(d):
                            dve.wait_ge(summed, c * 64 + 16 * (d + 1))
                            nc.vector.tensor_tensor(gate[:, d, :], P[:, Y[d % 2], :], gate[:, d, :],
                                                    ALU.mult).then_inc(gated, 1)

                        if dt == 0:
                            dve.wait_ge(bc_loaded[0], (c + 1) * 32)
                        units(0, True)
                        if dt:
                            gate_tile(dt - 1)
                        if dt == 0:
                            dve.wait_ge(gate_ready, (c + 2) * DT)
                            for q in range(1, 4):
                                dve.wait_ge(bc_loaded[q], (c + 1) * 32)
                                units(q, False)
                        else:
                            with nc.vector.Fori(1, 4) as q:
                                units(q, False)
                    gate_tile(DT - 1)
                    dve.wait_ge(proj_ready, c + 1)
                    dve.wait_ge(xres_loaded, (c + 1) * 16)
                    nc.vector.tensor_tensor(ln.res[:, :, :], two_banks(P, 0), xres[:, :, :],
                                            ALU.add).then_inc(res_added, 1)
                    dve.wait_ge(res_added, c + 1)
                    ln_dve(nc, dve, ln, lns, c)


def ffn_phase(nc, XN, XT, P, ident, w1, w1_rows, b1, w2, b2_all):
    MT = 8
    ctx = ExitStack()
    with ctx:
        def sb(name, shape, dt=FP32):
            return ctx.enter_context(nc.sbuf_tensor(name, shape, dt))

        def sem(name):
            return ctx.enter_context(nc.semaphore(name))

        w1_sb = sb("f_w1_sb", [128, 2, 1024])
        w1r_sb = sb("f_w1_rows", [128, MT, D])
        w2_sb = sb("f_w2", [128, MT, D])
        w2_abs = sb("f_w2_abs", [128, MT, D])
        b1_sb = sb("f_b1", [128, MT])
        b2_sb = sb("f_b2", [128, D])
        ones = sb("f_ones", [128, 128])
        alpha1 = sb("f_alpha1", [128, MT])
        alpha2 = sb("f_alpha2", [128, D])
        hT = sb("f_hT", [128, MT, CH])
        ln = LnTiles(sb, "f")
        loaded = sem("f_loaded")
        w1_sign = sem("f_w1_sign")
        w2_sign = sem("f_w2_sign")
        w2_abs_ready = sem("f_w2_abs_ready")
        alpha1_ready = sem("f_alpha1_ready")
        alpha2_sum = sem("f_alpha2_sum")
        alpha2_ready = sem("f_alpha2_ready")
        ones_ready = sem("f_ones_ready")
        up_ready = sem("f_up_ready")
        h_ready = sem("f_h_ready")
        down_ready = sem("f_down_ready")
        res_step = sem("f_res_step")
        lns = LnSems(sem, "f")
        UP, DOWN, TURN = 0, 4, 6
        block = ctx.enter_context(nc.Block())

        @block.sync
        def _(sync):
            for dst, src in ((w1_sb, w1), (w1r_sb, w1_rows), (w2_sb, w2)):
                sync.dma_start(dst[:, :, :], src).then_inc(loaded, 16)
            for dst, src in ((b1_sb, b1), (b2_sb, b2_all.partition_broadcast(128))):
                sync.dma_start(dst[:, :], src).then_inc(loaded, 16)

        @block.tensor
        def _(pe):
            pe.wait_ge(ones_ready, 1)
            pe.wait_ge(w2_abs_ready, 1)
            for k in range(MT):
                last = nc.tensor.matmul(P[:, DOWN, 0:D], ones[:, :], w2_abs[:, k, :], start=(k == 0), stop=(k == MT - 1))
            last.then_inc(alpha2_sum, 1)
            pe.wait_ge(w1_sign, 1)
            pe.wait_ge(w2_sign, 1)
            pe.wait_ge(alpha2_ready, 1)

            def up(c, first):
                for m in range(MT):
                    if not (first and m < 4):
                        pe.wait_ge(h_ready, c * MT + m - 3)
                    for k in range(2):
                        last = nc.tensor.matmul(P[:, UP + m % 4, :], w1_sb[:, k, m * 128:(m + 1) * 128],
                                                XT[:, k, bass.ds(c * CH, CH)], start=(k == 0), stop=(k == 1))
                    last.then_inc(up_ready, 1)

            def down(c, first):
                if not first:
                    pe.wait_ge(res_step, c * 3 - 2)
                for t in range(4):
                    for k in range(MT):
                        if t == 0:
                            pe.wait_ge(h_ready, c * MT + k + 1)
                        last = nc.tensor.matmul(P[:, DOWN + t // 2, (t % 2) * D:(t % 2) * D + D],
                                                hT[:, k, t * 128:(t + 1) * 128], w2_sb[:, k, :],
                                                start=(k == 0), stop=(k == MT - 1))
                last.then_inc(down_ready, 1)

            up(0, True)
            down(0, True)
            with nc.tensor.Fori(1, NCH) as c:
                up(c, False)
                ln_pe(nc, pe, ln, lns, P, TURN, ident, c - 1)
                down(c, False)
            ln_pe(nc, pe, ln, lns, P, TURN, ident, NCH - 1)

        @block.scalar
        def _(act):
            act.wait_ge(loaded, 16 * 5)
            nc.scalar.activation(w2_abs[:, :, :], w2_sb[:, :, :], ACT.Abs).then_inc(w2_abs_ready, 1)
            act.wait_ge(w2_abs_ready, 1)
            nc.scalar.sign(w2_sb[:, :, :], w2_sb[:, :, :]).then_inc(w2_sign, 1)
            nc.scalar.sign(w1_sb[:, :, :], w1_sb[:, :, :]).then_inc(w1_sign, 1)
            act.wait_ge(alpha2_sum, 1)
            nc.scalar.mul(alpha2[:, :], P[:, DOWN, 0:D], 1.0 / 1024).then_inc(alpha2_ready, 1)
            act.wait_ge(alpha1_ready, 2)

            def gelus(c, first):
                for m in range(MT):
                    act.wait_ge(up_ready, c * MT + m + 1)
                    if m == 0 and not first:
                        act.wait_ge(down_ready, c)
                    nc.scalar.activation(hT[:, m, :], P[:, UP + m % 4, :], ACT.Gelu, bias=b1_sb[:, m:m + 1],
                                         scale=alpha1[:, m:m + 1]).then_inc(h_ready, 1)

            gelus(0, True)
            with nc.scalar.Fori(1, NCH) as c:
                gelus(c, False)
                ln_act(nc, act, ln, lns, P, TURN, XN, XT, c - 1)
            ln_act(nc, act, ln, lns, P, TURN, XN, XT, NCH - 1)

        @block.gpsimd
        def _(pool):
            pool.wait_ge(lns.half, 1)
            with nc.gpsimd.Fori(0, NCH) as c:
                ln_pool(nc, pool, ln, lns, c)

        @block.vector
        def _(dve):
            ln_start(nc, ln, lns)
            nc.vector.memset(ones[:, :], 1.0).then_inc(ones_ready, 1)
            dve.wait_ge(loaded, 16 * 5)
            nc.vector.tensor_reduce(alpha1[:, :], w1r_sb[:, :, :], axis=AX.X, op=ALU.add,
                                    apply_absolute_value=True).then_inc(alpha1_ready, 1)
            dve.wait_ge(alpha1_ready, 1)
            nc.vector.tensor_scalar(alpha1[:, :], alpha1[:, :], 1.0 / D, None, ALU.mult).then_inc(alpha1_ready, 1)
            dve.wait_ge(alpha2_ready, 1)
            with nc.vector.Fori(0, NCH) as c:
                dve.wait_ge(down_ready, c + 1)
                nc.vector.tensor_tensor(ln.res[:, :, :], two_banks(P, DOWN), over_tiles(alpha2),
                                        ALU.mult).then_inc(res_step, 1)
                dve.wait_ge(res_step, c * 3 + 1)
                nc.vector.tensor_tensor(ln.res[:, :, :], ln.res[:, :, :], over_tiles(b2_sb), ALU.add).then_inc(res_step, 1)
                dve.wait_ge(res_step, c * 3 + 2)
                nc.vector.tensor_tensor(ln.res[:, :, :], ln.res[:, :, :], XN[:, bass.ds(c * 4, 4), :],
                                        ALU.add).then_inc(res_step, 1)
                dve.wait_ge(res_step, c * 3 + 3)
                ln_dve(nc, dve, ln, lns, c)


def attn_phase(nc, XN, XT, P, ident, wq, wk, wv, wo, bo, masks):
    HG = 8
    HD = 16
    QT = SEQ // 128
    SLOTS_Q = (0, 0, 1, 1, 0, 2)
    SLOTS_K = (0, 1, 0, 1, 2, 0)
    ROWS = 6 * HD
    WIN = 64

    MAX_GLOBAL = [(i, 0, min((i + 1) * 128, CH)) for i in range(4)]
    for i in range(4, QT):
        MAX_GLOBAL += [(i, 0, CH), (i, CH, (i + 1) * 128 - CH)]
    MAX_LOCAL = QT // 2
    MAX_ITEMS = HG * (len(MAX_GLOBAL) + MAX_LOCAL)
    EXP_GLOBAL = [[(0, 0, 0), (1, 0, CH)], [(2, 0, 0), (3, 0, 256)],
                  [(0, 1, 0), (1, 1, CH)], [(2, 1, 0), (3, 1, CH)],
                  [(4, 1, 0), (5, 1, CH)], [(6, 1, 0), (7, 1, 256)]]
    EXP_LOCAL = 2
    GROUPS = HG * (len(EXP_GLOBAL) + EXP_LOCAL)

    def queries(j, chunk):
        first = max(j * 128, chunk * CH)
        return first, (chunk + 1) * CH - first

    ctx = ExitStack()
    with ctx:
        def sb(name, shape, dt=FP32):
            return ctx.enter_context(nc.sbuf_tensor(name, shape, dt))

        def sem(name):
            return ctx.enter_context(nc.semaphore(name))

        wq_sb = sb("a_wq_sb", [128, 2, D])
        wk_sb = sb("a_wk_sb", [128, 2, D])
        wv_sb = sb("a_wv_sb", [128, 2, D])
        wo_sb = sb("a_wo_sb", [128, 4, D])
        bo_sb = sb("a_bo_sb", [128, D])
        mask_in = sb("a_mask_in", [128, 5, 192])
        mask = sb("a_mask", [128, 5, 192], BF16)
        eye = sb("a_eye", [128, 128], BF16)
        zeros = sb("a_zeros", [128, CH], BF16)
        xTb = sb("a_xTb", [128, 2, SEQ])
        rest = [sb(f"a_rest{i}", [128, CH]) for i in range(2)]
        parts = [sb(f"a_parts{i}", [128, 3, SEQ], BF16) for i in range(2)]
        qs = sb("a_qs", [128, HG, SEQ], BF16)
        ks = sb("a_ks", [128, HG, SEQ], BF16)
        v_sb = sb("a_v_sb", [128, QT, D])
        vpad = [sb(f"a_vpad{i}", [128, QT, 4, 128]) for i in range(2)]
        pT = [sb(f"a_pT{i}", [128, 2 * CH]) for i in range(2)]
        mx = sb("a_mx", [128, 2 * HG, QT])
        ones = sb("a_ones", [128, QT, HD])
        spare = sb("a_spare", [128, 2])
        mx2 = sb("a_mx2", [128, HG, 4, 2])
        mrest = sb("a_mrest", [64, 128])
        mparts = sb("a_mparts", [64, 3, 128], BF16)
        oT = sb("a_oT", [128, 4, SEQ])
        den = sb("a_den", [128, CH])
        ln = LnTiles(sb, "a", pT[0][:, :].rearrange("p (t d) -> p t d", d=D),
                     pT[1][:, :].rearrange("p (t d) -> p t d", d=D))
        scratch = nc.dram_tensor("a_scratch", [2, 128, 3, SEQ], BF16, kind="Internal").ap()

        loaded = sem("a_loaded")
        const_dve = sem("a_const_dve")
        const_pool = sem("a_const_pool")
        mask_ready = sem("a_mask_ready")
        x_loaded = sem("a_x_loaded")
        v_ready = sem("a_v_ready")
        v_kept = sem("a_v_kept")
        qk_ready = sem("a_qk_ready")
        hi_ready = sem("a_hi_ready")
        rest_ready = sem("a_rest_ready")
        mid_ready = sem("a_mid_ready")
        lo_ready = sem("a_lo_ready")
        parts_out = sem("a_parts_out")
        stacked = sem("a_stacked")
        s1_ready = sem("a_s1_ready")
        max_done = sem("a_max_done")
        mx_ready = sem("a_mx_ready")
        mx_turned = sem("a_mx_turned")
        mhi_ready = sem("a_mhi_ready")
        mrest_ready = sem("a_mrest_ready")
        mmid_ready = sem("a_mmid_ready")
        mlo_ready = sem("a_mlo_ready")
        m_stacked = sem("a_m_stacked")
        vpad_ready = sem("a_vpad_ready")
        s2_ready = sem("a_s2_ready")
        p_ready = sem("a_p_ready")
        pv_done = sem("a_pv_done")
        sum_ready = sem("a_sum_ready")
        den_step = sem("a_den_step")
        o_ready = sem("a_o_ready")
        out_ready = sem("a_out_ready")
        res_step = sem("a_res_step")
        lns = LnSems(sem, "a")
        block = ctx.enter_context(nc.Block())

        def max_base(b, hg):
            return b * MAX_ITEMS + hg * HG * len(MAX_GLOBAL)

        def group_base(b, hg):
            return b * GROUPS + hg * HG * len(EXP_GLOBAL)

        @block.sync
        def _(sync):
            for dst, src in ((wq_sb, wq), (wk_sb, wk), (wv_sb, wv), (wo_sb, wo), (mask_in, masks)):
                sync.dma_start(dst[:, :, :], src).then_inc(loaded, 16)
            sync.dma_start(bo_sb[:, :], bo.partition_broadcast(128)).then_inc(loaded, 16)
            with nc.sync.Fori(0, NB) as b:
                first_token = nc.sync.snap(b * SEQ)
                sync.wait_ge(lns.stored, b * 2 + 1)
                sync.dma_start(xTb[:, :, :], XT[:, :, bass.ds(first_token, SEQ)]).then_inc(x_loaded, 16)
                for hg in range(2):
                    if hg:
                        sync.wait_ge(pv_done, group_base(b, 1))
                    sync.wait_ge(lo_ready, (b * 2 + hg) * 4 + 4)
                    for i in range(2):
                        sync.dma_start(scratch[i], parts[i][:, :, :]).then_inc(parts_out, 16)
                    sync.wait_ge(parts_out, (b * 2 + hg + 1) * 32)
                    for i, (stack, slots) in enumerate(((qs, SLOTS_Q), (ks, SLOTS_K))):
                        for s in range(6):
                            src = scratch[i].rearrange("(h d) p t -> d p h t", d=HD)[:, slots[s]]
                            sync.dma_start(stack[s * HD:(s + 1) * HD, :, :], src).then_inc(stacked, 16)
                    sync.wait_ge(mlo_ready, b * 2 + hg + 1)
                    for p in range(3):
                        sync.dma_start(qs[ROWS + p:ROWS + p + 1, :, :], mparts[:, p, :]).then_inc(m_stacked, 16)

        @block.tensor
        def _(pe):
            pe.wait_ge(loaded, 16 * 6)
            pe.wait_ge(const_dve, 2)
            pe.wait_ge(const_pool, 3)
            pe.wait_ge(mask_ready, 2)
            with nc.tensor.Fori(0, NB) as b:
                pe.wait_ge(x_loaded, (b + 1) * 16)
                pe.wait_ge(lns.stored, b * 2 + 1)
                for t in range(QT):
                    for k in range(2):
                        last = nc.tensor.matmul(P[:, t // 2, (t % 2) * D:(t % 2) * D + D],
                                                xTb[:, k, t * 128:(t + 1) * 128], wv_sb[:, k, :],
                                                start=(k == 0), stop=(k == 1))
                    if t % 2:
                        last.then_inc(v_ready, 1)
                for hg in range(2):
                    if hg:
                        pe.wait_ge(o_ready, b * 8 + 4)
                    for s in range(4):
                        w, half = (wq_sb, wk_sb)[s // 2], s % 2
                        for k in range(2):
                            last = nc.tensor.matmul(P[:, 4 + s, :], w[:, k, hg * 128:(hg + 1) * 128],
                                                    xTb[:, k, half * CH:(half + 1) * CH], start=(k == 0), stop=(k == 1))
                        last.then_inc(qk_ready, 1)

                    pe.wait_ge(stacked, (b * 2 + hg + 1) * 16 * 12)
                    if hg == 0:
                        pe.wait_ge(v_kept, b * 4 + 4)
                    else:
                        pe.wait_ge(p_ready, group_base(b, 1))
                    nc.tensor.matmul(P[:, 0, 0:128], zeros[:, 0:128], zeros[:, 0:128], start=True, stop=True)
                    with nc.tensor.Fori(0, HG) as h:
                        if hg == 0:
                            for n, (i, first, keys) in enumerate(MAX_GLOBAL):
                                at = max_base(b, 0) + h * len(MAX_GLOBAL) + n
                                pe.wait_ge(max_done, at + 1)
                                diagonal = first + keys == (i + 1) * 128
                                last = nc.tensor.matmul(P[:, n % 4, 0:keys], qs[0:ROWS, h, i * 128:(i + 1) * 128],
                                                        ks[0:ROWS, h, first:first + keys], start=True, stop=not diagonal)
                                if diagonal:
                                    last = nc.tensor.matmul(P[:, n % 4, keys - 128:keys], eye[:, :], mask[:, 0, 0:128],
                                                            start=False, stop=True)
                                last.then_inc(s1_ready, 1)
                        else:
                            for n in range(MAX_LOCAL):
                                at = max_base(b, 1) + h * MAX_LOCAL + n
                                pe.wait_ge(max_done, at + 1)
                                for i in (2 * n, 2 * n + 1):
                                    col = (i % 2) * 192
                                    cut = WIN if i == 0 else 0
                                    nc.tensor.matmul(P[:, n % 4, col:col + 192], eye[:, :], mask[:, 2 if i == 0 else 1, :],
                                                     start=True, stop=False)
                                    last = nc.tensor.matmul(P[:, n % 4, col + cut:col + 192],
                                                            qs[0:ROWS, h, i * 128:(i + 1) * 128],
                                                            ks[0:ROWS, h, i * 128 - WIN + cut:(i + 1) * 128],
                                                            start=False, stop=True)
                                last.then_inc(s1_ready, 1)

                    pe.wait_ge(mx_ready, (b * 2 + hg + 1) * 1)
                    nc.tensor.transpose(P[:, 4, 0:128], mx[:, :, :].rearrange("p h i -> p (h i)"),
                                        ident[:, :]).then_inc(mx_turned, 1)

                    pe.wait_ge(m_stacked, (b * 2 + hg + 1) * 48)
                    for quad in range(2):
                        acc = 4 + 2 * quad
                        pe.wait_ge(vpad_ready, (b * 2 + hg) * 2 + quad + 1)
                        for chunk in range(2):
                            nc.tensor.matmul(P[:, acc + chunk, :], zeros[:, 0:128], zeros[:, :], start=True, stop=False)
                        n_groups = len(EXP_GLOBAL) if hg == 0 else EXP_LOCAL
                        base = group_base(b, hg) + quad * 4 * n_groups

                        def scores2(n):
                            hh, g = divmod(n, n_groups)
                            h, slot = quad * 4 + hh, 2 * (n % 2)
                            if not (quad == 0 and n < 2):
                                pe.wait_ge(p_ready, base + n - 1)
                            if hg == 0:
                                for j, chunk, col in EXP_GLOBAL[g]:
                                    first, count = queries(j, chunk)
                                    diagonal = first == j * 128
                                    out = P[:, slot + col // CH, col % CH:col % CH + count]
                                    last = nc.tensor.matmul(out, ks[0:ROWS + 3, h, j * 128:(j + 1) * 128],
                                                            qs[0:ROWS + 3, h, first:first + count],
                                                            start=True, stop=not diagonal)
                                    if diagonal:
                                        last = nc.tensor.matmul(out[:, 0:128], eye[:, :], mask[:, 3, 0:128],
                                                                start=False, stop=True)
                            else:
                                for j in range(4 * g, 4 * g + 4):
                                    count = min(192, SEQ - j * 128)
                                    at = (j % 2) * 192
                                    bank = slot + (j % 4) // 2
                                    nc.tensor.matmul(P[:, bank, at:at + 192], eye[:, :], mask[:, 4, :],
                                                     start=True, stop=False)
                                    last = nc.tensor.matmul(P[:, bank, at:at + count],
                                                            ks[0:ROWS + 3, h, j * 128:(j + 1) * 128],
                                                            qs[0:ROWS + 3, h, j * 128:j * 128 + count],
                                                            start=False, stop=True)
                            last.then_inc(s2_ready, 1)

                        def values(n):
                            hh, g = divmod(n, n_groups)
                            p = pT[n % 2]
                            pe.wait_ge(p_ready, base + n + 1)
                            final = n == 4 * n_groups - 1
                            if hg == 0:
                                items = [(j, chunk, queries(j, chunk)[0] - chunk * CH, col, queries(j, chunk)[1])
                                         for j, chunk, col in EXP_GLOBAL[g]]
                            else:
                                items = []
                                for j in range(4 * g, 4 * g + 4):
                                    at = ((j % 4) // 2) * CH + (j % 2) * 192
                                    for chunk in range(2):
                                        lo = max(j * 128, chunk * CH)
                                        hi = min(j * 128 + 192, (chunk + 1) * CH)
                                        if lo < hi:
                                            items.append((j, chunk, lo - chunk * CH, at + lo - j * 128, hi - lo))
                            for n_item, (j, chunk, dst, col, count) in enumerate(items):
                                last = nc.tensor.matmul(P[:, acc + chunk, dst:dst + count],
                                                        vpad[quad][:, j, hh, :], p[:, col:col + count], start=False,
                                                        stop=False)
                            last.then_inc(pv_done, 1)

                        scores2(0)
                        for n in range(4 * n_groups):
                            if n + 1 < 4 * n_groups:
                                scores2(n + 1)
                            values(n)
                        for chunk in range(2):
                            nc.tensor.matmul(P[:, acc + chunk, :], zeros[:, 0:128], zeros[:, :], start=False,
                                             stop=True).then_inc(sum_ready, 1)
                for half in range(2):
                    pe.wait_ge(o_ready, (b + 1) * 8)
                    for t in range(4):
                        for quad in range(4):
                            last = nc.tensor.matmul(P[:, 4 + 2 * half + t // 2, (t % 2) * D:(t % 2) * D + D],
                                                    oT[:, quad, half * CH + t * 128:half * CH + (t + 1) * 128],
                                                    wo_sb[:, quad, :], start=(quad == 0), stop=(quad == 3))
                    last.then_inc(out_ready, 1)
                for half in range(2):
                    ln_pe(nc, pe, ln, lns, P, 2 * half, ident, b * 2 + half)

        @block.scalar
        def _(act):
            act.wait_ge(loaded, 16 * 6)
            nc.scalar.copy(mask[:, :, :], mask_in[:, :, :]).then_inc(mask_ready, 1)
            nc.scalar.copy(eye[:, :], ident[:, :]).then_inc(mask_ready, 1)
            with nc.scalar.Fori(0, NB) as b:
                for t in range(4):
                    act.wait_ge(v_ready, b * 4 + t + 1)
                    nc.scalar.copy(v_sb[:, 2 * t:2 * t + 2, :],
                                   P[:, t, :].rearrange("p (t d) -> p t d", d=D)).then_inc(v_kept, 1)
                for hg in range(2):
                    for s in range(4):
                        act.wait_ge(qk_ready, (b * 2 + hg) * 4 + s + 1)
                        if hg and s == 0:
                            act.wait_ge(parts_out, (b * 2 + hg) * 32)
                        nc.scalar.activation(parts[s // 2][:, 0, (s % 2) * CH:(s % 2 + 1) * CH], P[:, 4 + s, :],
                                             ACT.Copy, scale=0.25 if s < 2 else 1.0).then_inc(hi_ready, 1)
                    for s in range(4):
                        act.wait_ge(rest_ready, (b * 2 + hg) * 4 + s + 1)
                        nc.scalar.copy(parts[s // 2][:, 1, (s % 2) * CH:(s % 2 + 1) * CH],
                                       rest[s % 2][:, :]).then_inc(mid_ready, 1)
                    act.wait_ge(mx_turned, b * 2 + hg + 1)
                    nc.scalar.activation(mparts[:, 0, :], P[0:HG * QT, 4, 0:128], ACT.Copy,
                                         scale=-1.0).then_inc(mhi_ready, 1)
                    act.wait_ge(mrest_ready, b * 2 + hg + 1)
                    nc.scalar.copy(mparts[:, 1, :], mrest[:, :]).then_inc(mmid_ready, 1)
                    for quad in range(2):
                        n_groups = len(EXP_GLOBAL) if hg == 0 else EXP_LOCAL
                        base = group_base(b, hg) + quad * 4 * n_groups
                        for n in range(4 * n_groups):
                            g, slot, p = n % n_groups, 2 * (n % 2), pT[n % 2]
                            act.wait_ge(s2_ready, base + n + 1)
                            if not (quad == 0 and n < 2):
                                act.wait_ge(pv_done, base + n - 1)
                            if hg == 0:
                                count = sum(queries(j, chunk)[1] for j, chunk, _ in EXP_GLOBAL[g])
                                src, dst = P[:, slot:slot + 2, :].rearrange("p a n -> p (a n)")[:, 0:count], p[:, 0:count]
                            else:
                                src = P[:, slot:slot + 2, 0:384]
                                dst = p[:, :].rearrange("p (a n) -> p a n", n=CH)[:, :, 0:384]
                            nc.scalar.activation(dst, src, ACT.Exp).then_inc(p_ready, 1)
                for half in range(2):
                    ln_act(nc, act, ln, lns, P, 2 * half, XN, XT, b * 2 + half)

        @block.gpsimd
        def _(pool):
            nc.gpsimd.memset(ones[:, :, :], 1.0)
            nc.gpsimd.memset(vpad[0][:, :, :, :], 0.0).then_inc(const_pool, 1)
            nc.gpsimd.memset(vpad[1][:, :, :, :], 0.0).then_inc(const_pool, 1)
            pool.wait_ge(const_pool, 2)
            for i in range(2):
                for hh in range(4):
                    last = nc.gpsimd.memset(vpad[i][:, :, hh, hh * 32 + HD:hh * 32 + 32], 1.0)
            last.then_inc(const_pool, 1)
            pool.wait_ge(const_pool, 3)
            pool.wait_ge(lns.half, 1)
            with nc.gpsimd.Fori(0, NB) as b:
                for hg in range(2):
                    for s in range(4):
                        cols = slice((s % 2) * CH, (s % 2 + 1) * CH)
                        pool.wait_ge(mid_ready, (b * 2 + hg) * 4 + s + 1)
                        nc.gpsimd.tensor_tensor(parts[s // 2][:, 2, cols], rest[s % 2][:, :], parts[s // 2][:, 1, cols],
                                                ALU.subtract).then_inc(lo_ready, 1)
                    pool.wait_ge(v_kept, b * 4 + 4)
                    if hg:
                        pool.wait_ge(pv_done, group_base(b, 1))
                    for quad in range(2):
                        for hh in range(4):
                            f = (hg * 2 + quad) * 64 + hh * HD
                            last = nc.gpsimd.tensor_tensor(vpad[quad][:, :, hh, hh * 32:hh * 32 + HD],
                                                           v_sb[:, :, f:f + HD], ones[:, :, :], ALU.mult)
                        last.then_inc(vpad_ready, 1)
                    pool.wait_ge(mmid_ready, b * 2 + hg + 1)
                    nc.gpsimd.tensor_tensor(mparts[:, 2, :], mrest[:, :], mparts[:, 1, :],
                                            ALU.subtract).then_inc(mlo_ready, 1)
                for half in range(2):
                    ln_pool(nc, pool, ln, lns, b * 2 + half)

        @block.vector
        def _(dve):
            ln_start(nc, ln, lns)
            nc.vector.memset(mrest[:, :], 0.0).then_inc(max_done, 4)
            nc.vector.memset(mx[:, :, :], 0.0)
            nc.vector.memset(ks[ROWS:ROWS + 3, :, :], 1.0).then_inc(const_dve, 1)
            nc.vector.memset(zeros[:, :], 0.0).then_inc(const_dve, 1)
            dve.wait_ge(const_dve, 2)
            with nc.vector.Fori(0, NB) as b:
                for hg in range(2):
                    for s in range(4):
                        cols = slice((s % 2) * CH, (s % 2 + 1) * CH)
                        dve.wait_ge(hi_ready, (b * 2 + hg) * 4 + s + 1)
                        if s >= 2:
                            dve.wait_ge(lo_ready, (b * 2 + hg) * 4 + s - 1)
                        nc.vector.scalar_tensor_tensor(rest[s % 2][:, :], P[:, 4 + s, :], 0.25 if s < 2 else 1.0,
                                                       parts[s // 2][:, 0, cols], ALU.mult,
                                                       ALU.subtract).then_inc(rest_ready, 1)
                    with nc.vector.Fori(0, HG) as h:
                        if hg == 0:
                            for n, (i, first, keys) in enumerate(MAX_GLOBAL):
                                at = max_base(b, 0) + h * len(MAX_GLOBAL) + n
                                dve.wait_ge(s1_ready, at + 1)
                                dst = mx[:, h, i:i + 1] if i < 4 else mx2[:, h, i - 4, first // CH:first // CH + 1]
                                nc.vector.tensor_reduce(dst, P[:, n % 4, 0:keys], axis=AX.X,
                                                        op=ALU.max).then_inc(max_done, 1)
                        else:
                            for n in range(MAX_LOCAL):
                                at = max_base(b, 1) + h * MAX_LOCAL + n
                                dve.wait_ge(s1_ready, at + 1)
                                nc.vector.tensor_reduce(mx[:, h, 2 * n:2 * n + 2],
                                                        P[:, n % 4, 0:384].rearrange("p (a k) -> p a k", a=2),
                                                        axis=AX.X, op=ALU.max).then_inc(max_done, 1)
                    dve.wait_ge(max_done, max_base(b, hg + 1) + 4 if hg == 0 else (b + 1) * MAX_ITEMS + 4)
                    if hg == 0:
                        nc.vector.tensor_reduce(mx[:, 0:HG, 4:8], mx2[:, :, :, :], axis=AX.X, op=ALU.max).then_inc(mx_ready, 1)
                    else:
                        nc.vector.memset(den[:, 0:1], 0.0).then_inc(mx_ready, 1)
                    dve.wait_ge(mhi_ready, b * 2 + hg + 1)
                    nc.vector.scalar_tensor_tensor(mrest[:, :], P[0:HG * QT, 4, 0:128], -1.0, mparts[:, 0, :],
                                                   ALU.mult, ALU.subtract).then_inc(mrest_ready, 1)
                    for quad in range(2):
                        for chunk in range(2):
                            n = ((b * 2 + hg) * 2 + quad) * 2 + chunk
                            acc = P[:, 4 + 2 * quad + chunk, :]
                            dve.wait_ge(sum_ready, n + 1)
                            nc.vector.memset(spare[:, chunk:chunk + 1], 0.0)
                            nc.vector.stream_shuffle(den[:, :], acc, [16 + r % 16 for r in range(32)]).then_inc(den_step, 1)
                            dve.wait_ge(den_step, n * 2 + 1)
                            nc.vector.reciprocal(den[:, :], den[:, :]).then_inc(den_step, 1)
                            dve.wait_ge(den_step, n * 2 + 2)
                            nc.vector.tensor_tensor(oT[:, hg * 2 + quad, chunk * CH:(chunk + 1) * CH], acc, den[:, :],
                                                    ALU.mult).then_inc(o_ready, 1)
                            dve.wait_ge(o_ready, n + 1)
                for half in range(2):
                    c = b * 2 + half
                    dve.wait_ge(out_ready, c + 1)
                    dve.wait_ge(lns.done, (c + 1) * 4)
                    nc.vector.tensor_tensor(ln.res[:, :, :], two_banks(P, 4 + 2 * half), over_tiles(bo_sb),
                                            ALU.add).then_inc(res_step, 1)
                    dve.wait_ge(res_step, c * 2 + 1)
                    nc.vector.tensor_tensor(ln.res[:, :, :], ln.res[:, :, :], XN[:, bass.ds(c * 4, 4), :],
                                            ALU.add).then_inc(res_step, 1)
                    dve.wait_ge(res_step, c * 2 + 2)
                    ln_dve(nc, dve, ln, lns, c)



def moe_phase(nc, XN, XT, P, ident, router_w, router_b, w1, b1, w2, b2, pads, out):
    NE = 16
    ctx = ExitStack()
    with ctx:
        def sb(name, shape, dt=FP32):
            return ctx.enter_context(nc.sbuf_tensor(name, shape, dt))

        def sem(name):
            return ctx.enter_context(nc.semaphore(name))

        rw_sb = sb("e_rw", [128, 2, 16])
        rb_sb = sb("e_rb", [16, 1])
        w1_sb = [sb(f"e_w1_{i}", [128, 2, D]) for i in range(2)]
        w2_sb = [sb(f"e_w2_{i}", [128, 2, D]) for i in range(2)]
        b1_sb = [sb(f"e_b1_{i}", [128, 2]) for i in range(2)]
        b2_sb = sb("e_b2", [128, D])
        logT = sb("e_logT", [16, CH])
        top = sb("e_top", [128, 4])
        expd = sb("e_expd", [128, 4, 15])
        total = sb("e_total", [128, 4])
        probs = sb("e_probs", [128, 4, 24])
        best = sb("e_best", [128, 4, 8])
        chosen = sb("e_chosen", [128, 4, 8])
        rest = sb("e_rest", [128, 4, 24])
        cw_chunk = sb("e_cw_chunk", [128, 4, 32])
        cw = sb("e_cw", [128, 32, 16])
        cwT = sb("e_cwT", [128, 128])
        hT = [sb(f"e_hT{i}", [128, 2, CH]) for i in range(2)]
        spare = sb("e_spare", [128, 8])
        ln = LnTiles(sb, "e")
        loaded = sem("e_loaded")
        w_loaded = [sem(f"e_w_loaded{i}") for i in range(2)]
        const_ready = sem("e_const_ready")
        logits_ready = sem("e_logits_ready")
        logT_ready = sem("e_logT_ready")
        log_turned = sem("e_log_turned")
        route = sem("e_route")
        exp_ready = sem("e_exp_ready")
        cw_ready = sem("e_cw_ready")
        cw_kept = sem("e_cw_kept")
        cw_turned = sem("e_cw_turned")
        cwT_ready = sem("e_cwT_ready")
        bias_ready = sem("e_bias_ready")
        bias_added = sem("e_bias_added")
        up_ready = sem("e_up_ready")
        relu_done = sem("e_relu_done")
        down_ready = sem("e_down_ready")
        added = sem("e_added")
        stored = sem("e_stored")
        lns = LnSems(sem, "e")
        ROUTE = 10
        block = ctx.enter_context(nc.Block())

        @block.sync
        def _(sync):
            for dst, src in ((rw_sb[:, :, :], router_w), (rb_sb[:, :], router_b),
                             (b2_sb[:, :], b2), (probs[:, :, 15:24], pads[:, :, 0:9]),
                             (chosen[:, :, 3:8], pads[:, :, 0:5])):
                sync.dma_start(dst, src).then_inc(loaded, 16)
            for e in range(2):
                sync.dma_start(w1_sb[e][:, :, :], w1[e]).then_inc(w_loaded[e], 16)
                sync.dma_start(w2_sb[e][:, :, :], w2[e]).then_inc(w_loaded[e], 16)
                sync.dma_start(b1_sb[e][:, :], b1[e]).then_inc(w_loaded[e], 16)
            with nc.sync.Fori(0, NE // 2 - 1) as pair:
                for i in range(2):
                    expert = nc.sync.snap(pair * 2 + (i + 2))
                    sync.wait_ge(down_ready, (pair * 2 + i + 1) * NCH * 2 + 4)
                    sync.dma_start(b1_sb[i][:, :], b1[bass.ds(expert, 1)].rearrange("a p k -> p (a k)")).then_inc(w_loaded[i], 16)
                    sync.dma_start(w1_sb[i][:, :, :], w1[bass.ds(expert, 1)].rearrange("a p k d -> p (a k) d")).then_inc(w_loaded[i], 16)
                    sync.dma_start(w2_sb[i][:, :, :], w2[bass.ds(expert, 1)].rearrange("a p k d -> p (a k) d")).then_inc(w_loaded[i], 16)
            with nc.sync.Fori(0, NCH) as c:
                first_tile = nc.sync.snap(c * 4)
                sync.wait_ge(lns.done, (c + 2) * 4)
                sync.dma_start(out[:, bass.ds(first_tile, 4), :], ln.nrm[:, :, :]).then_inc(stored, 16)
            sync.wait_ge(stored, 16 * (NCH + 1))

        @block.tensor
        def _(pe):
            pe.wait_ge(loaded, 16 * 5)
            pe.wait_ge(const_ready, 3)
            with nc.tensor.Fori(0, NCH) as c:
                pe.wait_ge(bias_added, c + 1)
                for k in range(2):
                    last = nc.tensor.matmul(P[0:16, 0, :], rw_sb[:, k, :], XT[:, k, bass.ds(c * CH, CH)],
                                            start=(k == 0), stop=(k == 1))
                last.then_inc(logits_ready, 1)
                pe.wait_ge(logT_ready, c + 1)
                for t in range(4):
                    last = nc.tensor.matmul(P[:, 1, t * 16:(t + 1) * 16], logT[:, t * 128:(t + 1) * 128],
                                            ident[0:16, 0:16], start=True, stop=True)
                last.then_inc(log_turned, 1)
                pe.wait_ge(cw_ready, c + 1)
                nc.tensor.transpose(P[:, 2, 0:128], cw_chunk[:, :, :].rearrange("p t e -> p (t e)"),
                                    ident[:, :]).then_inc(cw_turned, 1)
                pe.wait_ge(cwT_ready, c + 1)
                for t in range(4):
                    last = nc.tensor.matmul(P[:, 4 + t, 0:D], cwT[32 * t:32 * t + 16, :], b2_sb[32 * t:32 * t + 16, :],
                                            start=True, stop=True)
                last.then_inc(bias_ready, 1)
            pe.wait_ge(bias_added, NCH + 1)

            def up(i, par, n, c):
                pe.wait_ge(relu_done, n * 2 + 2)
                for m in range(2):
                    for k in range(2):
                        last = nc.tensor.matmul(P[:, 2 * par + m, :], w1_sb[i][:, k, m * 128:(m + 1) * 128],
                                                XT[:, k, bass.ds(c * CH, CH)], start=(k == 0), stop=(k == 1))
                    last.then_inc(up_ready, 1)

            def down(i, par, n):
                pe.wait_ge(relu_done, n * 2 + 6)
                pe.wait_ge(added, n * 4 + 4)
                for t in range(4):
                    for k in range(2):
                        last = nc.tensor.matmul(P[:, 4 + 2 * par + t // 2, (t % 2) * D:(t % 2) * D + D],
                                                hT[par][:, k, t * 128:(t + 1) * 128], w2_sb[i][:, k, :],
                                                start=(k == 0), stop=(k == 1))
                    if t % 2:
                        last.then_inc(down_ready, 1)

            def expert(i, e, w_count, final):
                with nc.tensor.Fori(0, NCH // 2 - 1) as j:
                    up(i, 1, e * NCH + j * 2 + 1, j * 2 + 1)
                    down(i, 0, e * NCH + j * 2)
                    up(i, 0, e * NCH + j * 2 + 2, j * 2 + 2)
                    down(i, 1, e * NCH + j * 2 + 1)
                up(i, 1, e * NCH + NCH - 1, NCH - 1)
                down(i, 0, e * NCH + NCH - 2)
                if not final:
                    pe.wait_ge(w_loaded[1 - i], w_count)
                    up(1 - i, 0, e * NCH + NCH, 0)
                down(i, 1, e * NCH + NCH - 1)

            pe.wait_ge(w_loaded[0], 48)
            up(0, 0, 0, 0)
            with nc.tensor.Fori(0, NE // 2 - 1) as pair:
                expert(0, pair * 2, (pair + 1) * 48, False)
                expert(1, pair * 2 + 1, (pair + 2) * 48, False)
            expert(0, NE - 2, NE // 2 * 48, False)
            expert(1, NE - 1, 0, True)

        @block.scalar
        def _(act):
            act.wait_ge(loaded, 16 * 5)
            with nc.scalar.Fori(0, NCH) as c:
                act.wait_ge(logits_ready, c + 1)
                nc.scalar.activation(logT[:, :], P[0:16, 0, :], ACT.Identity, bias=rb_sb[:, 0:1]).then_inc(logT_ready, 1)
                act.wait_ge(route, c * ROUTE + 2)
                nc.scalar.activation(expd[:, :, :], expd[:, :, :], ACT.Exp).then_inc(exp_ready, 1)
                act.wait_ge(cw_turned, c + 1)
                nc.scalar.copy(cwT[:, :], P[:, 2, 0:128]).then_inc(cwT_ready, 1)

            def relus(par, n, i):
                act.wait_ge(down_ready, n * 2 + 2)
                for m in range(2):
                    act.wait_ge(up_ready, n * 2 + m + 1)
                    nc.scalar.activation(hT[par][:, m, :], P[:, 2 * par + m, :], ACT.Relu,
                                         bias=b1_sb[i][:, m:m + 1]).then_inc(relu_done, 1)

            with nc.scalar.Fori(0, NE // 2) as pair:
                for i in range(2):
                    act.wait_ge(w_loaded[i], (pair + 1) * 48)
                    with nc.scalar.Fori(0, NCH // 2) as j:
                        relus(0, (pair * 2 + i) * NCH + j * 2, i)
                        relus(1, (pair * 2 + i) * NCH + j * 2 + 1, i)

        @block.gpsimd
        def _(pool):
            pool.wait_ge(const_ready, 3)
            with nc.gpsimd.Fori(0, NCH) as c:
                first_tile = nc.gpsimd.snap(c * 4)
                pool.wait_ge(cw_ready, c + 1)
                nc.gpsimd.tensor_tensor(cw[:, bass.ds(first_tile, 4), :], cw_chunk[:, :, 0:16], cw_chunk[:, :, 16:32],
                                        ALU.add).then_inc(cw_kept, 1)
            pool.wait_ge(lns.half, 1)
            with nc.gpsimd.Fori(0, NCH) as c:
                ln_pool(nc, pool, ln, lns, c)

        @block.vector
        def _(dve):
            ln_start(nc, ln, lns)
            nc.vector.memset(spare[:, 7:8], 0.0).then_inc(stored, 16)
            nc.vector.memset(cw_chunk[:, :, :], 0.0).then_inc(const_ready, 1)
            nc.vector.memset(spare[:, 0:1], 0.0).then_inc(relu_done, 4)
            nc.vector.memset(spare[:, 1:2], 0.0).then_inc(down_ready, 4)
            nc.vector.memset(spare[:, 2:3], 0.0).then_inc(added, 8)
            nc.vector.memset(spare[:, 3:4], 0.0).then_inc(bias_added, 1)
            dve.wait_ge(const_ready, 1)
            nc.vector.memset(cw_chunk[:, :, 15:16], 1.0).then_inc(const_ready, 1)
            nc.vector.memset(best[:, :, :], 0.0).then_inc(const_ready, 1)
            dve.wait_ge(const_ready, 3)
            dve.wait_ge(loaded, 16 * 5)
            with nc.vector.Fori(0, NCH) as c:
                at = c * ROUTE
                logits = P[:, 1, 0:64].rearrange("p (t e) -> p t e", e=16)[:, :, 0:15]
                dve.wait_ge(log_turned, c + 1)
                nc.vector.tensor_reduce(top[:, :], logits, axis=AX.X, op=ALU.max).then_inc(route, 1)
                dve.wait_ge(route, at + 1)
                nc.vector.tensor_tensor(expd[:, :, :], logits, top[:, :].unsqueeze(2).to_broadcast([128, 4, 15]),
                                        ALU.subtract).then_inc(route, 1)
                dve.wait_ge(exp_ready, c + 1)
                nc.vector.tensor_reduce(total[:, :], expd[:, :, :], axis=AX.X, op=ALU.add).then_inc(route, 1)
                dve.wait_ge(route, at + 3)
                nc.vector.reciprocal(total[:, :], total[:, :]).then_inc(route, 1)
                dve.wait_ge(route, at + 4)
                nc.vector.tensor_tensor(probs[:, :, 0:15], expd[:, :, :],
                                        total[:, :].unsqueeze(2).to_broadcast([128, 4, 15]), ALU.mult).then_inc(route, 1)
                dve.wait_ge(route, at + 5)
                nc.vector.memset(spare[:, 4:5], 0.0)
                for t in range(4):
                    last = nc.vector.max(best[:, t, :], probs[:, t, 0:15])
                last.then_inc(route, 1)
                dve.wait_ge(route, at + 6)
                nc.vector.tensor_copy(chosen[:, :, 0:3], best[:, :, 0:3]).then_inc(route, 1)
                dve.wait_ge(route, at + 7)
                nc.vector.memset(spare[:, 5:6], 0.0)
                for t in range(4):
                    last = nc.vector.match_replace(rest[:, t, :], chosen[:, t, :], probs[:, t, :], 0.0)
                last.then_inc(route, 1)
                dve.wait_ge(route, at + 8)
                nc.vector.tensor_tensor(cw_chunk[:, :, 0:15], probs[:, :, 0:15], rest[:, :, 0:15],
                                        ALU.subtract).then_inc(cw_ready, 1)
                nc.vector.memset(spare[:, 6:7], 0.0).then_inc(route, 2)
                dve.wait_ge(cw_kept, c + 1)
                dve.wait_ge(bias_ready, c + 1)
                nc.vector.tensor_tensor(XN[:, bass.ds(c * 4, 4), :], P[:, 4:8, 0:D], XN[:, bass.ds(c * 4, 4), :],
                                        ALU.add).then_inc(bias_added, 1)
            dve.wait_ge(cw_kept, NCH)
            dve.wait_ge(bias_added, NCH + 1)

            def add(par, n, c, e, last_expert):
                for t in range(4):
                    dve.wait_ge(down_ready, n * 2 + 4 + t // 2 + 1)
                    tile = c * 4 + t
                    dst = ln.res[:, t, :] if last_expert else XN[:, tile, :]
                    nc.vector.scalar_tensor_tensor(dst, P[:, 4 + 2 * par + t // 2, (t % 2) * D:(t % 2) * D + D],
                                                   cw[:, tile, bass.ds(e, 1)], XN[:, tile, :],
                                                   ALU.mult, ALU.add).then_inc(added, 1)

            with nc.vector.Fori(0, NE - 1) as e:
                with nc.vector.Fori(0, NCH // 2) as j:
                    dve.wait_ge(added, e * 32 + j * 8 + 8)
                    add(0, e * NCH + j * 2, j * 2, e, False)
                    add(1, e * NCH + j * 2 + 1, j * 2 + 1, e, False)
            with nc.vector.Fori(0, NCH // 2) as j:
                for par in range(2):
                    c = j * 2 + par
                    dve.wait_ge(lns.done, (c + 1) * 4)
                    add(par, (NE - 1) * NCH + c, c, NE - 1, True)
                    dve.wait_ge(added, (NE - 1) * 32 + c * 4 + 12)
                    ln_dve(nc, dve, ln, lns, c, stored, 16)


def block_kernel(nc, T, out):
    bc_scratch = nc.dram_tensor("bc_scratch", [2 * NS, CH], FP32, kind="Internal").ap()
    ctx = ExitStack()
    with ctx:
        XN = ctx.enter_context(nc.sbuf_tensor("XN", [128, TOK // 128, D], FP32))
        XT = ctx.enter_context(nc.sbuf_tensor("XT", [128, 2, TOK], FP32))
        ident = ctx.enter_context(nc.sbuf_tensor("ident", [128, 128], FP32))
        P = ctx.enter_context(nc.psum_tensor("P", [128, 8, CH], FP32))
        ident_loaded = ctx.enter_context(nc.semaphore("ident_loaded"))
        with nc.Block() as block:
            @block.sync
            def _(sync):
                sync.dma_start(ident[:, :], T["eye"]).then_inc(ident_loaded, 16)
                sync.wait_ge(ident_loaded, 16)
        mamba_phase(nc, XN, XT, P, ident, T["x_tok"], T["x_feat"], T["m_w_in"], T["m_conv_w"], T["m_conv_b"],
                    T["m_w_x"], T["m_w_dt"], T["m_b_dt"], T["m_a_log"], T["m_w_out"], bc_scratch)
        ffn_phase(nc, XN, XT, P, ident, T["f_w1"], T["f_w1_rows"], T["f_b1"], T["f_w2"], T["f_b2"])
        attn_phase(nc, XN, XT, P, ident, T["a_wq"], T["a_wk"], T["a_wv"], T["a_wo"], T["a_bo"], T["a_masks"])
        moe_phase(nc, XN, XT, P, ident, T["e_rw"], T["e_rb"], T["e_w1"], T["e_b1"], T["e_w2"], T["e_b2"],
                  T["e_pads"], out)


def _partitioned(a):
    return a.reshape((-1, 128) + a.shape[1:]).swapaxes(0, 1)


def _contraction_first(w):
    return _partitioned(w.T)


def _masks():
    r, c = np.arange(128)[:, None], np.arange(192)[None, :]
    band = (r <= c) & (c <= r + 64)
    allowed = [c <= r, band, band & (c >= 64), r <= c, band]
    return np.where(np.stack(allowed, 1), 0.0, -1e30).astype(np.float32)


def kernel(**inputs):
    import concourse.bacc as _bacc
    from concourse.bass_utils import run_bass_kernel_spmd as _run

    a = {k: np.asarray(v) for k, v in inputs.items()}
    x = a["L0_attn_x"].reshape(TOK, D)
    experts = {k: np.concatenate([a["L1_ffn_e" + k], a["L1_ffn_s" + k][None]]) for k in ("W1", "b1", "W2", "b2")}
    wo = np.zeros((4, 32, 4, D), np.float32)
    wo[:, :16] = a["L1_attn_Wo"].T.reshape(4, 4, 16, D).transpose(1, 2, 0, 3)
    router_w = np.zeros((D, 16), np.float32)
    router_w[:, :15] = a["L1_ffn_router_W"]
    router_b = np.zeros((16, 1), np.float32)
    router_b[:15, 0] = a["L1_ffn_router_b"]
    b2 = np.zeros((4, 32, D), np.float32)
    b2[:, :16] = experts["b2"]
    laid_out = {
        "eye": np.eye(128, dtype=np.float32),
        "x_tok": _partitioned(x),
        "x_feat": _contraction_first(x),
        "m_w_in": _contraction_first(a["L0_attn_W_in"]),
        "m_conv_w": _partitioned(a["L0_attn_conv_w"].reshape(512, 4)),
        "m_conv_b": _partitioned(a["L0_attn_conv_b"]),
        "m_w_x": _contraction_first(a["L0_attn_W_x"]),
        "m_w_dt": a["L0_attn_W_dt"].T,
        "m_b_dt": _partitioned(a["L0_attn_b_dt"]),
        "m_a_log": _partitioned(a["L0_attn_A_log"]),
        "m_w_out": _contraction_first(a["L0_attn_W_out"]),
        "f_w1": _contraction_first(a["L0_ffn_w1"]),
        "f_w1_rows": _partitioned(a["L0_ffn_w1"]),
        "f_b1": _partitioned(a["L0_ffn_b1"]),
        "f_w2": _contraction_first(a["L0_ffn_w2"]),
        "f_b2": a["L0_ffn_b2"],
        "a_wq": _contraction_first(a["L1_attn_Wq"]),
        "a_wk": _contraction_first(a["L1_attn_Wk"]),
        "a_wv": _contraction_first(a["L1_attn_Wv"]),
        "a_wo": wo.reshape(128, 4, D),
        "a_bo": a["L1_attn_bo"],
        "a_masks": _masks(),
        "e_rw": _partitioned(router_w),
        "e_rb": router_b,
        "e_w1": experts["W1"].reshape(16, 2, 128, D).transpose(0, 2, 1, 3),
        "e_b1": experts["b1"].reshape(16, 2, 128).transpose(0, 2, 1),
        "e_w2": experts["W2"].reshape(16, 2, 128, D).transpose(0, 2, 1, 3),
        "e_b2": b2.reshape(128, D),
        "e_pads": np.broadcast_to(-1.0 - np.arange(9, dtype=np.float32), (128, 4, 9)),
    }
    nc = _bacc.Bacc("TRN2", target_bir_lowering=False, num_devices=1)
    arrays = {"in_" + n: np.ascontiguousarray(v) for n, v in laid_out.items()}
    T = {n: nc.dram_tensor("in_" + n, v.shape, mybir.dt.from_np(v.dtype), kind="ExternalInput").ap()
         for n, v in laid_out.items()}
    out = nc.dram_tensor("out", (128, TOK // 128, D), FP32, kind="ExternalOutput").ap()
    block_kernel(nc, T, out)
    r = _run(nc, [arrays], core_ids=[0])
    return r.results[0]["out"].transpose(1, 0, 2).reshape(NB, SEQ, D)
```

```python
import numpy as np
import concourse.bass as bass
from concourse import mybir
from contextlib import ExitStack

FP32 = mybir.dt.float32
BF16 = mybir.dt.bfloat16
FP32R = mybir.dt.float32r
ALU = mybir.AluOpType
ACT = mybir.ActivationFunctionType
AX = mybir.AxisListType

NB = 4
SEQ = 1024
TOK = NB * SEQ
D = 256
CH = 512
NCH = TOK // CH
DT = 4
NS = 16
EPS = 1e-5


class LnTiles:

    def __init__(self, sb, p, res=None, nrm=None):
        self.res = sb(p + "_ln_res", [128, 4, D]) if res is None else res
        self.nrm = sb(p + "_ln_nrm", [128, 4, D]) if nrm is None else nrm
        self.stats = sb(p + "_ln_stats", [128, 4, 6])
        self.mean = sb(p + "_ln_mean", [128, 4])
        self.diff = sb(p + "_ln_diff", [128, 4])
        self.var = sb(p + "_ln_var", [128, 4])
        self.rstd = sb(p + "_ln_rstd", [128, 4])
        self.minus_half = sb(p + "_ln_minus_half", [128, 4])


class LnSems:

    def __init__(self, sem, p):
        self.steps = sem(p + "_ln_steps")
        self.rstd = sem(p + "_ln_rstd_ready")
        self.done = sem(p + "_ln_done")
        self.half = sem(p + "_ln_half_ready")
        self.turned = sem(p + "_ln_turned")
        self.stored = sem(p + "_ln_stored")


LN_STEPS = 11


def two_banks(P, at):
    return P[:, at:at + 2, :].rearrange("p b (t d) -> p (b t) d", d=D)


def over_tiles(row):
    return row[:, :].unsqueeze(1).to_broadcast([128, 4, D])


def ln_start(nc, ln, lns):
    nc.vector.memset(ln.minus_half[:, :], -0.5).then_inc(lns.half, 1)
    nc.vector.memset(ln.diff[:, :], 0.0).then_inc(lns.stored, 1)
    nc.vector.memset(ln.mean[:, :], 0.0).then_inc(lns.done, 4)


def ln_moments(nc, dve, ln, lns, step, count):
    dve.wait_ge(lns.steps, count[0])
    step(nc.vector.tensor_tensor(ln.mean[:, :], ln.stats[:, :, 1], ln.stats[:, :, 4], ALU.add))
    step(nc.vector.tensor_tensor(ln.diff[:, :], ln.stats[:, :, 1], ln.stats[:, :, 4], ALU.subtract))
    step(nc.vector.tensor_tensor(ln.var[:, :], ln.stats[:, :, 2], ln.stats[:, :, 5], ALU.add))
    dve.wait_ge(lns.steps, count[0])
    step(nc.vector.tensor_tensor(ln.diff[:, :], ln.diff[:, :], ln.diff[:, :], ALU.mult))
    step(nc.vector.tensor_scalar(ln.var[:, :], ln.var[:, :], 1.0 / D, EPS, ALU.mult, ALU.add))
    step(nc.vector.tensor_scalar(ln.mean[:, :], ln.mean[:, :], 0.5, None, ALU.mult))
    dve.wait_ge(lns.steps, count[0])
    step(nc.vector.scalar_tensor_tensor(ln.var[:, :], ln.diff[:, :], 0.25, ln.var[:, :], ALU.mult, ALU.add))


def ln_dve(nc, dve, ln, lns, c, stored=None, each=1):
    count = [c * LN_STEPS]

    def step(ins):
        ins.then_inc(lns.steps, 1)
        count[0] = count[0] + 1

    for t in range(4):
        step(nc.vector.bn_stats(ln.stats[:, t, :], ln.res[:, t, :]))
    ln_moments(nc, dve, ln, lns, step, count)
    dve.wait_ge(lns.rstd, c + 1)
    dve.wait_ge(lns.stored if stored is None else stored, (c + 1) * each)
    for t in range(4):
        nc.vector.tensor_scalar(ln.nrm[:, t, :], ln.res[:, t, :], ln.mean[:, t:t + 1],
                                ln.rstd[:, t:t + 1], ALU.subtract, ALU.mult).then_inc(lns.done, 1)


def ln_pool(nc, pool, ln, lns, c):
    pool.wait_ge(lns.steps, (c + 1) * LN_STEPS)
    nc.gpsimd.tensor_tensor(ln.rstd[:, :], ln.var[:, :], ln.minus_half[:, :], ALU.pow).then_inc(lns.rstd, 1)


def ln_pe(nc, pe, ln, lns, P, bank, ident, c):
    pe.wait_ge(lns.done, (c + 2) * 4)
    for k in range(2):
        for t in range(4):
            last = nc.tensor.transpose(P[:, bank + k, t * 128:(t + 1) * 128], ln.nrm[:, t, k * 128:(k + 1) * 128],
                                       ident[:, :])
    last.then_inc(lns.turned, 1)


def ln_act(nc, act, ln, lns, P, bank, XN, XT, c):
    act.wait_ge(lns.done, (c + 2) * 4)
    nc.scalar.copy(XN[:, bass.ds(c * 4, 4), :], ln.nrm[:, :, :])
    act.wait_ge(lns.turned, c + 1)
    nc.scalar.copy(XT[:, :, bass.ds(c * CH, CH)], P[:, bank:bank + 2, :]).then_inc(lns.stored, 1)
def mamba_phase(nc, XN, P, ident, x_tok, x_feat, w_in, conv_w, conv_b, w_x, w_dt, b_dt, a_log, w_out, bc_scratch):
    ctx = ExitStack()
    with ctx:
        def sb(name, shape, dt=FP32):
            return ctx.enter_context(nc.sbuf_tensor(name, shape, dt))

        def sem(name):
            return ctx.enter_context(nc.semaphore(name))

        w_in_sb = sb("w_in_sb", [128, 2, 1024])
        w_x_sb = sb("w_x_sb", [128, DT, 96])
        w_dt_sb = sb("w_dt_sb", [64, 512])
        w_out_sb = sb("w_out_sb", [128, DT, 256])
        conv_w_sb = sb("conv_w_sb", [128, DT, 4])
        conv_b_sb = sb("conv_b_sb", [128, DT])
        b_dt_sb = sb("b_dt_sb", [128, DT])
        a_neg = sb("a_neg", [128, DT, NS])
        a_exp = sb("a_exp", [128, DT, NS])
        xT = sb("m_xT", [128, 2, CH])
        xs = sb("m_xs", [128, DT, CH + 3])
        conv = sb("m_conv", [128, DT, CH])
        sp = conv
        gate = [sb(f"m_gate{i}", [128, DT, CH]) for i in range(2)]
        u = [sb(f"m_u{i}", [128, DT, CH]) for i in range(2)]
        z = [sb(f"m_z{i}", [128, DT, CH]) for i in range(2)]
        du, delta = u, z
        low = sb("m_low", [64, CH])
        bc_own = sb("m_bc_own", [96, CH])
        bc = sb("m_bc", [128, 2 * NS, CH])
        dbu = sb("m_dbu", [128, 4, CH])
        h3 = sb("m_h3", [128, CH])
        g = sb("m_g", [128, 4, CH])
        state = sb("m_state", [128, DT, NS])
        spare = sb("m_spare", [128, 2])
        ln = LnTiles(sb, "m", XN, XN)

        w_loaded = sem("m_w_loaded")
        x_loaded = sem("m_x_loaded")
        xT_loaded = sem("m_xT_loaded")
        scratch_written = sem("m_scratch_written")
        bc_loaded = [sem(f"m_bc_loaded{k}") for k in range(4)]
        a_ready = sem("m_a_ready")
        xr_ready = sem("m_xr_ready")
        xs_ready = sem("m_xs_ready")
        conv_part = [sem(f"m_conv_part{i}") for i in range(DT)]
        conv_done = sem("m_conv_done")
        xs_head = sem("m_xs_head")
        gate_ready = sem("m_gate_ready")
        u_ready = sem("m_u_ready")
        xdbl_ready = sem("m_xdbl_ready")
        low_ready = sem("m_low_ready")
        bc_own_ready = sem("m_bc_own_ready")
        dlow_ready = sem("m_dlow_ready")
        z_ready = sem("m_z_ready")
        sp_step = sem("m_sp_step")
        delta_ready = sem("m_delta_ready")
        du_ready = sem("m_du_ready")
        dA_ready = sem("m_dA_ready")
        dbu_ready = sem("m_dbu_ready")
        h_ready = sem("m_h_ready")
        g_dve = sem("m_g_dve")
        g_pool = sem("m_g_pool")
        summed = sem("m_summed")
        state_pool = sem("m_state_pool")
        state_dve = sem("m_state_dve")
        gated = sem("m_gated")
        proj_ready = sem("m_proj_ready")
        res_added = sem("m_res_added")
        lns = LnSems(sem, "m")

        DA, H, Y, SIDE = (0, 1), (2, 3, 4), (5, 6), 7
        block = ctx.enter_context(nc.Block())

        def at_start(c, dt, q):
            return isinstance(c, int) and c == 0 and dt == 0 and q == 0

        def none_before(c):
            return isinstance(c, int) and c == 0

        def all_chunks(engine, chunk):
            with engine.Fori(0, NB - 1) as b:
                for half in range(2):
                    chunk(b * 2 + half, b, half, False)
            for half in range(2):
                chunk((NB - 1) * 2 + half, NB - 1, half, half == 1)

        @block.sync
        def _(sync):
            for dst, src in ((w_in_sb, w_in), (w_x_sb, w_x), (w_out_sb, w_out), (conv_w_sb, conv_w)):
                sync.dma_start(dst[:, :, :], src).then_inc(w_loaded, 16)
            for dst, src in ((w_dt_sb, w_dt), (conv_b_sb, conv_b), (b_dt_sb, b_dt)):
                sync.dma_start(dst[:, :], src).then_inc(w_loaded, 16)
            sync.dma_start(a_exp[:, :, :], a_log).then_inc(w_loaded, 16)

            def load_xT(c):
                if none_before(c):
                    here = 0
                else:
                    here = c * CH if isinstance(c, int) else nc.sync.snap(c * CH)
                    sync.wait_ge(xr_ready, c * 8)
                sync.dma_start(xT[:, :, :], x_feat[:, :, bass.ds(here, CH)]).then_inc(xT_loaded, 16)

            def load_bc(c):
                sync.wait_ge(bc_own_ready, c + 1)
                sync.dma_start(bc_scratch, bc_own[64:96, :]).then_inc(scratch_written, 16)
                used = [(c - 1) * 64 + 48 + 4 * (k + 1) for k in range(4)]
                if not isinstance(c, int):
                    used = [nc.sync.snap(n) for n in used]
                sync.wait_ge(scratch_written, (c + 1) * 16)
                for k in range(4):
                    if not none_before(c):
                        sync.wait_ge(summed, used[k])
                    for s in (0, NS):
                        rows = slice(s + 4 * k, s + 4 * k + 4)
                        sync.dma_start(bc[:, rows, :],
                                       bc_scratch[rows, :].partition_broadcast(128)).then_inc(bc_loaded[k], 16)

            load_xT(0)
            sync.dma_start(XN[:, :, :], x_tok).then_inc(x_loaded, 16)
            load_bc(0)

            def chunk(c, b, half, last):
                if not last:
                    load_xT(c + 1)
                    load_bc(c + 1)
            all_chunks(nc.sync, chunk)

        @block.tensor
        def _(pe):
            pe.wait_ge(w_loaded, 16 * 8)

            def project_in(c, m):
                if m == 0:
                    pe.wait_ge(xT_loaded, (c + 1) * 16)
                    if not none_before(c):
                        pe.wait_ge(res_added, c * 2)
                elif m <= 4:
                    pe.wait_ge(xs_ready, c * DT + m)
                else:
                    pe.wait_ge(gate_ready, c * DT + m - 4)
                for k in range(2):
                    last = nc.tensor.matmul(P[:, SIDE, :], w_in_sb[:, k, m * 128:(m + 1) * 128], xT[:, k, :],
                                            start=(k == 0), stop=(k == 1))
                last.then_inc(xr_ready, 1)

            def project_x(c, par):
                pe.wait_ge(gate_ready, (c + 1) * DT)
                pe.wait_ge(u_ready, (c + 1) * DT)
                for k in range(DT):
                    last = nc.tensor.matmul(P[0:96, SIDE, :], w_x_sb[:, k, :], u[par][:, k, :],
                                            start=(k == 0), stop=(k == DT - 1))
                last.then_inc(xdbl_ready, 1)

            def project_dt(c, m):
                if m == 0:
                    pe.wait_ge(low_ready, c + 1)
                    pe.wait_ge(bc_own_ready, c + 1)
                else:
                    pe.wait_ge(z_ready, c * DT + m)
                nc.tensor.matmul(P[:, SIDE, :], w_dt_sb[:, m * 128:(m + 1) * 128], low[:, :],
                                 start=True, stop=True).then_inc(dlow_ready, 1)

            def prepare(c, par, slot):
                if slot < 8:
                    project_in(c, slot)
                if slot == 11:
                    project_x(c, par)
                if 15 <= slot < 19:
                    project_dt(c, slot - 15)

            def project_out(c, par, pair, final=False):
                if pair == 0:
                    if not final:
                        pe.wait_ge(z_ready, (c + 2) * DT)
                    pe.wait_ge(gated, (c + 1) * DT + 2)
                else:
                    pe.wait_ge(res_added, c * 2 + 3)
                for t in (2 * pair, 2 * pair + 1):
                    for k in range(DT):
                        last = nc.tensor.matmul(P[:, SIDE, (t % 2) * 256:(t % 2) * 256 + 256],
                                                gate[par][:, k, t * 128:(t + 1) * 128], w_out_sb[:, k, :],
                                                start=(k == 0), stop=(k == DT - 1))
                last.then_inc(proj_ready, 1)

            def units(c, dt, q, rs):
                for r in rs:
                    if r == 0 and q == 0:
                        pe.wait_ge(gated, c * DT + dt + 1)
                    if r < 3:
                        pe.wait_ge(g_dve, c * 48 + 12 * dt + q * 3 + r + 1)
                    else:
                        pe.wait_ge(g_pool, c * 16 + 4 * dt + q + 1)
                    nc.tensor.matmul(P[:, Y[dt % 2], :], ident[:, :], g[:, r, :], start=(q == 0 and r == 0),
                                     stop=(q == 3 and r == 3)).then_inc(summed, 1)

            for slot in range(24):
                prepare(0, 0, slot)
            for q in range(4):
                units(0, 0, q, range(4))

            def chunk(c, b, half, last):
                for s in range(12):
                    for pair in range(2):
                        units(c, 1 + s // 4, s % 4, (2 * pair, 2 * pair + 1))
                        if not last:
                            prepare(c + 1, 1 - half, 2 * s + pair)
                if last:
                    project_out(c, half, 0, True)
                    project_out(c, half, 1, True)
                else:
                    for q in range(4):
                        units(c + 1, 0, q, range(4))
                        if q < 2:
                            project_out(c, half, q)
            all_chunks(nc.tensor, chunk)

        @block.scalar
        def _(act):
            act.wait_ge(w_loaded, 16 * 8)
            nc.scalar.activation(a_exp[:, :, :], a_exp[:, :, :], ACT.Exp).then_inc(a_ready, 1)
            act.wait_ge(a_ready, 1)
            nc.scalar.mul(a_neg[:, :, :], a_exp[:, :, :], -1.0).then_inc(a_ready, 1)
            act.wait_ge(a_ready, 2)

            def prepare(c, par, slot):
                if 3 <= slot < 7:
                    m = slot - 3
                    if m == 0:
                        act.wait_ge(xs_head, c + 1)
                    act.wait_ge(xr_ready, c * 8 + m + 1)
                    nc.scalar.copy(xs[:, m, 3:CH + 3], P[:, SIDE, :]).then_inc(xs_ready, 1)
                if 7 <= slot < 11:
                    m = slot - 7
                    if m == 0 and not none_before(c):
                        act.wait_ge(proj_ready, c * 2)
                    act.wait_ge(xr_ready, c * 8 + 4 + m + 1)
                    nc.scalar.activation(gate[par][:, m, :], P[:, SIDE, :], ACT.Silu).then_inc(gate_ready, 1)
                if 11 <= slot < 13:
                    for m in (2 * slot - 22, 2 * slot - 21):
                        act.wait_ge(conv_done, c * DT + m + 1)
                        nc.scalar.activation(u[par][:, m, :], conv[:, m, :], ACT.Silu,
                                             bias=conv_b_sb[:, m:m + 1]).then_inc(u_ready, 1)
                if slot == 15:
                    act.wait_ge(xdbl_ready, c + 1)
                    nc.scalar.copy(low[:, :], P[0:64, SIDE, :]).then_inc(low_ready, 1)
                    if not none_before(c):
                        act.wait_ge(scratch_written, c * 16)
                    nc.scalar.copy(bc_own[64:96, :], P[64:96, SIDE, :]).then_inc(bc_own_ready, 1)
                if 18 <= slot < 22:
                    m = slot - 18
                    act.wait_ge(dlow_ready, c * DT + m + 1)
                    nc.scalar.activation(z[par][:, m, :], P[:, SIDE, :], ACT.Identity,
                                         bias=b_dt_sb[:, m:m + 1]).then_inc(z_ready, 1)
                if slot in (21, 22, 23):
                    for m in ((0, 1, 2, 3) if slot == 21 else ()):
                        if m == 0:
                            act.wait_ge(z_ready, (c + 1) * DT)
                        last = nc.scalar.activation(sp[:, m, :], z[par][:, m, :], ACT.Abs)
                    if slot == 22:
                        act.wait_ge(sp_step, c * 3 + 1)
                        last = nc.scalar.activation(sp[:, :, :], sp[:, :, :], ACT.Exp, scale=-1.0)
                    if slot == 23:
                        act.wait_ge(sp_step, c * 3 + 2)
                        last = nc.scalar.activation(sp[:, :, :], sp[:, :, :], ACT.Ln, bias=1.0)
                    last.then_inc(sp_step, 1)

            def decays(c, par, dt, q, rs):
                for r in rs:
                    unit = c * 64 + 16 * dt + q * 4 + r
                    if dt == 0 and q == 0 and r == 0:
                        act.wait_ge(delta_ready, c + 1)
                    if not (at_start(c, dt, q) and r < 2):
                        act.wait_ge(h_ready, unit - 1)
                    nc.scalar.activation(P[:, DA[r % 2], :], delta[par][:, dt, :], ACT.Exp,
                                         scale=a_neg[:, dt, q * 4 + r:q * 4 + r + 1]).then_inc(dA_ready, 1)

            for slot in range(24):
                prepare(0, 0, slot)
            for q in range(4):
                decays(0, 0, 0, q, range(4))

            def chunk(c, b, half, last):
                for s in range(12):
                    for pair in range(2):
                        decays(c, half, 1 + s // 4, s % 4, (2 * pair, 2 * pair + 1))
                        if not last:
                            prepare(c + 1, 1 - half, 2 * s + pair)
                if not last:
                    for q in range(4):
                        decays(c + 1, 1 - half, 0, q, range(4))
            all_chunks(nc.scalar, chunk)

        @block.gpsimd
        def _(pool):
            pool.wait_ge(lns.half, 1)

            def last_product(c, half, dt, q):
                unit = c * 64 + 16 * dt + q * 4 + 3
                pool.wait_ge(h_ready, unit + 1)
                if not at_start(c, dt, q):
                    pool.wait_ge(summed, unit - 3)
                nc.gpsimd.tensor_tensor(g[:, 3, :], h3[:, :], bc[:, NS + q * 4 + 3, :],
                                        ALU.mult).then_inc(g_pool, 1)
                if half == 0:
                    nc.gpsimd.tensor_copy(state[:, dt, q * 4 + 3:q * 4 + 4],
                                          h3[:, CH - 1:CH]).then_inc(state_pool, 1)

            def inputs(c, half, dt, q):
                for r in range(4):
                    unit = c * 64 + 16 * dt + q * 4 + r
                    if r == 0 and dt == 0:
                        pool.wait_ge(bc_loaded[q], (c + 1) * 32)
                        if q == 0:
                            pool.wait_ge(du_ready, c + 1)
                    if not at_start(c, dt, q):
                        pool.wait_ge(h_ready, unit - 3)
                    nc.gpsimd.tensor_tensor(dbu[:, r, :], du[half][:, dt, :], bc[:, q * 4 + r, :],
                                            ALU.mult).then_inc(dbu_ready, 1)
                    if r == 1 and not at_start(c, dt, q):
                        if q:
                            last_product(c, half, dt, q - 1)
                        elif dt:
                            last_product(c, half, dt - 1, 3)

            for q in range(4):
                inputs(0, 0, 0, q)

            def chunk(c, b, half, last):
                for s in range(12):
                    inputs(c, half, 1 + s // 4, s % 4)
                last_product(c, half, DT - 1, 3)
                if not last:
                    for q in range(4):
                        inputs(c + 1, 1 - half, 0, q)
                ln_pool(nc, pool, ln, lns, c)
            all_chunks(nc.gpsimd, chunk)

        @block.vector
        def _(dve):
            nc.vector.memset(ln.minus_half[:, :], -0.5).then_inc(lns.half, 1)
            nc.vector.memset(xs[:, :, 0:3], 0.0).then_inc(xs_head, 1)
            nc.vector.memset(state[:, :, :], 0.0).then_inc(gated, 2)
            nc.vector.memset(spare[:, 0:1], 0.0).then_inc(proj_ready, 2)
            nc.vector.memset(spare[:, 1:2], 0.0).then_inc(res_added, 2)
            dve.wait_ge(w_loaded, 16 * 8)

            def convolve(c, tiles):
                for tap in range(4):
                    for m in tiles:
                        if tap == 0:
                            dve.wait_ge(xs_ready, c * DT + m + 1)
                            if m == 0 and not none_before(c):
                                dve.wait_ge(delta_ready, c)
                            nc.vector.tensor_scalar(conv[:, m, :], xs[:, m, 0:CH], conv_w_sb[:, m, 0:1], None,
                                                    ALU.mult).then_inc(conv_part[m], 1)
                        else:
                            dve.wait_ge(conv_part[m], c * 3 + tap)
                            nc.vector.scalar_tensor_tensor(conv[:, m, :], xs[:, m, tap:CH + tap],
                                                           conv_w_sb[:, m, tap:tap + 1], conv[:, m, :],
                                                           ALU.mult, ALU.add).then_inc(
                                                               conv_part[m] if tap < 3 else conv_done, 1)

            def save_head(c, half):
                if half == 0:
                    nc.vector.tensor_copy(xs[:, :, 0:3], xs[:, :, CH:CH + 3]).then_inc(xs_head, 1)
                else:
                    nc.vector.memset(xs[:, :, 0:3], 0.0).then_inc(xs_head, 1)

            def finish_delta(c, par):
                dve.wait_ge(sp_step, (c + 1) * 3)
                nc.vector.scalar_tensor_tensor(delta[par][:, :, :], z[par][:, :, :], 0.0, sp[:, :, :],
                                               ALU.max, ALU.add).then_inc(delta_ready, 1)
                dve.wait_ge(delta_ready, c + 1)
                nc.vector.tensor_tensor(du[par][:, :, :], delta[par][:, :, :], u[par][:, :, :],
                                        ALU.mult).then_inc(du_ready, 1)

            def prepare(c, par, s):
                if s == 3:
                    convolve(c, (0, 1))
                if s == 4:
                    convolve(c, (2, 3))
                    save_head(c, par)
                if s == 11:
                    finish_delta(c, par)

            def scan(c, b, half, dt, q, r):
                unit = c * 64 + 16 * dt + q * 4 + r
                fresh = at_start(c, dt, q)
                dve.wait_ge(dA_ready, unit + 1)
                dve.wait_ge(dbu_ready, unit + 1)
                if half == 1 and dt == 0 and q == 0 and r == 0:
                    dve.wait_ge(state_pool, (b + 1) * 16)
                    dve.wait_ge(state_dve, (b + 1) * 16)
                if half == 0 and r == 0 and not (dt == 0 and q == 0):
                    dve.wait_ge(state_dve, b * 16 + 4 * dt + q)
                if (half == 1 or (dt == 0 and q == 0)) and r < 3 and not fresh:
                    dve.wait_ge(g_dve, c * 48 + 12 * dt + q * 3 - 3 + r + 1)
                if r == 3 and not fresh:
                    dve.wait_ge(g_pool, c * 16 + 4 * dt + q)
                    if half == 0:
                        dve.wait_ge(state_pool, b * 16 + 4 * dt + q)
                out = P[:, H[r], :] if r < 3 else h3[:, :]
                n = q * 4 + r
                initial = state[:, dt, n:n + 1] if half else 0.0
                nc.vector.tensor_tensor_scan(out, P[:, DA[r % 2], :], dbu[:, r, :], initial,
                                             ALU.mult, ALU.add).then_inc(h_ready, 1)

            def product(c, dt, q, r):
                unit = c * 64 + 16 * dt + q * 4 + r
                dve.wait_ge(h_ready, unit + 1)
                if not at_start(c, dt, q):
                    dve.wait_ge(summed, unit - 3)
                nc.vector.tensor_tensor(g[:, r, :], P[:, H[r], :], bc[:, NS + q * 4 + r, :],
                                        ALU.mult).then_inc(g_dve, 1)

            def units(c, b, half, dt, q):
                if dt == 0:
                    dve.wait_ge(bc_loaded[q], (c + 1) * 32)
                scan(c, b, half, dt, q, 0)
                scan(c, b, half, dt, q, 1)
                product(c, dt, q, 0)
                scan(c, b, half, dt, q, 2)
                product(c, dt, q, 1)
                scan(c, b, half, dt, q, 3)
                product(c, dt, q, 2)
                if half == 0:
                    nc.vector.tensor_copy(state[:, dt, q * 4:q * 4 + 3],
                                          P[:, H[0]:H[2] + 1, CH - 1]).then_inc(state_dve, 1)

            def gate_tile(c, half, d):
                dve.wait_ge(summed, c * 64 + 16 * (d + 1))
                nc.vector.tensor_tensor(gate[half][:, d, :], P[:, Y[d % 2], :], gate[half][:, d, :],
                                        ALU.mult).then_inc(gated, 1)

            def add_residual(c, pair):
                dve.wait_ge(proj_ready, c * 2 + pair + 3)
                here = XN[:, bass.ds(c * 4 + 2 * pair, 2), :]
                nc.vector.tensor_tensor(here, P[:, SIDE, :].rearrange("p (t d) -> p t d", d=D), here,
                                        ALU.add).then_inc(res_added, 1)

            def statistics(c):
                dve.wait_ge(res_added, c * 2 + 4)
                nc.vector.memset(spare[:, 0:1], 0.0)
                count = [c * LN_STEPS]

                def step(ins):
                    ins.then_inc(lns.steps, 1)
                    count[0] = count[0] + 1
                for t in range(4):
                    step(nc.vector.bn_stats(ln.stats[:, t, :], XN[:, c * 4 + t, :]))
                ln_moments(nc, dve, ln, lns, step, count)

            def normalise(c):
                dve.wait_ge(lns.rstd, c + 1)
                nc.vector.memset(spare[:, 1:2], 0.0)
                for t in range(4):
                    nc.vector.tensor_scalar(XN[:, c * 4 + t, :], XN[:, c * 4 + t, :], ln.mean[:, t:t + 1],
                                            ln.rstd[:, t:t + 1], ALU.subtract, ALU.mult).then_inc(lns.done, 1)

            convolve(0, (0, 1, 2, 3))
            save_head(0, 0)
            finish_delta(0, 0)
            dve.wait_ge(x_loaded, 16)
            dve.wait_ge(gate_ready, DT)
            for q in range(4):
                units(0, 0, 0, 0, q)

            def chunk(c, b, half, last):
                for s in range(12):
                    units(c, b, half, 1 + s // 4, s % 4)
                    if s % 4 == 0:
                        gate_tile(c, half, s // 4)
                    if not last:
                        prepare(c + 1, 1 - half, s)
                if last:
                    gate_tile(c, half, DT - 1)
                    add_residual(c, 0)
                    add_residual(c, 1)
                    statistics(c)
                else:
                    nb = b + 1 if half else b
                    units(c + 1, nb, 1 - half, 0, 0)
                    gate_tile(c, half, DT - 1)
                    units(c + 1, nb, 1 - half, 0, 1)
                    add_residual(c, 0)
                    units(c + 1, nb, 1 - half, 0, 2)
                    add_residual(c, 1)
                    statistics(c)
                    dve.wait_ge(gate_ready, (c + 2) * DT)
                    units(c + 1, nb, 1 - half, 0, 3)
                normalise(c)
            all_chunks(nc.vector, chunk)


def ffn_phase(nc, XN, XT, P, ident, w1, b1, w2, b2_all):
    MT = 8
    ctx = ExitStack()
    with ctx:
        def sb(name, shape, dt=FP32):
            return ctx.enter_context(nc.sbuf_tensor(name, shape, dt))

        def sem(name):
            return ctx.enter_context(nc.semaphore(name))

        w1_sb = sb("f_w1_sb", [128, 2, 1024])
        w2_sb = sb("f_w2_sb", [128, MT, D])
        w1_sign = sb("f_w1_sign", [128, 2, 1024], FP32R)
        w2_sign = sb("f_w2_sign", [128, MT, D], FP32R)
        b1_sb = sb("f_b1", [128, MT])
        b2_sb = sb("f_b2", [128, D])
        spare = sb("f_spare", [128, 2])
        ones = sb("f_ones", [128, 128])
        alpha1 = sb("f_alpha1", [128, MT])
        alpha2 = sb("f_alpha2", [128, D])
        x_hi = [sb(f"f_x_hi{i}", [128, 2, CH], FP32R) for i in range(2)]
        x_lo = [sb(f"f_x_lo{i}", [128, 2, CH], FP32R) for i in range(2)]
        x_chunk = [sb(f"f_x_chunk{i}", [128, 4, D]) for i in range(2)]
        h = sb("f_h", [128, 4, CH])
        h_hi = [sb(f"f_h_hi{i}", [128, MT, CH], FP32R) for i in range(2)]
        h_lo = [sb(f"f_h_lo{i}", [128, MT, CH], FP32R) for i in range(2)]
        ln_tiles = sb("f_ln_tiles", [128, 8, D])
        ln = LnTiles(sb, "f", ln_tiles[:, 0:4, :], ln_tiles[:, 4:8, :])
        w1_abs = h[:, :, :].rearrange("p a n -> p (a n)").rearrange("p (k n) -> p k n", k=2)
        w2_abs = ln_tiles
        w1_loaded = sem("f_w1_loaded")
        w2_loaded = sem("f_w2_loaded")
        signs_ready = sem("f_signs_ready")
        abs_ready = sem("f_abs_ready")
        means_summed = sem("f_means_summed")
        alpha1_ready = sem("f_alpha1_ready")
        alpha2_ready = sem("f_alpha2_ready")
        ones_ready = sem("f_ones_ready")
        x_turned = sem("f_x_turned")
        x_kept = sem("f_x_kept")
        x_loaded = [sem(f"f_x_loaded{i}") for i in range(2)]
        x_hi_ready = sem("f_x_hi_ready")
        x_lo_ready = sem("f_x_lo_ready")
        up_ready = sem("f_up_ready")
        gelu_done = sem("f_gelu_done")
        h_hi_ready = sem("f_h_hi_ready")
        h_lo_ready = sem("f_h_lo_ready")
        down_ready = sem("f_down_ready")
        res_step = sem("f_res_step")
        lns = LnSems(sem, "f")
        UP, DOWN, TURN = 0, 4, 6
        block = ctx.enter_context(nc.Block())

        @block.sync
        def _(sync):
            def load_x(c, par):
                here = c * 4 if isinstance(c, int) else nc.sync.snap(c * 4)
                if not isinstance(c, int):
                    sync.wait_ge(x_turned, c - 1)
                sync.dma_start(x_chunk[par][:, :, :], XN[:, bass.ds(here, 4), :]).then_inc(x_loaded[par], 16)

            load_x(0, 0)
            load_x(1, 1)
            sync.dma_start(w1_sb[:, :, :], w1).then_inc(w1_loaded, 16)
            sync.dma_start(w2_sb[:, :, :], w2).then_inc(w2_loaded, 16)
            for dst, src in ((b1_sb, b1), (b2_sb, b2_all.partition_broadcast(128))):
                sync.dma_start(dst[:, :], src).then_inc(w2_loaded, 16)
            with nc.sync.Fori(1, NCH // 2) as j:
                load_x(j * 2, 0)
                load_x(j * 2 + 1, 1)

        @block.tensor
        def _(pe):
            def up(c, par, first=False):
                pe.wait_ge(x_lo_ready, c + 1)
                for m in range(MT):
                    if not (first and m < 4):
                        pe.wait_ge(gelu_done, c * MT + m - 3)
                    for part in (x_hi, x_lo):
                        for k in range(2):
                            last = nc.tensor.matmul(P[:, UP + m % 4, :], w1_sign[:, k, m * 128:(m + 1) * 128],
                                                    part[par][:, k, :], start=(part is x_hi and k == 0),
                                                    stop=(part is x_lo and k == 1))
                    last.then_inc(up_ready, 1)

            def down(c, par, first):
                if first:
                    pe.wait_ge(alpha2_ready, 1)
                else:
                    pe.wait_ge(res_step, c * 3 - 2)
                for t in range(4):
                    for part, ready in ((h_hi, h_hi_ready), (h_lo, h_lo_ready)):
                        for k in range(MT):
                            if t == 0:
                                pe.wait_ge(ready, c * MT + k + 1)
                            last = nc.tensor.matmul(P[:, DOWN + t // 2, (t % 2) * D:(t % 2) * D + D],
                                                    part[par][:, k, t * 128:(t + 1) * 128], w2_sign[:, k, :],
                                                    start=(part is h_hi and k == 0),
                                                    stop=(part is h_lo and k == MT - 1))
                last.then_inc(down_ready, 1)

            def turn_x(c, par):
                if not isinstance(c, int) or c > 2:
                    pe.wait_ge(lns.stored, c - 2)
                if not isinstance(c, int) or c > 0:
                    pe.wait_ge(x_kept, c)
                pe.wait_ge(x_loaded[par], (c - par + 2) * 8)
                for k in range(2):
                    for t in range(4):
                        last = nc.tensor.transpose(P[:, TURN + k, t * 128:(t + 1) * 128],
                                                   x_chunk[par][:, t, k * 128:(k + 1) * 128], ident[:, :])
                last.then_inc(x_turned, 1)

            def step(c, par, first=False, last=False, more=True):
                if not last:
                    up(c + 1, 1 - par)
                if more:
                    turn_x(c + 2, par)
                down(c, par, first)
                if not first:
                    pe.wait_ge(x_kept, c + 3 if more else NCH)
                    ln_pe(nc, pe, ln, lns, P, TURN, ident, c - 1)

            turn_x(0, 0)
            turn_x(1, 1)
            pe.wait_ge(ones_ready, 1)
            pe.wait_ge(abs_ready, 1)
            for m in range(MT):
                for k in range(2):
                    nc.tensor.matmul(P[:, DOWN + 1, 2 * m:2 * m + 2], w1_abs[:, k, m * 128:(m + 1) * 128], ones[:, 0:2],
                                     start=(k == 0), stop=(k == 1))
            pe.wait_ge(abs_ready, 2)
            for k in range(MT):
                last = nc.tensor.matmul(P[:, DOWN, 0:D], ones[:, :], w2_abs[:, k, :], start=(k == 0), stop=(k == MT - 1))
            last.then_inc(means_summed, 1)
            pe.wait_ge(signs_ready, 2)
            up(0, 0, True)
            step(0, 0, first=True)
            step(1, 1)
            with nc.tensor.Fori(1, NCH // 2 - 1) as j:
                step(j * 2, 0)
                step(j * 2 + 1, 1)
            step(NCH - 2, 0, more=False)
            step(NCH - 1, 1, last=True, more=False)
            ln_pe(nc, pe, ln, lns, P, TURN, ident, NCH - 1)

        @block.scalar
        def _(act):
            def x_high(c, par):
                if not isinstance(c, int) or c > 1:
                    act.wait_ge(up_ready, (c - 1) * MT)
                act.wait_ge(x_turned, c + 1)
                nc.scalar.copy(spare[:, 0:1], ident[:, 0:1])
                nc.scalar.copy(XT[:, :, bass.ds(c * CH, CH)], P[:, TURN:TURN + 2, :]).then_inc(x_kept, 1)
                act.wait_ge(x_kept, c + 1)
                nc.scalar.copy(spare[:, 1:2], ident[:, 0:1])
                nc.scalar.copy(x_hi[par][:, :, :], XT[:, :, bass.ds(c * CH, CH)]).then_inc(x_hi_ready, 1)

            def gelus(c, par, fresh=False):
                for m in range(MT):
                    n = c * MT + m
                    act.wait_ge(up_ready, n + 1)
                    if fresh and isinstance(n, int) and n < 4:
                        pass
                    else:
                        act.wait_ge(h_lo_ready, n - 3)
                    nc.scalar.activation(h[:, m % 4, :], P[:, UP + m % 4, :], ACT.Gelu, bias=b1_sb[:, m:m + 1],
                                         scale=alpha1[:, m:m + 1]).then_inc(gelu_done, 1)
                    act.wait_ge(gelu_done, n + 1)
                    if m == 0 and not fresh:
                        act.wait_ge(down_ready, c - 1)
                    nc.scalar.copy(h_hi[par][:, m, :], h[:, m % 4, :]).then_inc(h_hi_ready, 1)

            def step(c, par, first=False, last=False, turn=True, more=True):
                if not last:
                    gelus(c + 1, 1 - par, first)
                if more:
                    x_high(c + 2, par)
                if turn:
                    ln_act(nc, act, ln, lns, P, TURN, XN, XT, c - 1)

            x_high(0, 0)
            x_high(1, 1)
            act.wait_ge(w1_loaded, 16)
            nc.scalar.sign(w1_sign[:, :, :], w1_sb[:, :, :]).then_inc(signs_ready, 1)
            act.wait_ge(w2_loaded, 48)
            nc.scalar.sign(w2_sign[:, :, :], w2_sb[:, :, :]).then_inc(signs_ready, 1)
            act.wait_ge(means_summed, 1)
            nc.scalar.mul(alpha2[:, :], P[:, DOWN, 0:D], 1.0 / 1024).then_inc(alpha2_ready, 1)
            act.wait_ge(alpha1_ready, 1)
            gelus(0, 0, True)
            step(0, 0, first=True, turn=False)
            step(1, 1)
            with nc.scalar.Fori(1, NCH // 2 - 1) as j:
                step(j * 2, 0)
                step(j * 2 + 1, 1)
            step(NCH - 2, 0, more=False)
            step(NCH - 1, 1, last=True, more=False)
            ln_act(nc, act, ln, lns, P, TURN, XN, XT, NCH - 1)

        @block.gpsimd
        def _(pool):
            def x_low(c, par):
                here = c * CH if isinstance(c, int) else nc.gpsimd.snap(c * CH)
                pool.wait_ge(x_hi_ready, c + 1)
                nc.gpsimd.tensor_tensor(x_lo[par][:, :, :], XT[:, :, bass.ds(here, CH)], x_hi[par][:, :, :],
                                        ALU.subtract).then_inc(x_lo_ready, 1)

            def lows(c, par):
                for m in range(MT):
                    pool.wait_ge(h_hi_ready, c * MT + m + 1)
                    nc.gpsimd.tensor_tensor(h_lo[par][:, m, :], h[:, m % 4, :], h_hi[par][:, m, :],
                                            ALU.subtract).then_inc(h_lo_ready, 1)

            def step(c, par, last=False, turn=True, more=True):
                if not last:
                    lows(c + 1, 1 - par)
                if turn:
                    ln_pool(nc, pool, ln, lns, c - 1)
                if more:
                    x_low(c + 2, par)

            x_low(0, 0)
            x_low(1, 1)
            pool.wait_ge(lns.half, 1)
            lows(0, 0)
            step(0, 0, turn=False)
            step(1, 1)
            with nc.gpsimd.Fori(1, NCH // 2 - 1) as j:
                step(j * 2, 0)
                step(j * 2 + 1, 1)
            step(NCH - 2, 0, more=False)
            step(NCH - 1, 1, last=True, more=False)
            ln_pool(nc, pool, ln, lns, NCH - 1)

        @block.vector
        def _(dve):
            ln_start(nc, ln, lns)
            nc.vector.memset(ones[:, :], 1.0).then_inc(ones_ready, 1)
            dve.wait_ge(w1_loaded, 16)
            nc.vector.scalar_tensor_tensor(w1_abs, w1_sb[:, :, :], -1.0, w1_sb[:, :, :], ALU.mult, ALU.max).then_inc(abs_ready, 1)
            dve.wait_ge(w2_loaded, 48)
            nc.vector.scalar_tensor_tensor(w2_abs[:, :, :], w2_sb[:, :, :], -1.0, w2_sb[:, :, :], ALU.mult, ALU.max).then_inc(abs_ready, 1)
            dve.wait_ge(means_summed, 1)
            nc.vector.tensor_scalar(alpha1[:, :], P[:, DOWN + 1, 0:2 * MT].rearrange("p (m two) -> p m two", two=2)[:, :, 0],
                                    1.0 / D, None, ALU.mult).then_inc(alpha1_ready, 1)
            dve.wait_ge(alpha2_ready, 1)
            with nc.vector.Fori(0, NCH) as c:
                dve.wait_ge(down_ready, c + 1)
                dve.wait_ge(lns.done, (c + 1) * 4)
                nc.vector.tensor_tensor(ln.res[:, :, :], two_banks(P, DOWN), over_tiles(alpha2),
                                        ALU.mult).then_inc(res_step, 1)
                dve.wait_ge(res_step, c * 3 + 1)
                nc.vector.tensor_tensor(ln.res[:, :, :], ln.res[:, :, :], over_tiles(b2_sb), ALU.add).then_inc(res_step, 1)
                dve.wait_ge(res_step, c * 3 + 2)
                nc.vector.tensor_tensor(ln.res[:, :, :], ln.res[:, :, :], XN[:, bass.ds(c * 4, 4), :],
                                        ALU.add).then_inc(res_step, 1)
                dve.wait_ge(res_step, c * 3 + 3)
                ln_dve(nc, dve, ln, lns, c)


def attn_phase(nc, XN, XT, P, ident, wq, wk, wv, wo, bo, masks):
    HG = 8
    HD = 16
    QT = SEQ // 128
    SLOTS_Q = (0, 0, 1, 1, 0, 2)
    SLOTS_K = (0, 1, 0, 1, 2, 0)
    ROWS = 6 * HD
    WIN = 64

    MAX_GLOBAL = [(i, 0, min((i + 1) * 128, CH)) for i in range(4)]
    for i in range(4, QT):
        MAX_GLOBAL += [(i, 0, CH), (i, CH, (i + 1) * 128 - CH)]
    MAX_LOCAL = QT // 2
    MAX_ITEMS = HG * (len(MAX_GLOBAL) + MAX_LOCAL)
    EXP_GLOBAL = [[(0, 0, 0), (1, 0, CH)], [(2, 0, 0), (3, 0, 256)],
                  [(0, 1, 0), (1, 1, CH)], [(2, 1, 0), (3, 1, CH)],
                  [(4, 1, 0), (5, 1, CH)], [(6, 1, 0), (7, 1, 256)]]
    EXP_LOCAL = 2
    GROUPS = HG * (len(EXP_GLOBAL) + EXP_LOCAL)

    def queries(j, chunk):
        first = max(j * 128, chunk * CH)
        return first, (chunk + 1) * CH - first

    ctx = ExitStack()
    with ctx:
        def sb(name, shape, dt=FP32):
            return ctx.enter_context(nc.sbuf_tensor(name, shape, dt))

        def sem(name):
            return ctx.enter_context(nc.semaphore(name))

        wq_sb = sb("a_wq_sb", [128, 2, D])
        wk_sb = sb("a_wk_sb", [128, 2, D])
        wv_sb = sb("a_wv_sb", [128, 2, D])
        wo_sb = sb("a_wo_sb", [128, 4, D])
        bo_sb = sb("a_bo_sb", [128, D])
        mask_in = sb("a_mask_in", [128, 5, 192])
        mask = sb("a_mask", [128, 5, 192], BF16)
        eye = sb("a_eye", [128, 128], BF16)
        zeros = sb("a_zeros", [128, CH], BF16)
        xTb = sb("a_xTb", [128, 2, SEQ])
        rest = [sb(f"a_rest{i}", [128, CH]) for i in range(2)]
        parts = [sb(f"a_parts{i}", [128, 3, SEQ], BF16) for i in range(2)]
        qs = sb("a_qs", [128, HG, SEQ], BF16)
        ks = sb("a_ks", [128, HG, SEQ], BF16)
        v_sb = sb("a_v_sb", [128, QT, D])
        vpad = [sb(f"a_vpad{i}", [128, QT, 4, 128]) for i in range(2)]
        pT = [sb(f"a_pT{i}", [128, 2 * CH]) for i in range(2)]
        mx = sb("a_mx", [128, 2 * HG, QT])
        ones = sb("a_ones", [128, QT, HD])
        spare = sb("a_spare", [128, 2])
        mx2 = sb("a_mx2", [128, HG, 4, 2])
        mrest = sb("a_mrest", [64, 128])
        mparts = sb("a_mparts", [64, 3, 128], BF16)
        oT = sb("a_oT", [128, 4, SEQ])
        den = sb("a_den", [128, CH])
        ln = LnTiles(sb, "a", pT[0][:, :].rearrange("p (t d) -> p t d", d=D),
                     pT[1][:, :].rearrange("p (t d) -> p t d", d=D))
        scratch = nc.dram_tensor("a_scratch", [2, 128, 3, SEQ], BF16, kind="Internal").ap()

        loaded = sem("a_loaded")
        const_dve = sem("a_const_dve")
        const_pool = sem("a_const_pool")
        mask_ready = sem("a_mask_ready")
        x_loaded = sem("a_x_loaded")
        v_ready = sem("a_v_ready")
        v_kept = sem("a_v_kept")
        qk_ready = sem("a_qk_ready")
        hi_ready = sem("a_hi_ready")
        rest_ready = sem("a_rest_ready")
        mid_ready = sem("a_mid_ready")
        lo_ready = sem("a_lo_ready")
        parts_out = sem("a_parts_out")
        stacked = sem("a_stacked")
        s1_ready = sem("a_s1_ready")
        max_done = sem("a_max_done")
        mx_ready = sem("a_mx_ready")
        mx_turned = sem("a_mx_turned")
        mhi_ready = sem("a_mhi_ready")
        mrest_ready = sem("a_mrest_ready")
        mmid_ready = sem("a_mmid_ready")
        mlo_ready = sem("a_mlo_ready")
        m_stacked = sem("a_m_stacked")
        vpad_ready = sem("a_vpad_ready")
        s2_ready = sem("a_s2_ready")
        p_ready = sem("a_p_ready")
        pv_done = sem("a_pv_done")
        sum_ready = sem("a_sum_ready")
        den_step = sem("a_den_step")
        o_ready = sem("a_o_ready")
        out_ready = sem("a_out_ready")
        res_step = sem("a_res_step")
        lns = LnSems(sem, "a")
        block = ctx.enter_context(nc.Block())

        def max_base(b, hg):
            return b * MAX_ITEMS + hg * HG * len(MAX_GLOBAL)

        def group_base(b, hg):
            return b * GROUPS + hg * HG * len(EXP_GLOBAL)

        @block.sync
        def _(sync):
            for dst, src in ((wq_sb, wq), (wk_sb, wk), (wv_sb, wv), (wo_sb, wo), (mask_in, masks)):
                sync.dma_start(dst[:, :, :], src).then_inc(loaded, 16)
            sync.dma_start(bo_sb[:, :], bo.partition_broadcast(128)).then_inc(loaded, 16)
            with nc.sync.Fori(0, NB) as b:
                first_token = nc.sync.snap(b * SEQ)
                sync.wait_ge(lns.stored, b * 2 + 1)
                sync.dma_start(xTb[:, :, :], XT[:, :, bass.ds(first_token, SEQ)]).then_inc(x_loaded, 16)
                for hg in range(2):
                    if hg:
                        sync.wait_ge(pv_done, group_base(b, 1))
                    sync.wait_ge(lo_ready, (b * 2 + hg) * 4 + 4)
                    for i in range(2):
                        sync.dma_start(scratch[i], parts[i][:, :, :]).then_inc(parts_out, 16)
                    sync.wait_ge(parts_out, (b * 2 + hg + 1) * 32)
                    for i, (stack, slots) in enumerate(((qs, SLOTS_Q), (ks, SLOTS_K))):
                        for s in range(6):
                            src = scratch[i].rearrange("(h d) p t -> d p h t", d=HD)[:, slots[s]]
                            sync.dma_start(stack[s * HD:(s + 1) * HD, :, :], src).then_inc(stacked, 16)
                    sync.wait_ge(mlo_ready, b * 2 + hg + 1)
                    for p in range(3):
                        sync.dma_start(qs[ROWS + p:ROWS + p + 1, :, :], mparts[:, p, :]).then_inc(m_stacked, 16)

        @block.tensor
        def _(pe):
            pe.wait_ge(loaded, 16 * 6)
            pe.wait_ge(const_dve, 2)
            pe.wait_ge(const_pool, 3)
            pe.wait_ge(mask_ready, 2)
            with nc.tensor.Fori(0, NB) as b:
                pe.wait_ge(x_loaded, (b + 1) * 16)
                pe.wait_ge(lns.stored, b * 2 + 1)
                for t in range(QT):
                    for k in range(2):
                        last = nc.tensor.matmul(P[:, t // 2, (t % 2) * D:(t % 2) * D + D],
                                                xTb[:, k, t * 128:(t + 1) * 128], wv_sb[:, k, :],
                                                start=(k == 0), stop=(k == 1))
                    if t % 2:
                        last.then_inc(v_ready, 1)
                for hg in range(2):
                    if hg:
                        pe.wait_ge(o_ready, b * 8 + 4)
                    for s in range(4):
                        w, half = (wq_sb, wk_sb)[s // 2], s % 2
                        for k in range(2):
                            last = nc.tensor.matmul(P[:, 4 + s, :], w[:, k, hg * 128:(hg + 1) * 128],
                                                    xTb[:, k, half * CH:(half + 1) * CH], start=(k == 0), stop=(k == 1))
                        last.then_inc(qk_ready, 1)

                    pe.wait_ge(stacked, (b * 2 + hg + 1) * 16 * 12)
                    if hg == 0:
                        pe.wait_ge(v_kept, b * 4 + 4)
                    else:
                        pe.wait_ge(p_ready, group_base(b, 1))
                    nc.tensor.matmul(P[:, 0, 0:128], zeros[:, 0:128], zeros[:, 0:128], start=True, stop=True)
                    with nc.tensor.Fori(0, HG) as h:
                        if hg == 0:
                            for n, (i, first, keys) in enumerate(MAX_GLOBAL):
                                at = max_base(b, 0) + h * len(MAX_GLOBAL) + n
                                pe.wait_ge(max_done, at + 1)
                                diagonal = first + keys == (i + 1) * 128
                                last = nc.tensor.matmul(P[:, n % 4, 0:keys], qs[0:ROWS, h, i * 128:(i + 1) * 128],
                                                        ks[0:ROWS, h, first:first + keys], start=True, stop=not diagonal)
                                if diagonal:
                                    last = nc.tensor.matmul(P[:, n % 4, keys - 128:keys], eye[:, :], mask[:, 0, 0:128],
                                                            start=False, stop=True)
                                last.then_inc(s1_ready, 1)
                        else:
                            for n in range(MAX_LOCAL):
                                at = max_base(b, 1) + h * MAX_LOCAL + n
                                pe.wait_ge(max_done, at + 1)
                                for i in (2 * n, 2 * n + 1):
                                    col = (i % 2) * 192
                                    cut = WIN if i == 0 else 0
                                    nc.tensor.matmul(P[:, n % 4, col:col + 192], eye[:, :], mask[:, 2 if i == 0 else 1, :],
                                                     start=True, stop=False)
                                    last = nc.tensor.matmul(P[:, n % 4, col + cut:col + 192],
                                                            qs[0:ROWS, h, i * 128:(i + 1) * 128],
                                                            ks[0:ROWS, h, i * 128 - WIN + cut:(i + 1) * 128],
                                                            start=False, stop=True)
                                last.then_inc(s1_ready, 1)

                    pe.wait_ge(mx_ready, (b * 2 + hg + 1) * 1)
                    nc.tensor.transpose(P[:, 4, 0:128], mx[:, :, :].rearrange("p h i -> p (h i)"),
                                        ident[:, :]).then_inc(mx_turned, 1)

                    pe.wait_ge(m_stacked, (b * 2 + hg + 1) * 48)
                    for quad in range(2):
                        acc = 4 + 2 * quad
                        pe.wait_ge(vpad_ready, (b * 2 + hg) * 2 + quad + 1)
                        for chunk in range(2):
                            nc.tensor.matmul(P[:, acc + chunk, :], zeros[:, 0:128], zeros[:, :], start=True, stop=False)
                        n_groups = len(EXP_GLOBAL) if hg == 0 else EXP_LOCAL
                        base = group_base(b, hg) + quad * 4 * n_groups

                        def scores2(n):
                            hh, g = divmod(n, n_groups)
                            h, slot = quad * 4 + hh, 2 * (n % 2)
                            if not (quad == 0 and n < 2):
                                pe.wait_ge(p_ready, base + n - 1)
                            if hg == 0:
                                for j, chunk, col in EXP_GLOBAL[g]:
                                    first, count = queries(j, chunk)
                                    diagonal = first == j * 128
                                    out = P[:, slot + col // CH, col % CH:col % CH + count]
                                    last = nc.tensor.matmul(out, ks[0:ROWS + 3, h, j * 128:(j + 1) * 128],
                                                            qs[0:ROWS + 3, h, first:first + count],
                                                            start=True, stop=not diagonal)
                                    if diagonal:
                                        last = nc.tensor.matmul(out[:, 0:128], eye[:, :], mask[:, 3, 0:128],
                                                                start=False, stop=True)
                            else:
                                for j in range(4 * g, 4 * g + 4):
                                    count = min(192, SEQ - j * 128)
                                    at = (j % 2) * 192
                                    bank = slot + (j % 4) // 2
                                    nc.tensor.matmul(P[:, bank, at:at + 192], eye[:, :], mask[:, 4, :],
                                                     start=True, stop=False)
                                    last = nc.tensor.matmul(P[:, bank, at:at + count],
                                                            ks[0:ROWS + 3, h, j * 128:(j + 1) * 128],
                                                            qs[0:ROWS + 3, h, j * 128:j * 128 + count],
                                                            start=False, stop=True)
                            last.then_inc(s2_ready, 1)

                        def values(n):
                            hh, g = divmod(n, n_groups)
                            p = pT[n % 2]
                            pe.wait_ge(p_ready, base + n + 1)
                            final = n == 4 * n_groups - 1
                            if hg == 0:
                                items = [(j, chunk, queries(j, chunk)[0] - chunk * CH, col, queries(j, chunk)[1])
                                         for j, chunk, col in EXP_GLOBAL[g]]
                            else:
                                items = []
                                for j in range(4 * g, 4 * g + 4):
                                    at = ((j % 4) // 2) * CH + (j % 2) * 192
                                    for chunk in range(2):
                                        lo = max(j * 128, chunk * CH)
                                        hi = min(j * 128 + 192, (chunk + 1) * CH)
                                        if lo < hi:
                                            items.append((j, chunk, lo - chunk * CH, at + lo - j * 128, hi - lo))
                            for n_item, (j, chunk, dst, col, count) in enumerate(items):
                                last = nc.tensor.matmul(P[:, acc + chunk, dst:dst + count],
                                                        vpad[quad][:, j, hh, :], p[:, col:col + count], start=False,
                                                        stop=False)
                            last.then_inc(pv_done, 1)

                        scores2(0)
                        for n in range(4 * n_groups):
                            if n + 1 < 4 * n_groups:
                                scores2(n + 1)
                            values(n)
                        for chunk in range(2):
                            nc.tensor.matmul(P[:, acc + chunk, :], zeros[:, 0:128], zeros[:, :], start=False,
                                             stop=True).then_inc(sum_ready, 1)
                for half in range(2):
                    pe.wait_ge(o_ready, (b + 1) * 8)
                    for t in range(4):
                        for quad in range(4):
                            last = nc.tensor.matmul(P[:, 4 + 2 * half + t // 2, (t % 2) * D:(t % 2) * D + D],
                                                    oT[:, quad, half * CH + t * 128:half * CH + (t + 1) * 128],
                                                    wo_sb[:, quad, :], start=(quad == 0), stop=(quad == 3))
                    last.then_inc(out_ready, 1)
                for half in range(2):
                    ln_pe(nc, pe, ln, lns, P, 2 * half, ident, b * 2 + half)

        @block.scalar
        def _(act):
            act.wait_ge(loaded, 16 * 6)
            nc.scalar.copy(mask[:, :, :], mask_in[:, :, :]).then_inc(mask_ready, 1)
            nc.scalar.copy(eye[:, :], ident[:, :]).then_inc(mask_ready, 1)
            with nc.scalar.Fori(0, NB) as b:
                for t in range(4):
                    act.wait_ge(v_ready, b * 4 + t + 1)
                    nc.scalar.copy(v_sb[:, 2 * t:2 * t + 2, :],
                                   P[:, t, :].rearrange("p (t d) -> p t d", d=D)).then_inc(v_kept, 1)
                for hg in range(2):
                    for s in range(4):
                        act.wait_ge(qk_ready, (b * 2 + hg) * 4 + s + 1)
                        if hg and s == 0:
                            act.wait_ge(parts_out, (b * 2 + hg) * 32)
                        nc.scalar.activation(parts[s // 2][:, 0, (s % 2) * CH:(s % 2 + 1) * CH], P[:, 4 + s, :],
                                             ACT.Copy, scale=0.25 if s < 2 else 1.0).then_inc(hi_ready, 1)
                    for s in range(4):
                        act.wait_ge(rest_ready, (b * 2 + hg) * 4 + s + 1)
                        nc.scalar.copy(parts[s // 2][:, 1, (s % 2) * CH:(s % 2 + 1) * CH],
                                       rest[s % 2][:, :]).then_inc(mid_ready, 1)
                    act.wait_ge(mx_turned, b * 2 + hg + 1)
                    nc.scalar.activation(mparts[:, 0, :], P[0:HG * QT, 4, 0:128], ACT.Copy,
                                         scale=-1.0).then_inc(mhi_ready, 1)
                    act.wait_ge(mrest_ready, b * 2 + hg + 1)
                    nc.scalar.copy(mparts[:, 1, :], mrest[:, :]).then_inc(mmid_ready, 1)
                    for quad in range(2):
                        n_groups = len(EXP_GLOBAL) if hg == 0 else EXP_LOCAL
                        base = group_base(b, hg) + quad * 4 * n_groups
                        for n in range(4 * n_groups):
                            g, slot, p = n % n_groups, 2 * (n % 2), pT[n % 2]
                            act.wait_ge(s2_ready, base + n + 1)
                            if not (quad == 0 and n < 2):
                                act.wait_ge(pv_done, base + n - 1)
                            if hg == 0:
                                count = sum(queries(j, chunk)[1] for j, chunk, _ in EXP_GLOBAL[g])
                                src, dst = P[:, slot:slot + 2, :].rearrange("p a n -> p (a n)")[:, 0:count], p[:, 0:count]
                            else:
                                src = P[:, slot:slot + 2, 0:384]
                                dst = p[:, :].rearrange("p (a n) -> p a n", n=CH)[:, :, 0:384]
                            nc.scalar.activation(dst, src, ACT.Exp).then_inc(p_ready, 1)
                for half in range(2):
                    ln_act(nc, act, ln, lns, P, 2 * half, XN, XT, b * 2 + half)

        @block.gpsimd
        def _(pool):
            nc.gpsimd.memset(ones[:, :, :], 1.0)
            nc.gpsimd.memset(vpad[0][:, :, :, :], 0.0).then_inc(const_pool, 1)
            nc.gpsimd.memset(vpad[1][:, :, :, :], 0.0).then_inc(const_pool, 1)
            pool.wait_ge(const_pool, 2)
            for i in range(2):
                for hh in range(4):
                    last = nc.gpsimd.memset(vpad[i][:, :, hh, hh * 32 + HD:hh * 32 + 32], 1.0)
            last.then_inc(const_pool, 1)
            pool.wait_ge(const_pool, 3)
            pool.wait_ge(lns.half, 1)
            with nc.gpsimd.Fori(0, NB) as b:
                for hg in range(2):
                    for s in range(4):
                        cols = slice((s % 2) * CH, (s % 2 + 1) * CH)
                        pool.wait_ge(mid_ready, (b * 2 + hg) * 4 + s + 1)
                        nc.gpsimd.tensor_tensor(parts[s // 2][:, 2, cols], rest[s % 2][:, :], parts[s // 2][:, 1, cols],
                                                ALU.subtract).then_inc(lo_ready, 1)
                    pool.wait_ge(v_kept, b * 4 + 4)
                    if hg:
                        pool.wait_ge(pv_done, group_base(b, 1))
                    for quad in range(2):
                        for hh in range(4):
                            f = (hg * 2 + quad) * 64 + hh * HD
                            last = nc.gpsimd.tensor_tensor(vpad[quad][:, :, hh, hh * 32:hh * 32 + HD],
                                                           v_sb[:, :, f:f + HD], ones[:, :, :], ALU.mult)
                        last.then_inc(vpad_ready, 1)
                    pool.wait_ge(mmid_ready, b * 2 + hg + 1)
                    nc.gpsimd.tensor_tensor(mparts[:, 2, :], mrest[:, :], mparts[:, 1, :],
                                            ALU.subtract).then_inc(mlo_ready, 1)
                for half in range(2):
                    ln_pool(nc, pool, ln, lns, b * 2 + half)

        @block.vector
        def _(dve):
            ln_start(nc, ln, lns)
            nc.vector.memset(mrest[:, :], 0.0).then_inc(max_done, 4)
            nc.vector.memset(mx[:, :, :], 0.0)
            nc.vector.memset(ks[ROWS:ROWS + 3, :, :], 1.0).then_inc(const_dve, 1)
            nc.vector.memset(zeros[:, :], 0.0).then_inc(const_dve, 1)
            dve.wait_ge(const_dve, 2)
            with nc.vector.Fori(0, NB) as b:
                for hg in range(2):
                    for s in range(4):
                        cols = slice((s % 2) * CH, (s % 2 + 1) * CH)
                        dve.wait_ge(hi_ready, (b * 2 + hg) * 4 + s + 1)
                        if s >= 2:
                            dve.wait_ge(lo_ready, (b * 2 + hg) * 4 + s - 1)
                        nc.vector.scalar_tensor_tensor(rest[s % 2][:, :], P[:, 4 + s, :], 0.25 if s < 2 else 1.0,
                                                       parts[s // 2][:, 0, cols], ALU.mult,
                                                       ALU.subtract).then_inc(rest_ready, 1)
                    with nc.vector.Fori(0, HG) as h:
                        if hg == 0:
                            for n, (i, first, keys) in enumerate(MAX_GLOBAL):
                                at = max_base(b, 0) + h * len(MAX_GLOBAL) + n
                                dve.wait_ge(s1_ready, at + 1)
                                dst = mx[:, h, i:i + 1] if i < 4 else mx2[:, h, i - 4, first // CH:first // CH + 1]
                                nc.vector.tensor_reduce(dst, P[:, n % 4, 0:keys], axis=AX.X,
                                                        op=ALU.max).then_inc(max_done, 1)
                        else:
                            for n in range(MAX_LOCAL):
                                at = max_base(b, 1) + h * MAX_LOCAL + n
                                dve.wait_ge(s1_ready, at + 1)
                                nc.vector.tensor_reduce(mx[:, h, 2 * n:2 * n + 2],
                                                        P[:, n % 4, 0:384].rearrange("p (a k) -> p a k", a=2),
                                                        axis=AX.X, op=ALU.max).then_inc(max_done, 1)
                    dve.wait_ge(max_done, max_base(b, hg + 1) + 4 if hg == 0 else (b + 1) * MAX_ITEMS + 4)
                    if hg == 0:
                        nc.vector.tensor_reduce(mx[:, 0:HG, 4:8], mx2[:, :, :, :], axis=AX.X, op=ALU.max).then_inc(mx_ready, 1)
                    else:
                        nc.vector.memset(den[:, 0:1], 0.0).then_inc(mx_ready, 1)
                    dve.wait_ge(mhi_ready, b * 2 + hg + 1)
                    nc.vector.scalar_tensor_tensor(mrest[:, :], P[0:HG * QT, 4, 0:128], -1.0, mparts[:, 0, :],
                                                   ALU.mult, ALU.subtract).then_inc(mrest_ready, 1)
                    for quad in range(2):
                        for chunk in range(2):
                            n = ((b * 2 + hg) * 2 + quad) * 2 + chunk
                            acc = P[:, 4 + 2 * quad + chunk, :]
                            dve.wait_ge(sum_ready, n + 1)
                            nc.vector.memset(spare[:, chunk:chunk + 1], 0.0)
                            nc.vector.stream_shuffle(den[:, :], acc, [16 + r % 16 for r in range(32)]).then_inc(den_step, 1)
                            dve.wait_ge(den_step, n * 2 + 1)
                            nc.vector.reciprocal(den[:, :], den[:, :]).then_inc(den_step, 1)
                            dve.wait_ge(den_step, n * 2 + 2)
                            nc.vector.tensor_tensor(oT[:, hg * 2 + quad, chunk * CH:(chunk + 1) * CH], acc, den[:, :],
                                                    ALU.mult).then_inc(o_ready, 1)
                            dve.wait_ge(o_ready, n + 1)
                for half in range(2):
                    c = b * 2 + half
                    dve.wait_ge(out_ready, c + 1)
                    dve.wait_ge(lns.done, (c + 1) * 4)
                    nc.vector.tensor_tensor(ln.res[:, :, :], two_banks(P, 4 + 2 * half), over_tiles(bo_sb),
                                            ALU.add).then_inc(res_step, 1)
                    dve.wait_ge(res_step, c * 2 + 1)
                    nc.vector.tensor_tensor(ln.res[:, :, :], ln.res[:, :, :], XN[:, bass.ds(c * 4, 4), :],
                                            ALU.add).then_inc(res_step, 1)
                    dve.wait_ge(res_step, c * 2 + 2)
                    ln_dve(nc, dve, ln, lns, c)



def moe_phase(nc, XN, XT, P, ident, router_w, router_b, w, b1, b2, pads, out):
    NE = 16
    NT = TOK // 128
    ctx = ExitStack()
    with ctx:
        def sb(name, shape, dt=FP32):
            return ctx.enter_context(nc.sbuf_tensor(name, shape, dt))

        def sem(name):
            return ctx.enter_context(nc.semaphore(name))

        rw_sb = sb("e_rw", [128, 2, 16])
        rb_sb = sb("e_rb", [16, 1])
        w_raw = sb("e_w_raw", [128, 4, D])
        w_hi = [sb(f"e_w_hi{i}", [128, 4, D], FP32R) for i in range(2)]
        w_lo = [sb(f"e_w_lo{i}", [128, 4, D], FP32R) for i in range(2)]
        x_hi = sb("e_x_hi", [128, 2, TOK], FP32R)
        x_lo = sb("e_x_lo", [128, 2, TOK], FP32R)
        b1_sb = [sb(f"e_b1_{i}", [128, 2]) for i in range(2)]
        b2_sb = sb("e_b2", [128, D])
        logT = [sb(f"e_logT{i}", [16, CH]) for i in range(2)]
        top = sb("e_top", [128, NT])
        expd = sb("e_expd", [128, NT, 15])
        total = sb("e_total", [128, NT])
        probs = sb("e_probs", [128, NT, 24])
        best = sb("e_best", [128, NT, 8])
        chosen = sb("e_chosen", [128, NT, 8])
        rest = sb("e_rest", [128, NT, 24])
        cw = sb("e_cw", [128, NT, 32])
        cwT = sb("e_cwT", [128, NCH, 128])
        hT = [sb(f"e_hT{i}", [128, 2, CH]) for i in range(2)]
        h_hi = [sb(f"e_h_hi{i}", [128, 2, CH], FP32R) for i in range(2)]
        h_lo = [sb(f"e_h_lo{i}", [128, 2, CH], FP32R) for i in range(2)]
        spare = sb("e_spare", [128, 12])
        ln = LnTiles(sb, "e", XT[:, 0, 0:1024].rearrange("p (t d) -> p t d", d=D),
                     XT[:, 0, 1024:2048].rearrange("p (t d) -> p t d", d=D))
        loaded = sem("e_loaded")
        w_loaded = sem("e_w_loaded")
        b1_loaded = [sem(f"e_b1_loaded{i}") for i in range(2)]
        w_hi_ready = sem("e_w_hi_ready")
        w_lo_ready = sem("e_w_lo_ready")
        x_hi_ready = sem("e_x_hi_ready")
        x_lo_ready = sem("e_x_lo_ready")
        const_ready = sem("e_const_ready")
        logits_ready = sem("e_logits_ready")
        logT_ready = sem("e_logT_ready")
        log_turned = sem("e_log_turned")
        route = sem("e_route")
        exp_ready = sem("e_exp_ready")
        cw_ready = sem("e_cw_ready")
        cw_turned = sem("e_cw_turned")
        cwT_ready = sem("e_cwT_ready")
        bias_ready = sem("e_bias_ready")
        bias_added = sem("e_bias_added")
        up_ready = sem("e_up_ready")
        relu_done = sem("e_relu_done")
        h_hi_ready = sem("e_h_hi_ready")
        h_lo_ready = sem("e_h_lo_ready")
        down_ready = sem("e_down_ready")
        added = sem("e_added")
        stored = sem("e_stored")
        lns = LnSems(sem, "e")
        ROUTER_LOADS = 16 * 5
        block = ctx.enter_context(nc.Block())

        @block.sync
        def _(sync):
            for dst, src in ((rw_sb[:, :, :], router_w), (rb_sb[:, :], router_b),
                             (b2_sb[:, :], b2), (probs[:, :, 15:24], pads[:, :, 0:9]),
                             (chosen[:, :, 3:8], pads[:, :, 0:5])):
                sync.dma_start(dst, src).then_inc(loaded, 16)
            for e in range(2):
                sync.dma_start(b1_sb[e][:, :], b1[e]).then_inc(b1_loaded[e], 16)
            sync.dma_start(w_raw[:, :, :], w[0]).then_inc(w_loaded, 16)
            sync.wait_ge(w_lo_ready, 1)
            sync.dma_start(w_raw[:, :, :], w[1]).then_inc(w_loaded, 16)
            with nc.sync.Fori(0, NE // 2 - 1) as pair:
                for i in range(2):
                    expert = nc.sync.snap(pair * 2 + (i + 2))
                    sync.wait_ge(w_lo_ready, pair * 2 + (i + 2))
                    sync.dma_start(w_raw[:, :, :], w[bass.ds(expert, 1)].rearrange("a p k d -> p (a k) d")).then_inc(w_loaded, 16)
                    sync.wait_ge(down_ready, (pair * 2 + i + 1) * NCH * 2 + 4)
                    sync.dma_start(b1_sb[i][:, :], b1[bass.ds(expert, 1)].rearrange("a p k -> p (a k)")).then_inc(b1_loaded[i], 16)
            with nc.sync.Fori(0, NCH) as c:
                first_tile = nc.sync.snap(c * 4)
                sync.wait_ge(lns.done, (c + 2) * 4)
                sync.dma_start(out[:, bass.ds(first_tile, 4), :], ln.nrm[:, :, :]).then_inc(stored, 16)
            sync.wait_ge(stored, 16 * (NCH + 1))

        @block.tensor
        def _(pe):
            pe.wait_ge(loaded, ROUTER_LOADS)
            pe.wait_ge(const_ready, 4)
            with nc.tensor.Fori(0, NCH // 2) as j:
                for p in range(2):
                    c = j * 2 + p
                    pe.wait_ge(logT_ready, c + 1)
                    for k in range(2):
                        last = nc.tensor.matmul(P[0:16, p, :], rw_sb[:, k, :], XT[:, k, bass.ds(c * CH, CH)],
                                                start=(k == 0), stop=(k == 1))
                    last.then_inc(logits_ready, 1)
                for p in range(2):
                    c = j * 2 + p
                    pe.wait_ge(logT_ready, c + 3)
                    for t in range(4):
                        last = nc.tensor.matmul(P[:, 2, bass.ds(c * 64 + t * 16, 16)], logT[p][:, t * 128:(t + 1) * 128],
                                                ident[0:16, 0:16], start=True, stop=True)
                    last.then_inc(log_turned, 1)
            pe.wait_ge(cw_ready, 1)
            for c in range(NCH):
                last = nc.tensor.transpose(P[:, c // 4, (c % 4) * 128:(c % 4 + 1) * 128],
                                           cw[:, 4 * c:4 * c + 4, :].rearrange("p t e -> p (t e)"), ident[:, :])
                if c % 4 == 3:
                    last.then_inc(cw_turned, 1)
            pe.wait_ge(cwT_ready, 2)
            for c in range(NCH):
                if c >= 2:
                    pe.wait_ge(bias_added, c - 1)
                for t in range(4):
                    last = nc.tensor.matmul(P[:, 4 - 4 * (c % 2) + t, 0:D], cwT[32 * t:32 * t + 16, c, :], b2_sb[32 * t:32 * t + 16, :],
                                            start=True, stop=True)
                last.then_inc(bias_ready, 1)

            def up(i, par, n, c):
                pe.wait_ge(relu_done, n * 2 + 2)
                for m in range(2):
                    cols = slice(m * 128, (m + 1) * 128)
                    for k in range(2):
                        here = bass.ds(c * CH, CH)
                        nc.tensor.matmul(P[:, 2 * par + m, :], w_hi[i][:, k, cols], x_hi[:, k, here],
                                         start=(k == 0), stop=False)
                        nc.tensor.matmul(P[:, 2 * par + m, :], w_hi[i][:, k, cols], x_lo[:, k, here],
                                         start=False, stop=False)
                        last = nc.tensor.matmul(P[:, 2 * par + m, :], w_lo[i][:, k, cols], x_hi[:, k, here],
                                                start=False, stop=(k == 1))
                    last.then_inc(up_ready, 1)

            def down(i, par, n):
                pe.wait_ge(added, n * 4 + 4)
                pe.wait_ge(h_hi_ready, n * 2 + 2)
                for t in range(4):
                    sums = P[:, 4 + 2 * par + t // 2, (t % 2) * D:(t % 2) * D + D]
                    cols = slice(t * 128, (t + 1) * 128)
                    for k in range(2):
                        nc.tensor.matmul(sums, h_hi[par][:, k, cols], w_hi[i][:, 2 + k, :], start=(k == 0), stop=False)
                        nc.tensor.matmul(sums, h_hi[par][:, k, cols], w_lo[i][:, 2 + k, :], start=False, stop=False)
                    for k in range(2):
                        if t == 0:
                            pe.wait_ge(h_lo_ready, n * 2 + k + 5)
                        last = nc.tensor.matmul(sums, h_lo[par][:, k, cols], w_hi[i][:, 2 + k, :],
                                                start=False, stop=(k == 1))
                    if t % 2:
                        last.then_inc(down_ready, 1)

            def expert(i, e, final):
                with nc.tensor.Fori(0, NCH // 2 - 1) as j:
                    up(i, 1, e * NCH + j * 2 + 1, j * 2 + 1)
                    down(i, 0, e * NCH + j * 2)
                    up(i, 0, e * NCH + j * 2 + 2, j * 2 + 2)
                    down(i, 1, e * NCH + j * 2 + 1)
                up(i, 1, e * NCH + NCH - 1, NCH - 1)
                down(i, 0, e * NCH + NCH - 2)
                if not final:
                    pe.wait_ge(w_lo_ready, e + 2)
                    up(1 - i, 0, e * NCH + NCH, 0)
                down(i, 1, e * NCH + NCH - 1)

            pe.wait_ge(bias_added, NCH)
            pe.wait_ge(x_lo_ready, NCH)
            pe.wait_ge(w_lo_ready, 1)
            up(0, 0, 0, 0)
            with nc.tensor.Fori(0, NE // 2 - 1) as pair:
                expert(0, pair * 2, False)
                expert(1, pair * 2 + 1, False)
            expert(0, NE - 2, False)
            expert(1, NE - 1, True)

        @block.scalar
        def _(act):
            act.wait_ge(loaded, ROUTER_LOADS)
            with nc.scalar.Fori(0, NCH // 2) as j:
                for p in range(2):
                    c = j * 2 + p
                    here = nc.scalar.snap(c * CH)
                    act.wait_ge(logits_ready, c + 1)
                    act.wait_ge(log_turned, c + 1)
                    nc.scalar.activation(logT[p][:, :], P[0:16, p, :], ACT.Identity,
                                         bias=rb_sb[:, 0:1]).then_inc(logT_ready, 1)
                    nc.scalar.copy(x_hi[:, :, bass.ds(here, CH)], XT[:, :, bass.ds(here, CH)]).then_inc(x_hi_ready, 1)

            def split(i, e):
                act.wait_ge(w_loaded, (e + 1) * 16)
                nc.scalar.copy(w_hi[i][:, :, :], w_raw[:, :, :]).then_inc(w_hi_ready, 1)

            split(0, 0)
            act.wait_ge(route, 2)
            nc.scalar.activation(expd[:, :, :], expd[:, :, :], ACT.Exp).then_inc(exp_ready, 1)
            for half in range(2):
                act.wait_ge(cw_turned, half + 1)
                nc.scalar.copy(cwT[:, 4 * half:4 * half + 4, :],
                               P[:, half, :].rearrange("p (c n) -> p c n", n=128)).then_inc(cwT_ready, 1)

            def relus(par, n, i):
                act.wait_ge(down_ready, n * 2 + 2)
                act.wait_ge(h_lo_ready, n * 2 + 2)
                for m in range(2):
                    act.wait_ge(up_ready, n * 2 + m + 1)
                    nc.scalar.activation(hT[par][:, m, :], P[:, 2 * par + m, :], ACT.Relu,
                                         bias=b1_sb[i][:, m:m + 1]).then_inc(relu_done, 1)
                    act.wait_ge(relu_done, n * 2 + m + 5)
                    nc.scalar.copy(h_hi[par][:, m, :], hT[par][:, m, :]).then_inc(h_hi_ready, 1)

            def passes(i, pair, final):
                e = pair * 2 + i
                act.wait_ge(b1_loaded[i], (pair + 1) * 16)
                relus(0, e * NCH, i)
                relus(1, e * NCH + 1, i)
                if not final:
                    split(1 - i, e + 1)
                with nc.scalar.Fori(1, NCH // 2) as j:
                    relus(0, e * NCH + j * 2, i)
                    relus(1, e * NCH + j * 2 + 1, i)

            with nc.scalar.Fori(0, NE // 2 - 1) as pair:
                passes(0, pair, False)
                passes(1, pair, False)
            passes(0, NE // 2 - 1, False)
            passes(1, NE // 2 - 1, True)

        @block.gpsimd
        def _(pool):
            with nc.gpsimd.Fori(0, NCH) as c:
                here = nc.gpsimd.snap(c * CH)
                pool.wait_ge(x_hi_ready, c + 1)
                nc.gpsimd.tensor_tensor(x_lo[:, :, bass.ds(here, CH)], XT[:, :, bass.ds(here, CH)],
                                        x_hi[:, :, bass.ds(here, CH)], ALU.subtract).then_inc(x_lo_ready, 1)

            def split(i, e):
                pool.wait_ge(w_hi_ready, e + 1)
                nc.gpsimd.tensor_tensor(w_lo[i][:, :, :], w_raw[:, :, :], w_hi[i][:, :, :],
                                        ALU.subtract).then_inc(w_lo_ready, 1)

            def low_parts(par, n):
                for m in range(2):
                    pool.wait_ge(h_hi_ready, n * 2 + m + 1)
                    nc.gpsimd.tensor_tensor(h_lo[par][:, m, :], hT[par][:, m, :], h_hi[par][:, m, :],
                                            ALU.subtract).then_inc(h_lo_ready, 1)

            def passes(i, pair):
                e = pair * 2 + i
                low_parts(0, e * NCH)
                low_parts(1, e * NCH + 1)
                split(1 - i, e + 1)
                with nc.gpsimd.Fori(1, NCH // 2) as j:
                    low_parts(0, e * NCH + j * 2)
                    low_parts(1, e * NCH + j * 2 + 1)

            split(0, 0)
            pool.wait_ge(const_ready, 4)
            pool.wait_ge(lns.half, 1)
            with nc.gpsimd.Fori(0, NE // 2 - 1) as pair:
                passes(0, pair)
                passes(1, pair)
            passes(0, NE // 2 - 1)
            base = (NE - 1) * NCH
            low_parts(0, base)
            with nc.gpsimd.Fori(0, NCH // 2 - 1) as j:
                low_parts(1, base + j * 2 + 1)
                ln_pool(nc, pool, ln, lns, j * 2)
                low_parts(0, base + j * 2 + 2)
                ln_pool(nc, pool, ln, lns, j * 2 + 1)
            low_parts(1, base + NCH - 1)
            ln_pool(nc, pool, ln, lns, NCH - 2)
            ln_pool(nc, pool, ln, lns, NCH - 1)

        @block.vector
        def _(dve):
            ln_start(nc, ln, lns)
            nc.vector.memset(spare[:, 7:8], 0.0).then_inc(stored, 16)
            nc.vector.memset(cw[:, :, :], 0.0).then_inc(const_ready, 1)
            nc.vector.memset(spare[:, 0:1], 0.0).then_inc(relu_done, 4)
            nc.vector.memset(spare[:, 1:2], 0.0).then_inc(down_ready, 4)
            nc.vector.memset(spare[:, 2:3], 0.0).then_inc(added, 8)
            nc.vector.memset(spare[:, 3:4], 0.0).then_inc(h_lo_ready, 4)
            nc.vector.memset(spare[:, 8:9], 0.0).then_inc(logT_ready, 2)
            nc.vector.memset(spare[:, 9:10], 0.0).then_inc(log_turned, 2)
            dve.wait_ge(const_ready, 1)
            nc.vector.memset(cw[:, :, 15:16], 1.0).then_inc(const_ready, 1)
            nc.vector.memset(best[:, :, :], 0.0).then_inc(const_ready, 1)
            dve.wait_ge(const_ready, 3)
            nc.vector.memset(spare[:, 10:11], 0.0).then_inc(const_ready, 1)
            dve.wait_ge(loaded, ROUTER_LOADS)
            logits = P[:, 2, :].rearrange("p (t e) -> p t e", e=16)[:, :, 0:15]
            dve.wait_ge(log_turned, NCH + 2)
            nc.vector.tensor_reduce(top[:, :], logits, axis=AX.X, op=ALU.max).then_inc(route, 1)
            dve.wait_ge(route, 1)
            nc.vector.tensor_tensor(expd[:, :, :], logits, top[:, :].unsqueeze(2).to_broadcast([128, NT, 15]),
                                    ALU.subtract).then_inc(route, 1)
            dve.wait_ge(exp_ready, 1)
            nc.vector.tensor_reduce(total[:, :], expd[:, :, :], axis=AX.X, op=ALU.add).then_inc(route, 1)
            dve.wait_ge(route, 3)
            nc.vector.reciprocal(total[:, :], total[:, :]).then_inc(route, 1)
            dve.wait_ge(route, 4)
            nc.vector.tensor_tensor(probs[:, :, 0:15], expd[:, :, :],
                                    total[:, :].unsqueeze(2).to_broadcast([128, NT, 15]), ALU.mult).then_inc(route, 1)
            dve.wait_ge(route, 5)
            nc.vector.memset(spare[:, 4:5], 0.0)
            for t in range(NT):
                last = nc.vector.max(best[:, t, :], probs[:, t, 0:15])
            last.then_inc(route, 1)
            dve.wait_ge(route, 6)
            nc.vector.tensor_copy(chosen[:, :, 0:3], best[:, :, 0:3]).then_inc(route, 1)
            dve.wait_ge(route, 7)
            nc.vector.memset(spare[:, 5:6], 0.0)
            for t in range(NT):
                last = nc.vector.match_replace(rest[:, t, :], chosen[:, t, :], probs[:, t, :], 0.0)
            last.then_inc(route, 1)
            dve.wait_ge(route, 8)
            nc.vector.tensor_tensor(cw[:, :, 0:15], probs[:, :, 0:15], rest[:, :, 0:15],
                                    ALU.subtract).then_inc(cw_ready, 1)
            with nc.vector.Fori(0, NCH // 2) as j:
                for p in range(2):
                    c = j * 2 + p
                    dve.wait_ge(bias_ready, c + 1)
                    nc.vector.tensor_tensor(XN[:, bass.ds(c * 4, 4), :], P[:, 4 - 4 * p:8 - 4 * p, 0:D],
                                            XN[:, bass.ds(c * 4, 4), :], ALU.add).then_inc(bias_added, 1)
            dve.wait_ge(cw_ready, 1)
            dve.wait_ge(bias_added, NCH)

            def add(par, n, c, e, last_expert):
                for t in range(4):
                    dve.wait_ge(down_ready, n * 2 + 4 + t // 2 + 1)
                    tile = c * 4 + t
                    dst = ln.res[:, t, :] if last_expert else XN[:, tile, :]
                    nc.vector.scalar_tensor_tensor(dst, P[:, 4 + 2 * par + t // 2, (t % 2) * D:(t % 2) * D + D],
                                                   cw[:, tile, bass.ds(e, 1)], XN[:, tile, :],
                                                   ALU.mult, ALU.add).then_inc(added, 1)

            with nc.vector.Fori(0, NE - 1) as e:
                with nc.vector.Fori(0, NCH // 2) as j:
                    dve.wait_ge(added, e * 32 + j * 8 + 8)
                    add(0, e * NCH + j * 2, j * 2, e, False)
                    add(1, e * NCH + j * 2 + 1, j * 2 + 1, e, False)
            with nc.vector.Fori(0, NCH // 2) as j:
                for par in range(2):
                    c = j * 2 + par
                    dve.wait_ge(lns.done, (c + 1) * 4)
                    add(par, (NE - 1) * NCH + c, c, NE - 1, True)
                    dve.wait_ge(added, (NE - 1) * 32 + c * 4 + 12)
                    ln_dve(nc, dve, ln, lns, c, stored, 16)


def block_kernel(nc, T, out):
    bc_scratch = nc.dram_tensor("bc_scratch", [2 * NS, CH], FP32, kind="Internal").ap()
    ctx = ExitStack()
    with ctx:
        XN = ctx.enter_context(nc.sbuf_tensor("XN", [128, TOK // 128, D], FP32))
        ident = ctx.enter_context(nc.sbuf_tensor("ident", [128, 128], FP32))
        P = ctx.enter_context(nc.psum_tensor("P", [128, 8, CH], FP32))
        ident_loaded = ctx.enter_context(nc.semaphore("ident_loaded"))
        with nc.Block() as block:
            @block.sync
            def _(sync):
                sync.dma_start(ident[:, :], T["eye"]).then_inc(ident_loaded, 16)
                sync.wait_ge(ident_loaded, 16)
        mamba_phase(nc, XN, P, ident, T["x_tok"], T["x_feat"], T["m_w_in"], T["m_conv_w"], T["m_conv_b"],
                    T["m_w_x"], T["m_w_dt"], T["m_b_dt"], T["m_a_log"], T["m_w_out"], bc_scratch)
        XT = ctx.enter_context(nc.sbuf_tensor("XT", [128, 2, TOK], FP32))
        ffn_phase(nc, XN, XT, P, ident, T["f_w1"], T["f_b1"], T["f_w2"], T["f_b2"])
        attn_phase(nc, XN, XT, P, ident, T["a_wq"], T["a_wk"], T["a_wv"], T["a_wo"], T["a_bo"], T["a_masks"])
        moe_phase(nc, XN, XT, P, ident, T["e_rw"], T["e_rb"], T["e_w"], T["e_b1"], T["e_b2"], T["e_pads"], out)


def _partitioned(a):
    return a.reshape((-1, 128) + a.shape[1:]).swapaxes(0, 1)


def _contraction_first(w):
    return _partitioned(w.T)


def _masks():
    r, c = np.arange(128)[:, None], np.arange(192)[None, :]
    band = (r <= c) & (c <= r + 64)
    allowed = [c <= r, band, band & (c >= 64), r <= c, band]
    return np.where(np.stack(allowed, 1), 0.0, -1e30).astype(np.float32)


def kernel(**inputs):
    import concourse.bacc as _bacc
    from concourse.bass_utils import run_bass_kernel_spmd as _run

    a = {k: np.asarray(v) for k, v in inputs.items()}
    x = a["L0_attn_x"].reshape(TOK, D)
    experts = {k: np.concatenate([a["L1_ffn_e" + k], a["L1_ffn_s" + k][None]]) for k in ("W1", "b1", "W2", "b2")}
    wo = np.zeros((4, 32, 4, D), np.float32)
    wo[:, :16] = a["L1_attn_Wo"].T.reshape(4, 4, 16, D).transpose(1, 2, 0, 3)
    router_w = np.zeros((D, 16), np.float32)
    router_w[:, :15] = a["L1_ffn_router_W"]
    router_b = np.zeros((16, 1), np.float32)
    router_b[:15, 0] = a["L1_ffn_router_b"]
    b2 = np.zeros((4, 32, D), np.float32)
    b2[:, :16] = experts["b2"]
    laid_out = {
        "eye": np.eye(128, dtype=np.float32),
        "x_tok": _partitioned(x),
        "x_feat": _contraction_first(x),
        "m_w_in": _contraction_first(a["L0_attn_W_in"]),
        "m_conv_w": _partitioned(a["L0_attn_conv_w"].reshape(512, 4)),
        "m_conv_b": _partitioned(a["L0_attn_conv_b"]),
        "m_w_x": _contraction_first(a["L0_attn_W_x"]),
        "m_w_dt": a["L0_attn_W_dt"].T,
        "m_b_dt": _partitioned(a["L0_attn_b_dt"]),
        "m_a_log": _partitioned(a["L0_attn_A_log"]),
        "m_w_out": _contraction_first(a["L0_attn_W_out"]),
        "f_w1": _contraction_first(a["L0_ffn_w1"]),
        "f_b1": _partitioned(a["L0_ffn_b1"]),
        "f_w2": _contraction_first(a["L0_ffn_w2"]),
        "f_b2": a["L0_ffn_b2"],
        "a_wq": _contraction_first(a["L1_attn_Wq"]),
        "a_wk": _contraction_first(a["L1_attn_Wk"]),
        "a_wv": _contraction_first(a["L1_attn_Wv"]),
        "a_wo": wo.reshape(128, 4, D),
        "a_bo": a["L1_attn_bo"],
        "a_masks": _masks(),
        "e_rw": _partitioned(router_w),
        "e_rb": router_b,
        "e_w": np.concatenate([experts[k].reshape(16, 2, 128, D).transpose(0, 2, 1, 3) for k in ("W1", "W2")], 2),
        "e_b1": experts["b1"].reshape(16, 2, 128).transpose(0, 2, 1),
        "e_b2": b2.reshape(128, D),
        "e_pads": np.broadcast_to(-1.0 - np.arange(9, dtype=np.float32), (128, TOK // 128, 9)),
    }
    nc = _bacc.Bacc("TRN2", target_bir_lowering=False, num_devices=1)
    arrays = {"in_" + n: np.ascontiguousarray(v) for n, v in laid_out.items()}
    T = {n: nc.dram_tensor("in_" + n, v.shape, mybir.dt.from_np(v.dtype), kind="ExternalInput").ap()
         for n, v in laid_out.items()}
    out = nc.dram_tensor("out", (128, TOK // 128, D), FP32, kind="ExternalOutput").ap()
    block_kernel(nc, T, out)
    r = _run(nc, [arrays], core_ids=[0])
    return r.results[0]["out"].transpose(1, 0, 2).reshape(NB, SEQ, D)
```

```python
import numpy as np
import concourse.bass as bass
from concourse import mybir
from contextlib import ExitStack

FP32 = mybir.dt.float32
BF16 = mybir.dt.bfloat16
FP32R = mybir.dt.float32r
ALU = mybir.AluOpType
ACT = mybir.ActivationFunctionType
AX = mybir.AxisListType

NB = 4
SEQ = 1024
TOK = NB * SEQ
D = 256
CH = 512
NCH = TOK // CH
DT = 4
NS = 16
EPS = 1e-5


class LnTiles:

    def __init__(self, sb, p, res=None, nrm=None):
        self.res = sb(p + "_ln_res", [128, 4, D]) if res is None else res
        self.nrm = sb(p + "_ln_nrm", [128, 4, D]) if nrm is None else nrm
        self.stats = sb(p + "_ln_stats", [128, 4, 6])
        self.mean = sb(p + "_ln_mean", [128, 4])
        self.diff = sb(p + "_ln_diff", [128, 4])
        self.var = sb(p + "_ln_var", [128, 4])
        self.rstd = sb(p + "_ln_rstd", [128, 4])
        self.minus_half = sb(p + "_ln_minus_half", [128, 4])


class LnSems:

    def __init__(self, sem, p):
        self.steps = sem(p + "_ln_steps")
        self.rstd = sem(p + "_ln_rstd_ready")
        self.done = sem(p + "_ln_done")
        self.half = sem(p + "_ln_half_ready")
        self.turned = sem(p + "_ln_turned")
        self.stored = sem(p + "_ln_stored")


LN_STEPS = 11


def two_banks(P, at):
    return P[:, at:at + 2, :].rearrange("p b (t d) -> p (b t) d", d=D)


def over_tiles(row):
    return row[:, :].unsqueeze(1).to_broadcast([128, 4, D])


def ln_start(nc, ln, lns):
    nc.vector.memset(ln.minus_half[:, :], -0.5).then_inc(lns.half, 1)
    nc.vector.memset(ln.diff[:, :], 0.0).then_inc(lns.stored, 1)
    nc.vector.memset(ln.mean[:, :], 0.0).then_inc(lns.done, 4)


def ln_moments(nc, dve, ln, lns, step, count):
    dve.wait_ge(lns.steps, count[0])
    step(nc.vector.tensor_tensor(ln.mean[:, :], ln.stats[:, :, 1], ln.stats[:, :, 4], ALU.add))
    step(nc.vector.tensor_tensor(ln.diff[:, :], ln.stats[:, :, 1], ln.stats[:, :, 4], ALU.subtract))
    step(nc.vector.tensor_tensor(ln.var[:, :], ln.stats[:, :, 2], ln.stats[:, :, 5], ALU.add))
    dve.wait_ge(lns.steps, count[0])
    step(nc.vector.tensor_tensor(ln.diff[:, :], ln.diff[:, :], ln.diff[:, :], ALU.mult))
    step(nc.vector.tensor_scalar(ln.var[:, :], ln.var[:, :], 1.0 / D, EPS, ALU.mult, ALU.add))
    step(nc.vector.tensor_scalar(ln.mean[:, :], ln.mean[:, :], 0.5, None, ALU.mult))
    dve.wait_ge(lns.steps, count[0])
    step(nc.vector.scalar_tensor_tensor(ln.var[:, :], ln.diff[:, :], 0.25, ln.var[:, :], ALU.mult, ALU.add))


def ln_dve(nc, dve, ln, lns, c, stored=None, each=1):
    count = [c * LN_STEPS]

    def step(ins):
        ins.then_inc(lns.steps, 1)
        count[0] = count[0] + 1

    for t in range(4):
        step(nc.vector.bn_stats(ln.stats[:, t, :], ln.res[:, t, :]))
    ln_moments(nc, dve, ln, lns, step, count)
    dve.wait_ge(lns.rstd, c + 1)
    dve.wait_ge(lns.stored if stored is None else stored, (c + 1) * each)
    for t in range(4):
        nc.vector.tensor_scalar(ln.nrm[:, t, :], ln.res[:, t, :], ln.mean[:, t:t + 1],
                                ln.rstd[:, t:t + 1], ALU.subtract, ALU.mult).then_inc(lns.done, 1)


def ln_pool(nc, pool, ln, lns, c):
    pool.wait_ge(lns.steps, (c + 1) * LN_STEPS)
    nc.gpsimd.tensor_tensor(ln.rstd[:, :], ln.var[:, :], ln.minus_half[:, :], ALU.pow).then_inc(lns.rstd, 1)


def ln_pe(nc, pe, ln, lns, P, bank, ident, c):
    pe.wait_ge(lns.done, (c + 2) * 4)
    for k in range(2):
        for t in range(4):
            last = nc.tensor.transpose(P[:, bank + k, t * 128:(t + 1) * 128], ln.nrm[:, t, k * 128:(k + 1) * 128],
                                       ident[:, :])
    last.then_inc(lns.turned, 1)


def ln_act(nc, act, ln, lns, P, bank, XN, XT, c):
    act.wait_ge(lns.done, (c + 2) * 4)
    nc.scalar.copy(XN[:, bass.ds(c * 4, 4), :], ln.nrm[:, :, :])
    act.wait_ge(lns.turned, c + 1)
    nc.scalar.copy(XT[:, :, bass.ds(c * CH, CH)], P[:, bank:bank + 2, :]).then_inc(lns.stored, 1)
def mamba_phase(nc, XN, P, ident, x_tok, x_feat, w_in, conv_w, conv_b, w_x, w_dt, b_dt, a_log, w_out, bc_scratch):
    ctx = ExitStack()
    with ctx:
        def sb(name, shape, dt=FP32):
            return ctx.enter_context(nc.sbuf_tensor(name, shape, dt))

        def sem(name):
            return ctx.enter_context(nc.semaphore(name))

        w_in_sb = sb("w_in_sb", [128, 2, 1024])
        w_x_sb = sb("w_x_sb", [128, DT, 96])
        w_dt_sb = sb("w_dt_sb", [64, 512])
        w_out_sb = sb("w_out_sb", [128, DT, 256])
        conv_w_sb = sb("conv_w_sb", [128, DT, 4])
        conv_b_sb = sb("conv_b_sb", [128, DT])
        b_dt_sb = sb("b_dt_sb", [128, DT])
        a_neg = sb("a_neg", [128, DT, NS])
        a_exp = sb("a_exp", [128, DT, NS])
        xT = sb("m_xT", [128, 2, CH])
        xs = sb("m_xs", [128, DT, CH + 3])
        conv = sb("m_conv", [128, DT, CH])
        sp = conv
        gate = [sb(f"m_gate{i}", [128, DT, CH]) for i in range(2)]
        u = [sb(f"m_u{i}", [128, DT, CH]) for i in range(2)]
        z = [sb(f"m_z{i}", [128, DT, CH]) for i in range(2)]
        du, delta = u, z
        low = sb("m_low", [64, CH])
        bc_own = sb("m_bc_own", [96, CH])
        bc = sb("m_bc", [128, 2 * NS, CH])
        dbu = sb("m_dbu", [128, 4, CH])
        h3 = sb("m_h3", [128, CH])
        g = sb("m_g", [128, 4, CH])
        state = sb("m_state", [128, DT, NS])
        spare = sb("m_spare", [128, 2])
        ln = LnTiles(sb, "m", XN, XN)

        w_loaded = sem("m_w_loaded")
        x_loaded = sem("m_x_loaded")
        xT_loaded = sem("m_xT_loaded")
        scratch_written = sem("m_scratch_written")
        bc_loaded = [sem(f"m_bc_loaded{k}") for k in range(4)]
        a_ready = sem("m_a_ready")
        xr_ready = sem("m_xr_ready")
        xs_ready = sem("m_xs_ready")
        conv_part = [sem(f"m_conv_part{i}") for i in range(DT)]
        conv_done = sem("m_conv_done")
        xs_head = sem("m_xs_head")
        gate_ready = sem("m_gate_ready")
        u_ready = sem("m_u_ready")
        xdbl_ready = sem("m_xdbl_ready")
        low_ready = sem("m_low_ready")
        bc_own_ready = sem("m_bc_own_ready")
        dlow_ready = sem("m_dlow_ready")
        z_ready = sem("m_z_ready")
        sp_step = sem("m_sp_step")
        delta_ready = sem("m_delta_ready")
        du_ready = sem("m_du_ready")
        dA_ready = sem("m_dA_ready")
        dbu_ready = sem("m_dbu_ready")
        h_ready = sem("m_h_ready")
        g_dve = sem("m_g_dve")
        g_pool = sem("m_g_pool")
        summed = sem("m_summed")
        state_pool = sem("m_state_pool")
        state_dve = sem("m_state_dve")
        gated = sem("m_gated")
        proj_ready = sem("m_proj_ready")
        res_added = sem("m_res_added")
        lns = LnSems(sem, "m")

        DA, H, Y, SIDE = (0, 1), (2, 3, 4), (5, 6), 7
        block = ctx.enter_context(nc.Block())

        def at_start(c, dt, q):
            return isinstance(c, int) and c == 0 and dt == 0 and q == 0

        def none_before(c):
            return isinstance(c, int) and c == 0

        def all_chunks(engine, chunk):
            with engine.Fori(0, NB - 1) as b:
                for half in range(2):
                    chunk(b * 2 + half, b, half, False)
            for half in range(2):
                chunk((NB - 1) * 2 + half, NB - 1, half, half == 1)

        @block.sync
        def _(sync):
            for dst, src in ((w_in_sb, w_in), (w_x_sb, w_x), (w_out_sb, w_out), (conv_w_sb, conv_w)):
                sync.dma_start(dst[:, :, :], src).then_inc(w_loaded, 16)
            for dst, src in ((w_dt_sb, w_dt), (conv_b_sb, conv_b), (b_dt_sb, b_dt)):
                sync.dma_start(dst[:, :], src).then_inc(w_loaded, 16)
            sync.dma_start(a_exp[:, :, :], a_log).then_inc(w_loaded, 16)

            def load_xT(c):
                if none_before(c):
                    here = 0
                else:
                    here = c * CH if isinstance(c, int) else nc.sync.snap(c * CH)
                    sync.wait_ge(xr_ready, c * 8)
                sync.dma_start(xT[:, :, :], x_feat[:, :, bass.ds(here, CH)]).then_inc(xT_loaded, 16)

            def load_bc(c):
                sync.wait_ge(bc_own_ready, c + 1)
                sync.dma_start(bc_scratch, bc_own[64:96, :]).then_inc(scratch_written, 16)
                used = [(c - 1) * 64 + 48 + 4 * (k + 1) for k in range(4)]
                if not isinstance(c, int):
                    used = [nc.sync.snap(n) for n in used]
                sync.wait_ge(scratch_written, (c + 1) * 16)
                for k in range(4):
                    if not none_before(c):
                        sync.wait_ge(summed, used[k])
                    for s in (0, NS):
                        rows = slice(s + 4 * k, s + 4 * k + 4)
                        sync.dma_start(bc[:, rows, :],
                                       bc_scratch[rows, :].partition_broadcast(128)).then_inc(bc_loaded[k], 16)

            load_xT(0)
            load_bc(0)
            sync.dma_start(XN[:, :, :], x_tok).then_inc(x_loaded, 16)

            def chunk(c, b, half, last):
                if not last:
                    load_xT(c + 1)
                    load_bc(c + 1)
            all_chunks(nc.sync, chunk)

        @block.tensor
        def _(pe):
            pe.wait_ge(w_loaded, 16 * 8)

            def project_in(c, m):
                if m == 0:
                    pe.wait_ge(xT_loaded, (c + 1) * 16)
                    if not none_before(c):
                        pe.wait_ge(res_added, c * 2)
                elif m <= 4:
                    pe.wait_ge(xs_ready, c * DT + m)
                else:
                    pe.wait_ge(gate_ready, c * DT + m - 4)
                for k in range(2):
                    last = nc.tensor.matmul(P[:, SIDE, :], w_in_sb[:, k, m * 128:(m + 1) * 128], xT[:, k, :],
                                            start=(k == 0), stop=(k == 1))
                last.then_inc(xr_ready, 1)

            def project_x(c, par):
                pe.wait_ge(gate_ready, (c + 1) * DT)
                pe.wait_ge(u_ready, (c + 1) * DT)
                for k in range(DT):
                    last = nc.tensor.matmul(P[0:96, SIDE, :], w_x_sb[:, k, :], u[par][:, k, :],
                                            start=(k == 0), stop=(k == DT - 1))
                last.then_inc(xdbl_ready, 1)

            def project_dt(c, m):
                if m == 0:
                    pe.wait_ge(low_ready, c + 1)
                    pe.wait_ge(bc_own_ready, c + 1)
                else:
                    pe.wait_ge(z_ready, c * DT + m)
                nc.tensor.matmul(P[:, SIDE, :], w_dt_sb[:, m * 128:(m + 1) * 128], low[:, :],
                                 start=True, stop=True).then_inc(dlow_ready, 1)

            def prepare(c, par, slot):
                if slot < 8:
                    project_in(c, slot)
                if slot == 14:
                    project_x(c, par)
                if 17 <= slot < 21:
                    project_dt(c, slot - 17)

            def project_out(c, par, pair, final=False):
                if pair == 0:
                    if not final:
                        pe.wait_ge(z_ready, (c + 2) * DT)
                    pe.wait_ge(gated, (c + 1) * DT + 2)
                else:
                    pe.wait_ge(res_added, c * 2 + 3)
                for t in (2 * pair, 2 * pair + 1):
                    for k in range(DT):
                        last = nc.tensor.matmul(P[:, SIDE, (t % 2) * 256:(t % 2) * 256 + 256],
                                                gate[par][:, k, t * 128:(t + 1) * 128], w_out_sb[:, k, :],
                                                start=(k == 0), stop=(k == DT - 1))
                last.then_inc(proj_ready, 1)

            def units(c, dt, q, rs):
                for r in rs:
                    if r == 0 and q == 0:
                        pe.wait_ge(gated, c * DT + dt + 1)
                    if r < 3:
                        pe.wait_ge(g_dve, c * 48 + 12 * dt + q * 3 + r + 1)
                    else:
                        pe.wait_ge(g_pool, c * 16 + 4 * dt + q + 1)
                    nc.tensor.matmul(P[:, Y[dt % 2], :], ident[:, :], g[:, r, :], start=(q == 0 and r == 0),
                                     stop=(q == 3 and r == 3)).then_inc(summed, 1)

            for slot in range(24):
                prepare(0, 0, slot)
            for q in range(4):
                units(0, 0, q, range(4))

            def chunk(c, b, half, last):
                for s in range(12):
                    for pair in range(2):
                        units(c, 1 + s // 4, s % 4, (2 * pair, 2 * pair + 1))
                        if not last:
                            prepare(c + 1, 1 - half, 2 * s + pair)
                if last:
                    project_out(c, half, 0, True)
                    project_out(c, half, 1, True)
                else:
                    for q in range(4):
                        units(c + 1, 0, q, range(4))
                        if q < 2:
                            project_out(c, half, q)
            all_chunks(nc.tensor, chunk)

        @block.scalar
        def _(act):
            act.wait_ge(w_loaded, 16 * 8)
            nc.scalar.activation(a_exp[:, :, :], a_exp[:, :, :], ACT.Exp).then_inc(a_ready, 1)
            act.wait_ge(a_ready, 1)
            nc.scalar.mul(a_neg[:, :, :], a_exp[:, :, :], -1.0).then_inc(a_ready, 1)
            act.wait_ge(a_ready, 2)

            def prepare(c, par, slot):
                if 3 <= slot < 7:
                    m = slot - 3
                    if m == 0:
                        act.wait_ge(xs_head, c + 1)
                    act.wait_ge(xr_ready, c * 8 + m + 1)
                    nc.scalar.copy(xs[:, m, 3:CH + 3], P[:, SIDE, :]).then_inc(xs_ready, 1)
                if 7 <= slot < 11:
                    m = slot - 7
                    if m == 0 and not none_before(c):
                        act.wait_ge(proj_ready, c * 2)
                    act.wait_ge(xr_ready, c * 8 + 4 + m + 1)
                    nc.scalar.activation(gate[par][:, m, :], P[:, SIDE, :], ACT.Silu).then_inc(gate_ready, 1)
                if slot in (9, 11, 13, 15):
                    for m in ((slot - 9) // 2,):
                        act.wait_ge(conv_done, c * DT + m + 1)
                        nc.scalar.activation(u[par][:, m, :], conv[:, m, :], ACT.Silu,
                                             bias=conv_b_sb[:, m:m + 1]).then_inc(u_ready, 1)
                if slot == 17:
                    act.wait_ge(xdbl_ready, c + 1)
                    nc.scalar.copy(low[:, :], P[0:64, SIDE, :]).then_inc(low_ready, 1)
                    if not none_before(c):
                        act.wait_ge(scratch_written, c * 16)
                    nc.scalar.copy(bc_own[64:96, :], P[64:96, SIDE, :]).then_inc(bc_own_ready, 1)
                if 19 <= slot < 23:
                    m = slot - 19
                    act.wait_ge(dlow_ready, c * DT + m + 1)
                    nc.scalar.activation(z[par][:, m, :], P[:, SIDE, :], ACT.Identity,
                                         bias=b_dt_sb[:, m:m + 1]).then_inc(z_ready, 1)
                if slot == 22:
                    act.wait_ge(z_ready, (c + 1) * DT)
                    nc.scalar.activation(sp[:, :, :], z[par][:, :, :], ACT.Abs).then_inc(sp_step, 1)
                if slot == 23:
                    act.wait_ge(sp_step, c * 4 + 1)
                    nc.scalar.activation(sp[:, :, :], sp[:, :, :], ACT.Exp, scale=-1.0).then_inc(sp_step, 1)
                    act.wait_ge(sp_step, c * 4 + 2)
                    for tiles in (slice(0, 1), slice(1, DT)):
                        nc.scalar.activation(sp[:, tiles, :], sp[:, tiles, :], ACT.Ln, bias=1.0).then_inc(sp_step, 1)

            def decays(c, par, dt, q, rs):
                for r in rs:
                    unit = c * 64 + 16 * dt + q * 4 + r
                    if q == 0 and r == 0:
                        act.wait_ge(delta_ready, c * DT + dt + 1)
                    if not (at_start(c, dt, q) and r < 2):
                        act.wait_ge(h_ready, unit - 1)
                    nc.scalar.activation(P[:, DA[r % 2], :], delta[par][:, dt, :], ACT.Exp,
                                         scale=a_neg[:, dt, q * 4 + r:q * 4 + r + 1]).then_inc(dA_ready, 1)

            for slot in range(24):
                prepare(0, 0, slot)
            for q in range(4):
                decays(0, 0, 0, q, range(4))

            def chunk(c, b, half, last):
                for s in range(12):
                    for pair in range(2):
                        decays(c, half, 1 + s // 4, s % 4, (2 * pair, 2 * pair + 1))
                        if not last:
                            prepare(c + 1, 1 - half, 2 * s + pair)
                if not last:
                    for q in range(4):
                        decays(c + 1, 1 - half, 0, q, range(4))
            all_chunks(nc.scalar, chunk)

        @block.gpsimd
        def _(pool):
            pool.wait_ge(lns.half, 1)

            def last_product(c, half, dt, q):
                unit = c * 64 + 16 * dt + q * 4 + 3
                pool.wait_ge(h_ready, unit + 1)
                if not at_start(c, dt, q):
                    pool.wait_ge(summed, unit - 3)
                nc.gpsimd.tensor_tensor(g[:, 3, :], h3[:, :], bc[:, NS + q * 4 + 3, :],
                                        ALU.mult).then_inc(g_pool, 1)
                if half == 0:
                    nc.gpsimd.tensor_copy(state[:, dt, q * 4 + 3:q * 4 + 4],
                                          h3[:, CH - 1:CH]).then_inc(state_pool, 1)

            def inputs(c, half, dt, q):
                for r in range(4):
                    unit = c * 64 + 16 * dt + q * 4 + r
                    if r == 0 and dt == 0:
                        pool.wait_ge(bc_loaded[q], (c + 1) * 32)
                    if r == 0 and q == 0:
                        pool.wait_ge(du_ready, c * DT + dt + 1)
                    if not at_start(c, dt, q):
                        pool.wait_ge(h_ready, unit - 3)
                    nc.gpsimd.tensor_tensor(dbu[:, r, :], du[half][:, dt, :], bc[:, q * 4 + r, :],
                                            ALU.mult).then_inc(dbu_ready, 1)
                    if r == 1 and not at_start(c, dt, q):
                        if q:
                            last_product(c, half, dt, q - 1)
                        elif dt:
                            last_product(c, half, dt - 1, 3)

            for q in range(4):
                inputs(0, 0, 0, q)

            def chunk(c, b, half, last):
                for s in range(12):
                    inputs(c, half, 1 + s // 4, s % 4)
                last_product(c, half, DT - 1, 3)
                if not last:
                    for q in range(4):
                        inputs(c + 1, 1 - half, 0, q)
                ln_pool(nc, pool, ln, lns, c)
            all_chunks(nc.gpsimd, chunk)

        @block.vector
        def _(dve):
            nc.vector.memset(ln.minus_half[:, :], -0.5).then_inc(lns.half, 1)
            nc.vector.memset(xs[:, :, 0:3], 0.0).then_inc(xs_head, 1)
            nc.vector.memset(state[:, :, :], 0.0).then_inc(gated, 2)
            nc.vector.memset(spare[:, 0:1], 0.0).then_inc(proj_ready, 2)
            nc.vector.memset(spare[:, 1:2], 0.0).then_inc(res_added, 2)
            dve.wait_ge(w_loaded, 16 * 8)

            def convolve(c, tiles):
                for tap in range(4):
                    for m in tiles:
                        if tap == 0:
                            dve.wait_ge(xs_ready, c * DT + m + 1)
                            if m == 0 and not none_before(c):
                                dve.wait_ge(delta_ready, c * DT)
                            nc.vector.tensor_scalar(conv[:, m, :], xs[:, m, 0:CH], conv_w_sb[:, m, 0:1], None,
                                                    ALU.mult).then_inc(conv_part[m], 1)
                        else:
                            dve.wait_ge(conv_part[m], c * 3 + tap)
                            nc.vector.scalar_tensor_tensor(conv[:, m, :], xs[:, m, tap:CH + tap],
                                                           conv_w_sb[:, m, tap:tap + 1], conv[:, m, :],
                                                           ALU.mult, ALU.add).then_inc(
                                                               conv_part[m] if tap < 3 else conv_done, 1)

            def save_head(c, half):
                if half == 0:
                    nc.vector.tensor_copy(xs[:, :, 0:3], xs[:, :, CH:CH + 3]).then_inc(xs_head, 1)
                else:
                    nc.vector.memset(xs[:, :, 0:3], 0.0).then_inc(xs_head, 1)

            def finish_delta(c, par, m):
                dve.wait_ge(sp_step, c * 4 + (4 if m else 3))
                nc.vector.scalar_tensor_tensor(delta[par][:, m, :], z[par][:, m, :], 0.0, sp[:, m, :],
                                               ALU.max, ALU.add).then_inc(delta_ready, 1)
                dve.wait_ge(delta_ready, c * DT + m + 1)
                nc.vector.tensor_tensor(du[par][:, m, :], delta[par][:, m, :], u[par][:, m, :],
                                        ALU.mult).then_inc(du_ready, 1)

            def prepare(c, par, s):
                if 3 <= s < 7:
                    convolve(c, (s - 3,))
                if s == 6:
                    save_head(c, par)
                if s == 11:
                    finish_delta(c, par, 0)

            def scan(c, b, half, dt, q, r):
                unit = c * 64 + 16 * dt + q * 4 + r
                fresh = at_start(c, dt, q)
                dve.wait_ge(dA_ready, unit + 1)
                dve.wait_ge(dbu_ready, unit + 1)
                if half == 1 and dt == 0 and q == 0 and r == 0:
                    dve.wait_ge(state_pool, (b + 1) * 16)
                    dve.wait_ge(state_dve, (b + 1) * 16)
                if half == 0 and r == 0 and not (dt == 0 and q == 0):
                    dve.wait_ge(state_dve, b * 16 + 4 * dt + q)
                if (half == 1 or (dt == 0 and q == 0)) and r < 3 and not fresh:
                    dve.wait_ge(g_dve, c * 48 + 12 * dt + q * 3 - 3 + r + 1)
                if r == 3 and not fresh:
                    dve.wait_ge(g_pool, c * 16 + 4 * dt + q)
                    if half == 0:
                        dve.wait_ge(state_pool, b * 16 + 4 * dt + q)
                out = P[:, H[r], :] if r < 3 else h3[:, :]
                n = q * 4 + r
                initial = state[:, dt, n:n + 1] if half else 0.0
                nc.vector.tensor_tensor_scan(out, P[:, DA[r % 2], :], dbu[:, r, :], initial,
                                             ALU.mult, ALU.add).then_inc(h_ready, 1)

            def product(c, dt, q, r):
                unit = c * 64 + 16 * dt + q * 4 + r
                dve.wait_ge(h_ready, unit + 1)
                if not at_start(c, dt, q):
                    dve.wait_ge(summed, unit - 3)
                nc.vector.tensor_tensor(g[:, r, :], P[:, H[r], :], bc[:, NS + q * 4 + r, :],
                                        ALU.mult).then_inc(g_dve, 1)

            def units(c, b, half, dt, q):
                if dt == 0:
                    dve.wait_ge(bc_loaded[q], (c + 1) * 32)
                scan(c, b, half, dt, q, 0)
                scan(c, b, half, dt, q, 1)
                product(c, dt, q, 0)
                scan(c, b, half, dt, q, 2)
                product(c, dt, q, 1)
                scan(c, b, half, dt, q, 3)
                product(c, dt, q, 2)
                if half == 0:
                    nc.vector.tensor_copy(state[:, dt, q * 4:q * 4 + 3],
                                          P[:, H[0]:H[2] + 1, CH - 1]).then_inc(state_dve, 1)

            def gate_tile(c, half, d):
                dve.wait_ge(summed, c * 64 + 16 * (d + 1))
                nc.vector.tensor_tensor(gate[half][:, d, :], P[:, Y[d % 2], :], gate[half][:, d, :],
                                        ALU.mult).then_inc(gated, 1)

            def add_residual(c, pair):
                if pair == 0:
                    dve.wait_ge(x_loaded, 16)
                dve.wait_ge(proj_ready, c * 2 + pair + 3)
                here = XN[:, bass.ds(c * 4 + 2 * pair, 2), :]
                nc.vector.tensor_tensor(here, P[:, SIDE, :].rearrange("p (t d) -> p t d", d=D), here,
                                        ALU.add).then_inc(res_added, 1)

            def statistics(c):
                dve.wait_ge(res_added, c * 2 + 4)
                nc.vector.memset(spare[:, 0:1], 0.0)
                count = [c * LN_STEPS]

                def step(ins):
                    ins.then_inc(lns.steps, 1)
                    count[0] = count[0] + 1
                for t in range(4):
                    step(nc.vector.bn_stats(ln.stats[:, t, :], XN[:, c * 4 + t, :]))
                ln_moments(nc, dve, ln, lns, step, count)

            def normalise(c):
                dve.wait_ge(lns.rstd, c + 1)
                nc.vector.memset(spare[:, 1:2], 0.0)
                for t in range(4):
                    nc.vector.tensor_scalar(XN[:, c * 4 + t, :], XN[:, c * 4 + t, :], ln.mean[:, t:t + 1],
                                            ln.rstd[:, t:t + 1], ALU.subtract, ALU.mult).then_inc(lns.done, 1)

            convolve(0, (0, 1, 2, 3))
            save_head(0, 0)
            finish_delta(0, 0, 0)
            dve.wait_ge(gate_ready, DT)
            for q in range(4):
                units(0, 0, 0, 0, q)
                if q < 3:
                    finish_delta(0, 0, q + 1)

            def chunk(c, b, half, last):
                for s in range(12):
                    units(c, b, half, 1 + s // 4, s % 4)
                    if s % 4 == 0:
                        gate_tile(c, half, s // 4)
                    if not last:
                        prepare(c + 1, 1 - half, s)
                if last:
                    gate_tile(c, half, DT - 1)
                    add_residual(c, 0)
                    add_residual(c, 1)
                    statistics(c)
                else:
                    nb = b + 1 if half else b
                    units(c + 1, nb, 1 - half, 0, 0)
                    gate_tile(c, half, DT - 1)
                    finish_delta(c + 1, 1 - half, 1)
                    units(c + 1, nb, 1 - half, 0, 1)
                    add_residual(c, 0)
                    finish_delta(c + 1, 1 - half, 2)
                    units(c + 1, nb, 1 - half, 0, 2)
                    finish_delta(c + 1, 1 - half, 3)
                    add_residual(c, 1)
                    statistics(c)
                    dve.wait_ge(gate_ready, (c + 2) * DT)
                    units(c + 1, nb, 1 - half, 0, 3)
                normalise(c)
            all_chunks(nc.vector, chunk)


def ffn_phase(nc, XN, XT, P, ident, w1, b1, w2, b2_all):
    MT = 8
    ctx = ExitStack()
    with ctx:
        def sb(name, shape, dt=FP32):
            return ctx.enter_context(nc.sbuf_tensor(name, shape, dt))

        def sem(name):
            return ctx.enter_context(nc.semaphore(name))

        w1_sb = sb("f_w1_sb", [128, 2, 1024])
        w2_sb = sb("f_w2_sb", [128, MT, D])
        w1_sign = sb("f_w1_sign", [128, 2, 1024], FP32R)
        w2_sign = sb("f_w2_sign", [128, MT, D], FP32R)
        b1_sb = sb("f_b1", [128, MT])
        b2_sb = sb("f_b2", [128, D])
        spare = sb("f_spare", [128, 2])
        ones = sb("f_ones", [128, 128])
        alpha1 = sb("f_alpha1", [128, MT])
        alpha2 = sb("f_alpha2", [128, D])
        x_hi = [sb(f"f_x_hi{i}", [128, 2, CH], FP32R) for i in range(2)]
        x_lo = [sb(f"f_x_lo{i}", [128, 2, CH], FP32R) for i in range(2)]
        x_chunk = [sb(f"f_x_chunk{i}", [128, 4, D]) for i in range(2)]
        h = sb("f_h", [128, 4, CH])
        h_hi = [sb(f"f_h_hi{i}", [128, MT, CH], FP32R) for i in range(2)]
        h_lo = [sb(f"f_h_lo{i}", [128, MT, CH], FP32R) for i in range(2)]
        ln_tiles = sb("f_ln_tiles", [128, 8, D])
        ln = LnTiles(sb, "f", ln_tiles[:, 0:4, :], ln_tiles[:, 4:8, :])
        w1_abs = h[:, :, :].rearrange("p a n -> p (a n)").rearrange("p (k n) -> p k n", k=2)
        w2_abs = ln_tiles
        w1_loaded = sem("f_w1_loaded")
        w2_loaded = sem("f_w2_loaded")
        signs_ready = sem("f_signs_ready")
        abs_ready = sem("f_abs_ready")
        means_summed = sem("f_means_summed")
        alpha1_ready = sem("f_alpha1_ready")
        alpha2_ready = sem("f_alpha2_ready")
        ones_ready = sem("f_ones_ready")
        x_turned = sem("f_x_turned")
        x_kept = sem("f_x_kept")
        x_loaded = [sem(f"f_x_loaded{i}") for i in range(2)]
        x_hi_ready = sem("f_x_hi_ready")
        x_lo_ready = sem("f_x_lo_ready")
        up_ready = sem("f_up_ready")
        gelu_done = sem("f_gelu_done")
        h_hi_ready = sem("f_h_hi_ready")
        h_lo_ready = sem("f_h_lo_ready")
        down_ready = sem("f_down_ready")
        res_step = sem("f_res_step")
        lns = LnSems(sem, "f")
        UP, DOWN, TURN = 0, 4, 6
        block = ctx.enter_context(nc.Block())

        @block.sync
        def _(sync):
            def load_x(c, par):
                here = c * 4 if isinstance(c, int) else nc.sync.snap(c * 4)
                if not isinstance(c, int):
                    sync.wait_ge(x_turned, c - 1)
                sync.dma_start(x_chunk[par][:, :, :], XN[:, bass.ds(here, 4), :]).then_inc(x_loaded[par], 16)

            load_x(0, 0)
            load_x(1, 1)
            sync.dma_start(w1_sb[:, :, :], w1).then_inc(w1_loaded, 16)
            sync.dma_start(w2_sb[:, :, :], w2).then_inc(w2_loaded, 16)
            for dst, src in ((b1_sb, b1), (b2_sb, b2_all.partition_broadcast(128))):
                sync.dma_start(dst[:, :], src).then_inc(w2_loaded, 16)
            with nc.sync.Fori(1, NCH // 2) as j:
                load_x(j * 2, 0)
                load_x(j * 2 + 1, 1)

        @block.tensor
        def _(pe):
            def up(c, par, first=False):
                pe.wait_ge(x_lo_ready, c + 1)
                for m in range(MT):
                    if not (first and m < 4):
                        pe.wait_ge(gelu_done, c * MT + m - 3)
                    for part in (x_hi, x_lo):
                        for k in range(2):
                            last = nc.tensor.matmul(P[:, UP + m % 4, :], w1_sign[:, k, m * 128:(m + 1) * 128],
                                                    part[par][:, k, :], start=(part is x_hi and k == 0),
                                                    stop=(part is x_lo and k == 1))
                    last.then_inc(up_ready, 1)

            def down(c, par, first):
                if first:
                    pe.wait_ge(alpha2_ready, 1)
                else:
                    pe.wait_ge(res_step, c * 3 - 2)
                for t in range(4):
                    for part, ready in ((h_hi, h_hi_ready), (h_lo, h_lo_ready)):
                        for k in range(MT):
                            if t == 0:
                                pe.wait_ge(ready, c * MT + k + 1)
                            last = nc.tensor.matmul(P[:, DOWN + t // 2, (t % 2) * D:(t % 2) * D + D],
                                                    part[par][:, k, t * 128:(t + 1) * 128], w2_sign[:, k, :],
                                                    start=(part is h_hi and k == 0),
                                                    stop=(part is h_lo and k == MT - 1))
                last.then_inc(down_ready, 1)

            def turn_x(c, par):
                if not isinstance(c, int) or c > 2:
                    pe.wait_ge(lns.stored, c - 2)
                if not isinstance(c, int) or c > 0:
                    pe.wait_ge(x_kept, c)
                pe.wait_ge(x_loaded[par], (c - par + 2) * 8)
                for k in range(2):
                    for t in range(4):
                        last = nc.tensor.transpose(P[:, TURN + k, t * 128:(t + 1) * 128],
                                                   x_chunk[par][:, t, k * 128:(k + 1) * 128], ident[:, :])
                last.then_inc(x_turned, 1)

            def step(c, par, first=False, last=False, more=True):
                if not last:
                    up(c + 1, 1 - par)
                if more:
                    turn_x(c + 2, par)
                down(c, par, first)
                if not first:
                    pe.wait_ge(x_kept, c + 3 if more else NCH)
                    ln_pe(nc, pe, ln, lns, P, TURN, ident, c - 1)

            turn_x(0, 0)
            turn_x(1, 1)
            pe.wait_ge(ones_ready, 1)
            pe.wait_ge(abs_ready, 1)
            for m in range(MT):
                for k in range(2):
                    nc.tensor.matmul(P[:, DOWN + 1, 2 * m:2 * m + 2], w1_abs[:, k, m * 128:(m + 1) * 128], ones[:, 0:2],
                                     start=(k == 0), stop=(k == 1))
            pe.wait_ge(abs_ready, 2)
            for k in range(MT):
                last = nc.tensor.matmul(P[:, DOWN, 0:D], ones[:, :], w2_abs[:, k, :], start=(k == 0), stop=(k == MT - 1))
            last.then_inc(means_summed, 1)
            pe.wait_ge(signs_ready, 2)
            up(0, 0, True)
            step(0, 0, first=True)
            step(1, 1)
            with nc.tensor.Fori(1, NCH // 2 - 1) as j:
                step(j * 2, 0)
                step(j * 2 + 1, 1)
            step(NCH - 2, 0, more=False)
            step(NCH - 1, 1, last=True, more=False)
            ln_pe(nc, pe, ln, lns, P, TURN, ident, NCH - 1)

        @block.scalar
        def _(act):
            def x_high(c, par):
                if not isinstance(c, int) or c > 1:
                    act.wait_ge(up_ready, (c - 1) * MT)
                act.wait_ge(x_turned, c + 1)
                nc.scalar.copy(spare[:, 0:1], ident[:, 0:1])
                nc.scalar.copy(XT[:, :, bass.ds(c * CH, CH)], P[:, TURN:TURN + 2, :]).then_inc(x_kept, 1)
                act.wait_ge(x_kept, c + 1)
                nc.scalar.copy(spare[:, 1:2], ident[:, 0:1])
                nc.scalar.copy(x_hi[par][:, :, :], XT[:, :, bass.ds(c * CH, CH)]).then_inc(x_hi_ready, 1)

            def gelus(c, par, fresh=False):
                for m in range(MT):
                    n = c * MT + m
                    act.wait_ge(up_ready, n + 1)
                    if fresh and isinstance(n, int) and n < 4:
                        pass
                    else:
                        act.wait_ge(h_lo_ready, n - 3)
                    nc.scalar.activation(h[:, m % 4, :], P[:, UP + m % 4, :], ACT.Gelu, bias=b1_sb[:, m:m + 1],
                                         scale=alpha1[:, m:m + 1]).then_inc(gelu_done, 1)
                    act.wait_ge(gelu_done, n + 1)
                    if m == 0 and not fresh:
                        act.wait_ge(down_ready, c - 1)
                    nc.scalar.copy(h_hi[par][:, m, :], h[:, m % 4, :]).then_inc(h_hi_ready, 1)

            def step(c, par, first=False, last=False, turn=True, more=True):
                if not last:
                    gelus(c + 1, 1 - par, first)
                if more:
                    x_high(c + 2, par)
                if turn:
                    ln_act(nc, act, ln, lns, P, TURN, XN, XT, c - 1)

            x_high(0, 0)
            x_high(1, 1)
            act.wait_ge(w1_loaded, 16)
            nc.scalar.sign(w1_sign[:, :, :], w1_sb[:, :, :]).then_inc(signs_ready, 1)
            act.wait_ge(w2_loaded, 48)
            nc.scalar.sign(w2_sign[:, :, :], w2_sb[:, :, :]).then_inc(signs_ready, 1)
            act.wait_ge(means_summed, 1)
            nc.scalar.mul(alpha2[:, :], P[:, DOWN, 0:D], 1.0 / 1024).then_inc(alpha2_ready, 1)
            act.wait_ge(alpha1_ready, 1)
            gelus(0, 0, True)
            step(0, 0, first=True, turn=False)
            step(1, 1)
            with nc.scalar.Fori(1, NCH // 2 - 1) as j:
                step(j * 2, 0)
                step(j * 2 + 1, 1)
            step(NCH - 2, 0, more=False)
            step(NCH - 1, 1, last=True, more=False)
            ln_act(nc, act, ln, lns, P, TURN, XN, XT, NCH - 1)

        @block.gpsimd
        def _(pool):
            def x_low(c, par):
                here = c * CH if isinstance(c, int) else nc.gpsimd.snap(c * CH)
                pool.wait_ge(x_hi_ready, c + 1)
                nc.gpsimd.tensor_tensor(x_lo[par][:, :, :], XT[:, :, bass.ds(here, CH)], x_hi[par][:, :, :],
                                        ALU.subtract).then_inc(x_lo_ready, 1)

            def lows(c, par):
                for m in range(MT):
                    pool.wait_ge(h_hi_ready, c * MT + m + 1)
                    nc.gpsimd.tensor_tensor(h_lo[par][:, m, :], h[:, m % 4, :], h_hi[par][:, m, :],
                                            ALU.subtract).then_inc(h_lo_ready, 1)

            def step(c, par, last=False, turn=True, more=True):
                if not last:
                    lows(c + 1, 1 - par)
                if turn:
                    ln_pool(nc, pool, ln, lns, c - 1)
                if more:
                    x_low(c + 2, par)

            x_low(0, 0)
            x_low(1, 1)
            pool.wait_ge(lns.half, 1)
            lows(0, 0)
            step(0, 0, turn=False)
            step(1, 1)
            with nc.gpsimd.Fori(1, NCH // 2 - 1) as j:
                step(j * 2, 0)
                step(j * 2 + 1, 1)
            step(NCH - 2, 0, more=False)
            step(NCH - 1, 1, last=True, more=False)
            ln_pool(nc, pool, ln, lns, NCH - 1)

        @block.vector
        def _(dve):
            ln_start(nc, ln, lns)
            nc.vector.memset(ones[:, :], 1.0).then_inc(ones_ready, 1)
            dve.wait_ge(w1_loaded, 16)
            nc.vector.scalar_tensor_tensor(w1_abs, w1_sb[:, :, :], -1.0, w1_sb[:, :, :], ALU.mult, ALU.max).then_inc(abs_ready, 1)
            dve.wait_ge(w2_loaded, 48)
            nc.vector.scalar_tensor_tensor(w2_abs[:, :, :], w2_sb[:, :, :], -1.0, w2_sb[:, :, :], ALU.mult, ALU.max).then_inc(abs_ready, 1)
            dve.wait_ge(means_summed, 1)
            nc.vector.tensor_scalar(alpha1[:, :], P[:, DOWN + 1, 0:2 * MT].rearrange("p (m two) -> p m two", two=2)[:, :, 0],
                                    1.0 / D, None, ALU.mult).then_inc(alpha1_ready, 1)
            dve.wait_ge(alpha2_ready, 1)
            with nc.vector.Fori(0, NCH) as c:
                dve.wait_ge(down_ready, c + 1)
                dve.wait_ge(lns.done, (c + 1) * 4)
                nc.vector.tensor_tensor(ln.res[:, :, :], two_banks(P, DOWN), over_tiles(alpha2),
                                        ALU.mult).then_inc(res_step, 1)
                dve.wait_ge(res_step, c * 3 + 1)
                nc.vector.tensor_tensor(ln.res[:, :, :], ln.res[:, :, :], over_tiles(b2_sb), ALU.add).then_inc(res_step, 1)
                dve.wait_ge(res_step, c * 3 + 2)
                nc.vector.tensor_tensor(ln.res[:, :, :], ln.res[:, :, :], XN[:, bass.ds(c * 4, 4), :],
                                        ALU.add).then_inc(res_step, 1)
                dve.wait_ge(res_step, c * 3 + 3)
                ln_dve(nc, dve, ln, lns, c)


def attn_phase(nc, XN, XT, P, ident, wqk, wv, wo, bo, masks):
    HD = 16
    QT = SEQ // 128
    SLOTS_Q = (0, 0, 1, 1, 0, 2)
    SLOTS_K = (0, 1, 0, 1, 2, 0)
    ROWS = 6 * HD
    STACK_LOADS = 7 * 16
    PARTS_SENT = 6 * 16
    WIN = 64
    SIDE = 6
    GLOBAL = (True, True, False, False)

    MAX_GLOBAL = [(i, 0, min((i + 1) * 128, CH)) for i in range(4)]
    for i in range(4, QT):
        MAX_GLOBAL += [(i, 0, CH), (i, CH, (i + 1) * 128 - CH)]
    MAX_LOCAL = QT // 2
    MAX_COUNT = [4 * (len(MAX_GLOBAL) if g else MAX_LOCAL) for g in GLOBAL]
    EXP_GLOBAL = [[(0, 0, 0)], [(1, 0, 0), (3, 0, 384)], [(2, 0, 0), (6, 1, 256)], [(0, 1, 0)], [(1, 1, 0)],
                  [(2, 1, 0)], [(3, 1, 0)], [(4, 1, 0)], [(5, 1, 0), (7, 1, 384)]]
    STEPS = [len(EXP_GLOBAL) if g else QT // 2 for g in GLOBAL]

    def queries(j, chunk):
        first = max(j * 128, chunk * CH)
        return first, (chunk + 1) * CH - first

    def maxima_after(i, n):
        first, each = ((0, 6), (3, 3), (2, 8), (0, 6))[i]
        return range(max(each * (n - first), 0), min(each * (n - first + 1), MAX_COUNT[(i + 1) % 4]))
    EARLY = 24

    ctx = ExitStack()
    with ctx:
        def sb(name, shape, dt=FP32):
            return ctx.enter_context(nc.sbuf_tensor(name, shape, dt))

        def sem(name):
            return ctx.enter_context(nc.semaphore(name))

        wqk_sb = sb("a_wqk_sb", [128, 2, 4 * 128])
        wv_sb = sb("a_wv_sb", [128, 2, D])
        wo_sb = sb("a_wo_sb", [128, 4, D])
        bo_sb = sb("a_bo_sb", [128, D])
        scale = sb("a_scale", [128, 1])
        mask = sb("a_mask", [128, 5, 192], BF16)
        eye = sb("a_eye", [128, 128], BF16)
        zeros = sb("a_zeros", [128, CH], BF16)
        xTb = sb("a_xTb", [128, 2, SEQ])
        rest = [sb(f"a_rest{i}", [128, CH]) for i in range(2)]
        parts = sb("a_parts", [128, 3, SEQ], BF16)
        qs = [sb(f"a_qs{i}", [128, 4, SEQ], BF16) for i in range(2)]
        ks = [sb(f"a_ks{i}", [128, 4, SEQ], BF16) for i in range(2)]
        v_sb = sb("a_v_sb", [128, QT, D])
        vpad = [sb(f"a_vpad{i}", [128, QT, 4, 32]) for i in range(2)]
        pT = [sb(f"a_pT{i}", [128, 4, CH]) for i in range(2)]
        mx = sb("a_mx", [128, 16, QT])
        ones = sb("a_ones", [128, QT, HD])
        spare = sb("a_spare", [128, 4])
        mx2 = sb("a_mx2", [128, 4, 4, 2])
        mrest = sb("a_mrest", [32, 128])
        mparts = sb("a_mparts", [32, 3, 128], BF16)
        oT = sb("a_oT", [128, 4, SEQ])
        mask_in = oT[:, 0, 0:5 * 192].rearrange("p (m n) -> p m n", n=192)
        acc_sb = sb("a_acc", [128, 2 * CH])
        den_pack = sb("a_den_pack", [128, SEQ // 32])
        den = sb("a_den", [128, 2 * CH])
        ln = LnTiles(sb, "a", XN)
        scratch = nc.dram_tensor("a_scratch", [2, 2, 3, HD, 4 * SEQ], BF16, kind="Internal").ap()

        inverses = nc.dram_tensor("a_inverses", [128, SEQ // 32], FP32, kind="Internal").ap()

        loaded = sem("a_loaded")
        const_dve = sem("a_const_dve")
        const_pool = sem("a_const_pool")
        mask_ready = sem("a_mask_ready")
        x_loaded = sem("a_x_loaded")
        v_ready = sem("a_v_ready")
        v_kept = sem("a_v_kept")
        qk_ready = sem("a_qk_ready")
        hi_ready = sem("a_hi_ready")
        rest_ready = sem("a_rest_ready")
        mid_ready = sem("a_mid_ready")
        lo_ready = sem("a_lo_ready")
        parts_out = sem("a_parts_out")
        stacked = sem("a_stacked")
        s1_ready = sem("a_s1_ready")
        max_done = sem("a_max_done")
        mx_ready = sem("a_mx_ready")
        mx_turned = sem("a_mx_turned")
        mhi_ready = sem("a_mhi_ready")
        mrest_ready = sem("a_mrest_ready")
        mmid_ready = sem("a_mmid_ready")
        mlo_ready = sem("a_mlo_ready")
        m_stacked = sem("a_m_stacked")
        vpad_ready = sem("a_vpad_ready")
        s2_ready = sem("a_s2_ready")
        p_ready = sem("a_p_ready")
        pv_done = sem("a_pv_done")
        sum_ready = sem("a_sum_ready")
        acc_kept = sem("a_acc_kept")
        den_packed = sem("a_den_packed")
        inv_ready = sem("a_inv_ready")
        inv_sent = sem("a_inv_sent")
        den_spread = sem("a_den_spread")
        o_ready = sem("a_o_ready")
        out_ready = sem("a_out_ready")
        bo_added = sem("a_bo_added")
        res_added = sem("a_res_added")
        lns = LnSems(sem, "a")
        block = ctx.enter_context(nc.Block())

        def max_base(b, i):
            return b * sum(MAX_COUNT) + sum(MAX_COUNT[:i])

        def step_base(b, i):
            return b * sum(STEPS) + sum(STEPS[:i])

        def buffer(i, n):
            return pT[(sum(STEPS[:i]) + n) % 2]

        def after(b, i, steps):
            return (b, i + steps) if i + steps < 4 else (b + 1, i + steps - 4)

        def all_sequences(engine, sequence):
            sequence(0, True, False)
            with engine.Fori(1, NB - 1) as b:
                sequence(b, False, False)
            sequence(NB - 1, False, True)

        @block.sync
        def _(sync):
            def val(n):
                return n if isinstance(n, int) else nc.sync.snap(n)

            def load_x(b):
                here, before = val(b * SEQ), val(b * 8)
                if not isinstance(b, int) or b:
                    sync.wait_ge(qk_ready, before)
                sync.dma_start(xTb[:, :, :], XT[:, :, bass.ds(here, SEQ)]).then_inc(x_loaded, 16)

            def send_parts(b, i):
                sync.wait_ge(lo_ready, (b * 4 + i) * 2 + 2)
                for at in range(2):
                    for p in range(3):
                        dst = scratch[i % 2, at, p].rearrange("d (h t) -> h d t", t=SEQ)
                        sync.dma_start(dst, parts[64 * at:64 * at + 64, p, :]).then_inc(parts_out, 16)

            def fill_stacks(b, i):
                if isinstance(b, int) and b * 4 + i == 0:
                    sync.wait_ge(parts_out, PARTS_SENT)
                else:
                    sync.wait_ge(vpad_ready, b * 4 + i + 1)
                for at, stack in enumerate((qs[i % 2], ks[i % 2])):
                    src = scratch[i % 2, at]
                    for s in (0, 2, 4):
                        this, following = (SLOTS_Q, SLOTS_K)[at][s:s + 2]
                        if this == following:
                            pieces = [(2, src[this:this + 1].to_broadcast([2, HD, 4 * SEQ]))]
                        elif this < following:
                            pieces = [(2, src[this:following + 1:following - this])]
                        else:
                            pieces = [(1, src[this:this + 1]), (1, src[following:following + 1])]
                        row = s * HD
                        for count, piece in pieces:
                            sync.dma_start(stack[row:row + count * HD, :, :], piece).then_inc(stacked, 16)
                            row = row + count * HD

            def stack_maxima(b, i):
                sync.wait_ge(mlo_ready, b * 4 + i + 1)
                for p in range(3):
                    sync.dma_start(qs[i % 2][ROWS + p:ROWS + p + 1, :, :], mparts[:, p, :]).then_inc(m_stacked, 16)

            load_x(0)
            for dst, src in ((wqk_sb[:, :, :], wqk), (wv_sb[:, :, :], wv), (wo_sb[:, :, :], wo), (mask_in, masks),
                             (bo_sb[:, :], bo.partition_broadcast(128))):
                sync.dma_start(dst, src).then_inc(loaded, 16)
            send_parts(0, 0)
            fill_stacks(0, 0)
            send_parts(0, 1)
            stack_maxima(0, 0)

            def sequence(b, first, last):
                for i in range(4):
                    if not (last and i == 3):
                        fill_stacks(*after(b, i, 1))
                    if not (last and i >= 2):
                        send_parts(*after(b, i, 2))
                    if not last and i == 1:
                        load_x(b + 1)
                    if not (last and i == 3):
                        stack_maxima(*after(b, i, 1))
            all_sequences(nc.sync, sequence)

        @block.tensor
        def _(pe):
            pe.wait_ge(loaded, 16 * 5)
            pe.wait_ge(const_dve, 5)
            pe.wait_ge(const_pool, 1)
            pe.wait_ge(mask_ready, 2)

            def project_v(b, t):
                if t >= 2:
                    pe.wait_ge(v_kept, b * 4 + t - 1)
                for tile in (2 * t, 2 * t + 1):
                    for k in range(2):
                        last = nc.tensor.matmul(P[:, SIDE + 1 - t % 2, (tile % 2) * D:(tile % 2) * D + D],
                                                xTb[:, k, tile * 128:(tile + 1) * 128], wv_sb[:, k, :],
                                                start=(k == 0), stop=(k == 1))
                last.then_inc(v_ready, 1)

            def project_qk(b, i, half):
                if half == 0:
                    pe.wait_ge(x_loaded, (b + 1) * 16)
                for k in range(2):
                    last = nc.tensor.matmul(P[:, SIDE + half, :], wqk_sb[:, k, i * 128:(i + 1) * 128],
                                            xTb[:, k, half * CH:(half + 1) * CH], start=(k == 0), stop=(k == 1))
                last.then_inc(qk_ready, 1)

            def scores1(b, i, items):
                for item in items:
                    bank = SIDE + item % 2
                    pe.wait_ge(max_done, max_base(b, i) + item + 1)
                    if GLOBAL[i]:
                        h, n = divmod(item, len(MAX_GLOBAL))
                        t, first, keys = MAX_GLOBAL[n]
                        diagonal = first + keys == (t + 1) * 128
                        last = nc.tensor.matmul(P[:, bank, 0:keys], qs[i % 2][0:ROWS, h, t * 128:(t + 1) * 128],
                                                ks[i % 2][0:ROWS, h, first:first + keys], start=True, stop=not diagonal)
                        if diagonal:
                            last = nc.tensor.matmul(P[:, bank, keys - 128:keys], eye[:, :], mask[:, 0, 0:128],
                                                    start=False, stop=True)
                    else:
                        h, n = divmod(item, MAX_LOCAL)
                        for t in (2 * n, 2 * n + 1):
                            col = (t % 2) * 192
                            cut = WIN if t == 0 else 0
                            nc.tensor.matmul(P[:, bank, col:col + 192], eye[:, :], mask[:, 2 if t == 0 else 1, :],
                                             start=True, stop=False)
                            last = nc.tensor.matmul(P[:, bank, col + cut:col + 192],
                                                    qs[i % 2][0:ROWS, h, t * 128:(t + 1) * 128],
                                                    ks[i % 2][0:ROWS, h, t * 128 - WIN + cut:(t + 1) * 128],
                                                    start=False, stop=True)
                    last.then_inc(s1_ready, 1)

            def turn_maxima(b, i):
                pe.wait_ge(mx_ready, b * 4 + i + 1)
                nc.tensor.transpose(P[:, SIDE, 0:128], mx[:, :, :].rearrange("p h i -> p (h i)"),
                                    ident[:, :]).then_inc(mx_turned, 1)

            def start_maxima(b, i, coming):
                pe.wait_ge(stacked, (b * 4 + i + 1) * STACK_LOADS)
                if coming:
                    pe.wait_ge(rest_ready, (b * 4 + i + 2) * 2)

            def project_out(b, half):
                if half == 0:
                    pe.wait_ge(o_ready, (b + 1) * 4)
                else:
                    pe.wait_ge(res_added, b * 2 + 1)
                for t in range(4):
                    for quad in range(4):
                        last = nc.tensor.matmul(P[:, SIDE + t // 2, (t % 2) * D:(t % 2) * D + D],
                                                oT[:, quad, half * CH + t * 128:half * CH + (t + 1) * 128],
                                                wo_sb[:, quad, :], start=(quad == 0), stop=(quad == 3))
                last.then_inc(out_ready, 1)

            def pass2(b, i, side, maxima):
                base = step_base(b, i)
                start = isinstance(b, int) and b * 4 + i == 0

                def scores2(n):
                    for pair in range(2):
                        if not (start and n == 0):
                            pe.wait_ge(p_ready, (base + n) * 2 + pair - 1)
                        for h in (2 * pair, 2 * pair + 1):
                            if GLOBAL[i]:
                                for j, chunk, col in EXP_GLOBAL[n]:
                                    first, count = queries(j, chunk)
                                    diagonal = first == j * 128
                                    last = nc.tensor.matmul(P[:, h, col:col + count],
                                                            ks[i % 2][0:ROWS + 3, h, j * 128:(j + 1) * 128],
                                                            qs[i % 2][0:ROWS + 3, h, first:first + count],
                                                            start=True, stop=not diagonal)
                                    if diagonal:
                                        last = nc.tensor.matmul(P[:, h, col:col + 128], eye[:, :], mask[:, 3, 0:128],
                                                                start=False, stop=True)
                            else:
                                for j in (2 * n, 2 * n + 1):
                                    count = min(192, SEQ - j * 128)
                                    at = (j % 2) * 192
                                    nc.tensor.matmul(P[:, h, at:at + 192], eye[:, :], mask[:, 4, :],
                                                     start=True, stop=False)
                                    last = nc.tensor.matmul(P[:, h, at:at + count],
                                                            ks[i % 2][0:ROWS + 3, h, j * 128:(j + 1) * 128],
                                                            qs[i % 2][0:ROWS + 3, h, j * 128:j * 128 + count],
                                                            start=False, stop=True)
                        last.then_inc(s2_ready, 1)
                        if n:
                            maxima(n - 1, pair)

                def values(n):
                    pe.wait_ge(p_ready, (base + n) * 2 + 2)
                    if GLOBAL[i]:
                        items = [(j, chunk, queries(j, chunk)[0] - chunk * CH, col, queries(j, chunk)[1])
                                 for j, chunk, col in EXP_GLOBAL[n]]
                    else:
                        items = []
                        for j in (2 * n, 2 * n + 1):
                            for chunk in range(2):
                                lo = max(j * 128, chunk * CH)
                                hi = min(j * 128 + 192, (chunk + 1) * CH)
                                if lo < hi:
                                    items.append((j, chunk, lo - chunk * CH, (j % 2) * 192 + lo - j * 128, hi - lo))
                    for j, chunk, dst, col, count in items:
                        for h in range(4):
                            last = nc.tensor.matmul(P[32 * h:32 * h + 32, 4 + chunk, dst:dst + count],
                                                    vpad[i % 2][:, j, h, :], buffer(i, n)[:, h, col:col + count],
                                                    start=False, stop=False, tile_position=(0, 32 * h))
                    last.then_inc(pv_done, 1)

                pe.wait_ge(m_stacked, (b * 4 + i + 1) * 48)
                pe.wait_ge(vpad_ready, b * 4 + i + 1)
                scores2(0)
                if not start:
                    pe.wait_ge(acc_kept, b * 4 + i)
                for chunk in range(2):
                    nc.tensor.matmul(P[:, 4 + chunk, :], zeros[:, 0:128], zeros[:, :], start=True, stop=False)
                for n in range(STEPS[i]):
                    if n + 1 < STEPS[i]:
                        scores2(n + 1)
                    else:
                        maxima(n, 0)
                        maxima(n, 1)
                    values(n)
                    maxima(n, 2)
                    side(n)
                for chunk in range(2):
                    last = nc.tensor.matmul(P[:, 4 + chunk, :], zeros[:, 0:128], zeros[:, :], start=False, stop=True)
                last.then_inc(sum_ready, 1)

            pe.wait_ge(x_loaded, 16)
            for t in range(4):
                project_v(0, t)
            pe.wait_ge(v_kept, 4)
            for half in range(2):
                project_qk(0, 0, half)
            pe.wait_ge(rest_ready, 2)
            for half in range(2):
                project_qk(0, 1, half)
            start_maxima(0, 0, True)
            scores1(0, 0, range(MAX_COUNT[0]))
            turn_maxima(0, 0)

            def sequence(b, first, last):
                for i in range(4):
                    if not (last and i >= 2):
                        pe.wait_ge(mrest_ready, b * 4 + i + 1)
                        pe.wait_ge(mhi_ready, b * 4 + i + 1)
                        if i == 1 and not first:
                            pe.wait_ge(res_added, b * 2)
                        if i == 3:
                            pe.wait_ge(v_kept, (b + 2) * 4)
                        nb, ni = after(b, i, 2)
                        for half in range(2):
                            project_qk(nb, ni, half)

                    def maxima(n, part):
                        if not (last and i == 3):
                            nb, ni = after(b, i, 1)
                            items = maxima_after(i, n)
                            items = items[part * len(items) // 3:(part + 1) * len(items) // 3]
                            if items and items[0] == 0:
                                start_maxima(nb, ni, not (last and i >= 2))
                                if i in (1, 2) and not first:
                                    pe.wait_ge(lns.stored, b * 2 - 1 + i)
                            scores1(nb, ni, items)

                    def side(n):
                        if i in (1, 2) and n == 3 - i and not first:
                            if not (last and i == 2):
                                pe.wait_ge(rest_ready, (b * 4 + i + 3) * 2)
                            else:
                                pe.wait_ge(mrest_ready, b * 4 + i + 1)
                                pe.wait_ge(mhi_ready, b * 4 + i + 1)
                            ln_pe(nc, pe, ln, lns, P, SIDE, ident, b * 2 - 3 + i)
                    pass2(b, i, side, maxima)
                    if i < 3:
                        turn_maxima(b, i + 1)
                    if i == 0 and not first or i == 2 and not last:
                        pe.wait_ge(mrest_ready, b * 4 + i + 2)
                        pe.wait_ge(mhi_ready, b * 4 + i + 2)
                    if i == 0 and not first:
                        project_out(b - 1, 0)
                        project_out(b - 1, 1)
                    if i == 2 and not last:
                        for t in range(4):
                            project_v(b + 1, t)
                if not last:
                    scores1(b + 1, 0, range(EARLY, MAX_COUNT[0]))
                    turn_maxima(b + 1, 0)
                else:
                    project_out(b, 0)
                    project_out(b, 1)
                    pe.wait_ge(res_added, b * 2 + 2)
                    ln_pe(nc, pe, ln, lns, P, SIDE, ident, b * 2)
                    pe.wait_ge(lns.stored, b * 2 + 2)
                    ln_pe(nc, pe, ln, lns, P, SIDE, ident, b * 2 + 1)
            all_sequences(nc.tensor, sequence)

        @block.scalar
        def _(act):
            act.wait_ge(loaded, 16 * 5)
            nc.scalar.copy(mask[:, :, :], mask_in).then_inc(mask_ready, 1)
            nc.scalar.copy(eye[:, :], ident[:, :]).then_inc(mask_ready, 1)
            act.wait_ge(const_dve, 5)

            def keep_v(b, t):
                act.wait_ge(v_ready, b * 4 + t + 1)
                if t == 0 and not (isinstance(b, int) and b == 0):
                    act.wait_ge(vpad_ready, b * 4)
                nc.scalar.copy(v_sb[:, 2 * t:2 * t + 2, :],
                               P[:, SIDE + 1 - t % 2, :].rearrange("p (t d) -> p t d", d=D)).then_inc(v_kept, 1)

            def high(b, i, half):
                Q = b * 4 + i
                act.wait_ge(qk_ready, Q * 2 + half + 1)
                if half == 0 and not (isinstance(Q, int) and Q == 0):
                    act.wait_ge(parts_out, Q * PARTS_SENT)
                nc.scalar.activation(parts[:, 0, half * CH:(half + 1) * CH], P[:, SIDE + half, :], ACT.Copy,
                                     scale=scale[:, 0:1]).then_inc(hi_ready, 1)

            def middle(b, i, half):
                act.wait_ge(rest_ready, (b * 4 + i) * 2 + half + 1)
                nc.scalar.copy(parts[:, 1, half * CH:(half + 1) * CH], rest[half][:, :]).then_inc(mid_ready, 1)

            def maxima_high(b, i):
                Q = b * 4 + i
                act.wait_ge(mx_turned, Q + 1)
                if not (isinstance(Q, int) and Q == 0):
                    act.wait_ge(m_stacked, Q * 48)
                nc.scalar.activation(mparts[:, 0, :], P[0:32, SIDE, 0:128], ACT.Copy, scale=-1.0).then_inc(mhi_ready, 1)

            def maxima_middle(b, i):
                act.wait_ge(mrest_ready, b * 4 + i + 1)
                nc.scalar.copy(mparts[:, 1, :], mrest[:, :]).then_inc(mmid_ready, 1)

            def pack_denominators(Q):
                act.wait_ge(acc_kept, Q + 1)
                nc.scalar.dma_start(den_pack[:, :], acc_sb[HD:128:32, :]).then_inc(den_packed, 16)

            def send_inverses(Q):
                act.wait_ge(inv_ready, Q + 1)
                nc.scalar.dma_start(inverses, den_pack[:, :]).then_inc(inv_sent, 16)

            def spread_inverses(Q):
                act.wait_ge(inv_sent, (Q + 1) * 16)
                for h in range(4):
                    src = inverses[32 * h:32 * h + 32, :].rearrange("p n -> (p n)").partition_broadcast(HD)
                    nc.scalar.dma_start(den[32 * h:32 * h + HD, :], src).then_inc(den_spread, 16)

            def exponentials(b, i, side):
                base = step_base(b, i)
                start = isinstance(b, int) and b * 4 + i == 0
                for n in range(STEPS[i]):
                    count = CH if GLOBAL[i] else 384
                    for pair in range(2):
                        heads = slice(2 * pair, 2 * pair + 2)
                        act.wait_ge(s2_ready, (base + n) * 2 + pair + 1)
                        if pair == 0 and not (start and n < 2):
                            act.wait_ge(pv_done, base + n - 1)
                        nc.scalar.activation(buffer(i, n)[:, heads, 0:count], P[:, heads, 0:count],
                                             ACT.Exp).then_inc(p_ready, 1)
                    side(n)

            for t in range(4):
                keep_v(0, t)
            for i in range(2):
                for half in range(2):
                    high(0, i, half)
                for half in range(2):
                    middle(0, i, half)
            maxima_high(0, 0)
            maxima_middle(0, 0)

            def sequence(b, first, last):
                for i in range(4):
                    nb, ni = after(b, i, 2)
                    coming = not (last and i >= 2)
                    if i or not first:
                        pack_denominators(b * 4 + i - 1)
                    if coming:
                        for half in range(2):
                            high(nb, ni, half)

                    def side(n):
                        if coming and n == 2:
                            for half in range(2):
                                middle(nb, ni, half)
                        if n == 2 and (i or not first):
                            send_inverses(b * 4 + i - 1)
                        if n == 3 and (i or not first):
                            spread_inverses(b * 4 + i - 1)
                        if not first and (i, n) in ((1, 3), (2, 2)):
                            ln_act(nc, act, ln, lns, P, SIDE, XN, XT, b * 2 - 3 + i)
                    exponentials(b, i, side)
                    if i < 3:
                        maxima_high(b, i + 1)
                        maxima_middle(b, i + 1)
                    if i == 2 and not last:
                        for t in range(4):
                            keep_v(b + 1, t)
                if not last:
                    maxima_high(b + 1, 0)
                    maxima_middle(b + 1, 0)
                else:
                    pack_denominators(b * 4 + 3)
                    send_inverses(b * 4 + 3)
                    spread_inverses(b * 4 + 3)
                    for half in range(2):
                        ln_act(nc, act, ln, lns, P, SIDE, XN, XT, b * 2 + half)
            all_sequences(nc.scalar, sequence)

        @block.gpsimd
        def _(pool):
            nc.gpsimd.memset(ones[:, :, :], 1.0)
            for i in range(2):
                last = nc.gpsimd.memset(vpad[i][:, :, :, :], 1.0)
            last.then_inc(const_pool, 1)
            pool.wait_ge(const_pool, 1)
            pool.wait_ge(lns.half, 1)

            def lay_out_v(b, i):
                Q = b * 4 + i
                if i == 0:
                    pool.wait_ge(v_kept, (b + 1) * 4)
                if not isinstance(Q, int) or Q >= 2:
                    pool.wait_ge(pv_done, step_base(b, i - 1) if i else step_base(b - 1, 3))
                if not isinstance(Q, int) or Q >= 1:
                    pool.wait_ge(parts_out, (Q + 1) * PARTS_SENT)
                for h in range(4):
                    f = i * 64 + h * HD
                    last = nc.gpsimd.tensor_tensor(vpad[i % 2][:, :, h, 0:HD], v_sb[:, :, f:f + HD],
                                                   ones[:, :, :], ALU.mult)
                last.then_inc(vpad_ready, 1)

            def low(b, i):
                for half in range(2):
                    cols = slice(half * CH, (half + 1) * CH)
                    pool.wait_ge(mid_ready, (b * 4 + i) * 2 + half + 1)
                    nc.gpsimd.tensor_tensor(parts[:, 2, cols], rest[half][:, :], parts[:, 1, cols],
                                            ALU.subtract).then_inc(lo_ready, 1)

            def maxima_low(b, i):
                pool.wait_ge(mmid_ready, b * 4 + i + 1)
                nc.gpsimd.tensor_tensor(mparts[:, 2, :], mrest[:, :], mparts[:, 1, :],
                                        ALU.subtract).then_inc(mlo_ready, 1)

            lay_out_v(0, 0)
            low(0, 0)
            low(0, 1)
            maxima_low(0, 0)

            def sequence(b, first, last):
                for i in range(4):
                    if not (last and i == 3):
                        lay_out_v(*after(b, i, 1))
                    if not (last and i >= 2):
                        low(*after(b, i, 2))
                    if i == 0:
                        here = XN[:, bass.ds(b * QT, QT), :]
                        nc.gpsimd.tensor_tensor(here, here, bo_sb[:, :].unsqueeze(1).to_broadcast([128, QT, D]),
                                                ALU.add).then_inc(bo_added, 1)
                    if not (last and i == 3):
                        maxima_low(*after(b, i, 1))
                    if i < 2 and not first:
                        ln_pool(nc, pool, ln, lns, b * 2 - 2 + i)
                if last:
                    for half in range(2):
                        ln_pool(nc, pool, ln, lns, b * 2 + half)
            all_sequences(nc.gpsimd, sequence)

        @block.vector
        def _(dve):
            ln_start(nc, ln, lns)
            nc.vector.memset(mrest[:, :], 0.0).then_inc(max_done, 2)
            nc.vector.memset(mx[:, :, :], 0.0)
            for i in range(2):
                last = nc.vector.memset(ks[i][ROWS:ROWS + 3, :, :], 1.0)
            last.then_inc(const_dve, 1)
            nc.vector.memset(zeros[:, :], 0.0).then_inc(const_dve, 1)
            nc.vector.memset(scale[0:64, :], 0.25).then_inc(const_dve, 1)
            nc.vector.memset(scale[64:128, :], 1.0).then_inc(const_dve, 1)
            nc.vector.memset(den[:, :], 1.0).then_inc(const_dve, 1)
            dve.wait_ge(const_dve, 5)

            def remainder(b, i):
                Q = b * 4 + i
                for half in range(2):
                    dve.wait_ge(hi_ready, Q * 2 + half + 1)
                    if not (isinstance(Q, int) and Q == 0):
                        dve.wait_ge(lo_ready, Q * 2 + half - 1)
                    nc.vector.scalar_tensor_tensor(rest[half][:, :], P[:, SIDE + half, :], scale[:, 0:1],
                                                   parts[:, 0, half * CH:(half + 1) * CH], ALU.mult,
                                                   ALU.subtract).then_inc(rest_ready, 1)

            def maxima(b, i, items):
                for item in items:
                    dve.wait_ge(s1_ready, max_base(b, i) + item + 1)
                    bank = SIDE + item % 2
                    if GLOBAL[i]:
                        h, n = divmod(item, len(MAX_GLOBAL))
                        t, first, keys = MAX_GLOBAL[n]
                        dst = mx[:, h, t:t + 1] if t < 4 else mx2[:, h, t - 4, first // CH:first // CH + 1]
                        nc.vector.tensor_reduce(dst, P[:, bank, 0:keys], axis=AX.X, op=ALU.max).then_inc(max_done, 1)
                    else:
                        h, n = divmod(item, MAX_LOCAL)
                        nc.vector.tensor_reduce(mx[:, h, 2 * n:2 * n + 2],
                                                P[:, bank, 0:384].rearrange("p (a k) -> p a k", a=2),
                                                axis=AX.X, op=ALU.max).then_inc(max_done, 1)

            def maxima_end(b, i):
                dve.wait_ge(max_done, max_base(b, i) + MAX_COUNT[i] + 2)
                if GLOBAL[i]:
                    nc.vector.tensor_reduce(mx[:, 0:4, 4:8], mx2[:, :, :, :], axis=AX.X, op=ALU.max).then_inc(mx_ready, 1)
                else:
                    nc.vector.memset(spare[:, 0:1], 0.0).then_inc(mx_ready, 1)
                dve.wait_ge(mhi_ready, b * 4 + i + 1)
                nc.vector.scalar_tensor_tensor(mrest[:, :], P[0:32, SIDE, 0:128], -1.0, mparts[:, 0, :],
                                               ALU.mult, ALU.subtract).then_inc(mrest_ready, 1)

            def take_sums(Q):
                if not (isinstance(Q, int) and Q == 0):
                    dve.wait_ge(o_ready, Q)
                dve.wait_ge(sum_ready, Q + 1)
                nc.vector.tensor_copy(acc_sb[:, :], P[:, 4:6, :].rearrange("p a n -> p (a n)")).then_inc(acc_kept, 1)

            def invert(Q):
                dve.wait_ge(den_packed, (Q + 1) * 16)
                nc.vector.reciprocal(den_pack[:, :], den_pack[:, :]).then_inc(inv_ready, 1)

            def outputs(b, i):
                Q = b * 4 + i
                if i == 0 and not (isinstance(Q, int) and Q == 0):
                    dve.wait_ge(out_ready, b * 2)
                dve.wait_ge(den_spread, (Q + 1) * 64)
                nc.vector.tensor_tensor(oT[:, i, :], acc_sb[:, :], den[:, :], ALU.mult).then_inc(o_ready, 1)

            def add_residual(c):
                dve.wait_ge(out_ready, c + 1)
                here = XN[:, bass.ds(c * 4, 4), :]
                nc.vector.tensor_tensor(here, two_banks(P, SIDE), here, ALU.add).then_inc(res_added, 1)

            def normalise(c):
                dve.wait_ge(res_added, c + 1)
                nc.vector.memset(spare[:, 2:3], 0.0)
                count = [c * LN_STEPS]

                def step(ins):
                    ins.then_inc(lns.steps, 1)
                    count[0] = count[0] + 1
                for t in range(4):
                    step(nc.vector.bn_stats(ln.stats[:, t, :], XN[:, c * 4 + t, :]))
                ln_moments(nc, dve, ln, lns, step, count)
                dve.wait_ge(lns.rstd, c + 1)
                dve.wait_ge(lns.stored, c + 1)
                nc.vector.memset(spare[:, 3:4], 0.0)
                for t in range(4):
                    nc.vector.tensor_scalar(ln.nrm[:, t, :], XN[:, c * 4 + t, :], ln.mean[:, t:t + 1],
                                            ln.rstd[:, t:t + 1], ALU.subtract, ALU.mult).then_inc(lns.done, 1)

            remainder(0, 0)
            remainder(0, 1)
            maxima(0, 0, range(MAX_COUNT[0]))
            maxima_end(0, 0)

            def sequence(b, first, last):
                for i in range(4):
                    Q = b * 4 + i
                    if not (last and i >= 2):
                        remainder(*after(b, i, 2))
                    if i or not first:
                        invert(Q - 1)
                    if i < 3:
                        maxima(b, i + 1, range(MAX_COUNT[i + 1]))
                        maxima_end(b, i + 1)
                    elif not last:
                        maxima(b + 1, 0, range(EARLY))
                    if i:
                        outputs(b, i - 1)
                    elif not first:
                        outputs(b - 1, 3)
                    take_sums(Q)
                    if i == 3 and not last:
                        maxima(b + 1, 0, range(EARLY, MAX_COUNT[0]))
                        maxima_end(b + 1, 0)
                    if i == 0 and not first:
                        add_residual(b * 2 - 2)
                        add_residual(b * 2 - 1)
                    if i < 2 and not first:
                        normalise(b * 2 - 2 + i)
                if last:
                    invert(b * 4 + 3)
                    outputs(b, 3)
                dve.wait_ge(bo_added, b + 1)
                if last:
                    add_residual(b * 2)
                    add_residual(b * 2 + 1)
                    normalise(b * 2)
                    normalise(b * 2 + 1)
            all_sequences(nc.vector, sequence)


def moe_phase(nc, XN, XT, P, ident, router_w, router_b, w, b1, b2, pads, out):
    NE = 16
    NT = TOK // 128
    ctx = ExitStack()
    with ctx:
        def sb(name, shape, dt=FP32):
            return ctx.enter_context(nc.sbuf_tensor(name, shape, dt))

        def sem(name):
            return ctx.enter_context(nc.semaphore(name))

        rw_sb = sb("e_rw", [128, 2, 16])
        rb_sb = sb("e_rb", [16, 1])
        w_raw = sb("e_w_raw", [128, 4, D])
        w_hi = [sb(f"e_w_hi{i}", [128, 4, D], FP32R) for i in range(2)]
        w_lo = [sb(f"e_w_lo{i}", [128, 4, D], FP32R) for i in range(2)]
        x_hi = sb("e_x_hi", [128, 2, TOK], FP32R)
        x_lo = sb("e_x_lo", [128, 2, TOK], FP32R)
        b1_sb = [sb(f"e_b1_{i}", [128, 2]) for i in range(2)]
        b2_sb = sb("e_b2", [128, D])
        logT = [sb(f"e_logT{i}", [16, CH]) for i in range(2)]
        top = sb("e_top", [128, NT])
        expd = sb("e_expd", [128, NT, 15])
        total = sb("e_total", [128, NT])
        probs = sb("e_probs", [128, NT, 24])
        best = sb("e_best", [128, NT, 8])
        chosen = sb("e_chosen", [128, NT, 8])
        rest = sb("e_rest", [128, NT, 24])
        cw = sb("e_cw", [128, NT, 32])
        cwT = sb("e_cwT", [128, NCH, 128])
        hT = [sb(f"e_hT{i}", [128, 2, CH]) for i in range(2)]
        h_hi = [sb(f"e_h_hi{i}", [128, 2, CH], FP32R) for i in range(2)]
        h_lo = [sb(f"e_h_lo{i}", [128, 2, CH], FP32R) for i in range(2)]
        spare = sb("e_spare", [128, 12])
        ln = LnTiles(sb, "e", XT[:, 0, 0:1024].rearrange("p (t d) -> p t d", d=D),
                     XT[:, 0, 1024:2048].rearrange("p (t d) -> p t d", d=D))
        loaded = sem("e_loaded")
        w_loaded = sem("e_w_loaded")
        b1_loaded = [sem(f"e_b1_loaded{i}") for i in range(2)]
        w_hi_ready = sem("e_w_hi_ready")
        w_lo_ready = sem("e_w_lo_ready")
        x_hi_ready = sem("e_x_hi_ready")
        x_lo_ready = sem("e_x_lo_ready")
        const_ready = sem("e_const_ready")
        logits_ready = sem("e_logits_ready")
        logT_ready = sem("e_logT_ready")
        log_turned = sem("e_log_turned")
        route = sem("e_route")
        exp_ready = sem("e_exp_ready")
        cw_ready = sem("e_cw_ready")
        cw_turned = sem("e_cw_turned")
        cwT_ready = sem("e_cwT_ready")
        bias_ready = sem("e_bias_ready")
        bias_added = sem("e_bias_added")
        up_ready = sem("e_up_ready")
        relu_done = sem("e_relu_done")
        h_hi_ready = sem("e_h_hi_ready")
        h_lo_ready = sem("e_h_lo_ready")
        down_ready = sem("e_down_ready")
        added = sem("e_added")
        stored = sem("e_stored")
        lns = LnSems(sem, "e")
        ROUTER_LOADS = 16 * 5
        block = ctx.enter_context(nc.Block())

        @block.sync
        def _(sync):
            for dst, src in ((rw_sb[:, :, :], router_w), (rb_sb[:, :], router_b),
                             (b2_sb[:, :], b2), (probs[:, :, 15:24], pads[:, :, 0:9]),
                             (chosen[:, :, 3:8], pads[:, :, 0:5])):
                sync.dma_start(dst, src).then_inc(loaded, 16)
            for e in range(2):
                sync.dma_start(b1_sb[e][:, :], b1[e]).then_inc(b1_loaded[e], 16)
            sync.dma_start(w_raw[:, :, :], w[0]).then_inc(w_loaded, 16)
            sync.wait_ge(w_lo_ready, 1)
            sync.dma_start(w_raw[:, :, :], w[1]).then_inc(w_loaded, 16)
            with nc.sync.Fori(0, NE // 2 - 1) as pair:
                for i in range(2):
                    expert = nc.sync.snap(pair * 2 + (i + 2))
                    sync.wait_ge(w_lo_ready, pair * 2 + (i + 2))
                    sync.dma_start(w_raw[:, :, :], w[bass.ds(expert, 1)].rearrange("a p k d -> p (a k) d")).then_inc(w_loaded, 16)
                    sync.wait_ge(down_ready, (pair * 2 + i + 1) * NCH * 2 + 4)
                    sync.dma_start(b1_sb[i][:, :], b1[bass.ds(expert, 1)].rearrange("a p k -> p (a k)")).then_inc(b1_loaded[i], 16)
            with nc.sync.Fori(0, NCH) as c:
                first_tile = nc.sync.snap(c * 4)
                sync.wait_ge(lns.done, (c + 2) * 4)
                sync.dma_start(out[:, bass.ds(first_tile, 4), :], ln.nrm[:, :, :]).then_inc(stored, 16)
            sync.wait_ge(stored, 16 * (NCH + 1))

        @block.tensor
        def _(pe):
            pe.wait_ge(loaded, ROUTER_LOADS)
            pe.wait_ge(const_ready, 4)
            with nc.tensor.Fori(0, NCH // 2) as j:
                for p in range(2):
                    c = j * 2 + p
                    pe.wait_ge(logT_ready, c + 1)
                    for k in range(2):
                        last = nc.tensor.matmul(P[0:16, p, :], rw_sb[:, k, :], XT[:, k, bass.ds(c * CH, CH)],
                                                start=(k == 0), stop=(k == 1))
                    last.then_inc(logits_ready, 1)
                for p in range(2):
                    c = j * 2 + p
                    pe.wait_ge(logT_ready, c + 3)
                    for t in range(4):
                        last = nc.tensor.matmul(P[:, 2, bass.ds(c * 64 + t * 16, 16)], logT[p][:, t * 128:(t + 1) * 128],
                                                ident[0:16, 0:16], start=True, stop=True)
                    last.then_inc(log_turned, 1)
            pe.wait_ge(cw_ready, 1)
            for c in range(NCH):
                last = nc.tensor.transpose(P[:, c // 4, (c % 4) * 128:(c % 4 + 1) * 128],
                                           cw[:, 4 * c:4 * c + 4, :].rearrange("p t e -> p (t e)"), ident[:, :])
                if c % 4 == 3:
                    last.then_inc(cw_turned, 1)
            pe.wait_ge(cwT_ready, 2)
            for c in range(NCH):
                if c >= 2:
                    pe.wait_ge(bias_added, c - 1)
                for t in range(4):
                    last = nc.tensor.matmul(P[:, 4 - 4 * (c % 2) + t, 0:D], cwT[32 * t:32 * t + 16, c, :], b2_sb[32 * t:32 * t + 16, :],
                                            start=True, stop=True)
                last.then_inc(bias_ready, 1)

            def up(i, par, n, c):
                pe.wait_ge(relu_done, n * 2 + 2)
                for m in range(2):
                    cols = slice(m * 128, (m + 1) * 128)
                    for k in range(2):
                        here = bass.ds(c * CH, CH)
                        nc.tensor.matmul(P[:, 2 * par + m, :], w_hi[i][:, k, cols], x_hi[:, k, here],
                                         start=(k == 0), stop=False)
                        nc.tensor.matmul(P[:, 2 * par + m, :], w_hi[i][:, k, cols], x_lo[:, k, here],
                                         start=False, stop=False)
                        last = nc.tensor.matmul(P[:, 2 * par + m, :], w_lo[i][:, k, cols], x_hi[:, k, here],
                                                start=False, stop=(k == 1))
                    last.then_inc(up_ready, 1)

            def down(i, par, n):
                pe.wait_ge(added, n * 4 + 4)
                pe.wait_ge(h_hi_ready, n * 2 + 2)
                for t in range(4):
                    sums = P[:, 4 + 2 * par + t // 2, (t % 2) * D:(t % 2) * D + D]
                    cols = slice(t * 128, (t + 1) * 128)
                    for k in range(2):
                        nc.tensor.matmul(sums, h_hi[par][:, k, cols], w_hi[i][:, 2 + k, :], start=(k == 0), stop=False)
                        nc.tensor.matmul(sums, h_hi[par][:, k, cols], w_lo[i][:, 2 + k, :], start=False, stop=False)
                    for k in range(2):
                        if t == 0:
                            pe.wait_ge(h_lo_ready, n * 2 + k + 5)
                        last = nc.tensor.matmul(sums, h_lo[par][:, k, cols], w_hi[i][:, 2 + k, :],
                                                start=False, stop=(k == 1))
                    if t % 2:
                        last.then_inc(down_ready, 1)

            def expert(i, e, final):
                with nc.tensor.Fori(0, NCH // 2 - 1) as j:
                    up(i, 1, e * NCH + j * 2 + 1, j * 2 + 1)
                    down(i, 0, e * NCH + j * 2)
                    up(i, 0, e * NCH + j * 2 + 2, j * 2 + 2)
                    down(i, 1, e * NCH + j * 2 + 1)
                up(i, 1, e * NCH + NCH - 1, NCH - 1)
                down(i, 0, e * NCH + NCH - 2)
                if not final:
                    pe.wait_ge(w_lo_ready, e + 2)
                    up(1 - i, 0, e * NCH + NCH, 0)
                down(i, 1, e * NCH + NCH - 1)

            pe.wait_ge(bias_added, NCH)
            pe.wait_ge(x_lo_ready, NCH)
            pe.wait_ge(w_lo_ready, 1)
            up(0, 0, 0, 0)
            with nc.tensor.Fori(0, NE // 2 - 1) as pair:
                expert(0, pair * 2, False)
                expert(1, pair * 2 + 1, False)
            expert(0, NE - 2, False)
            expert(1, NE - 1, True)

        @block.scalar
        def _(act):
            act.wait_ge(loaded, ROUTER_LOADS)
            with nc.scalar.Fori(0, NCH // 2) as j:
                for p in range(2):
                    c = j * 2 + p
                    here = nc.scalar.snap(c * CH)
                    act.wait_ge(logits_ready, c + 1)
                    act.wait_ge(log_turned, c + 1)
                    nc.scalar.activation(logT[p][:, :], P[0:16, p, :], ACT.Identity,
                                         bias=rb_sb[:, 0:1]).then_inc(logT_ready, 1)
                    nc.scalar.copy(x_hi[:, :, bass.ds(here, CH)], XT[:, :, bass.ds(here, CH)]).then_inc(x_hi_ready, 1)

            def split(i, e):
                act.wait_ge(w_loaded, (e + 1) * 16)
                nc.scalar.copy(w_hi[i][:, :, :], w_raw[:, :, :]).then_inc(w_hi_ready, 1)

            split(0, 0)
            act.wait_ge(route, 2)
            nc.scalar.activation(expd[:, :, :], expd[:, :, :], ACT.Exp).then_inc(exp_ready, 1)
            for half in range(2):
                act.wait_ge(cw_turned, half + 1)
                nc.scalar.copy(cwT[:, 4 * half:4 * half + 4, :],
                               P[:, half, :].rearrange("p (c n) -> p c n", n=128)).then_inc(cwT_ready, 1)

            def relus(par, n, i):
                act.wait_ge(down_ready, n * 2 + 2)
                act.wait_ge(h_lo_ready, n * 2 + 2)
                for m in range(2):
                    act.wait_ge(up_ready, n * 2 + m + 1)
                    nc.scalar.activation(hT[par][:, m, :], P[:, 2 * par + m, :], ACT.Relu,
                                         bias=b1_sb[i][:, m:m + 1]).then_inc(relu_done, 1)
                    act.wait_ge(relu_done, n * 2 + m + 5)
                    nc.scalar.copy(h_hi[par][:, m, :], hT[par][:, m, :]).then_inc(h_hi_ready, 1)

            def passes(i, pair, final):
                e = pair * 2 + i
                act.wait_ge(b1_loaded[i], (pair + 1) * 16)
                relus(0, e * NCH, i)
                relus(1, e * NCH + 1, i)
                if not final:
                    split(1 - i, e + 1)
                with nc.scalar.Fori(1, NCH // 2) as j:
                    relus(0, e * NCH + j * 2, i)
                    relus(1, e * NCH + j * 2 + 1, i)

            with nc.scalar.Fori(0, NE // 2 - 1) as pair:
                passes(0, pair, False)
                passes(1, pair, False)
            passes(0, NE // 2 - 1, False)
            passes(1, NE // 2 - 1, True)

        @block.gpsimd
        def _(pool):
            with nc.gpsimd.Fori(0, NCH) as c:
                here = nc.gpsimd.snap(c * CH)
                pool.wait_ge(x_hi_ready, c + 1)
                nc.gpsimd.tensor_tensor(x_lo[:, :, bass.ds(here, CH)], XT[:, :, bass.ds(here, CH)],
                                        x_hi[:, :, bass.ds(here, CH)], ALU.subtract).then_inc(x_lo_ready, 1)

            def split(i, e):
                pool.wait_ge(w_hi_ready, e + 1)
                nc.gpsimd.tensor_tensor(w_lo[i][:, :, :], w_raw[:, :, :], w_hi[i][:, :, :],
                                        ALU.subtract).then_inc(w_lo_ready, 1)

            def low_parts(par, n):
                for m in range(2):
                    pool.wait_ge(h_hi_ready, n * 2 + m + 1)
                    nc.gpsimd.tensor_tensor(h_lo[par][:, m, :], hT[par][:, m, :], h_hi[par][:, m, :],
                                            ALU.subtract).then_inc(h_lo_ready, 1)

            def passes(i, pair):
                e = pair * 2 + i
                low_parts(0, e * NCH)
                low_parts(1, e * NCH + 1)
                split(1 - i, e + 1)
                with nc.gpsimd.Fori(1, NCH // 2) as j:
                    low_parts(0, e * NCH + j * 2)
                    low_parts(1, e * NCH + j * 2 + 1)

            split(0, 0)
            pool.wait_ge(const_ready, 4)
            pool.wait_ge(lns.half, 1)
            with nc.gpsimd.Fori(0, NE // 2 - 1) as pair:
                passes(0, pair)
                passes(1, pair)
            passes(0, NE // 2 - 1)
            base = (NE - 1) * NCH
            low_parts(0, base)
            with nc.gpsimd.Fori(0, NCH // 2 - 1) as j:
                low_parts(1, base + j * 2 + 1)
                ln_pool(nc, pool, ln, lns, j * 2)
                low_parts(0, base + j * 2 + 2)
                ln_pool(nc, pool, ln, lns, j * 2 + 1)
            low_parts(1, base + NCH - 1)
            ln_pool(nc, pool, ln, lns, NCH - 2)
            ln_pool(nc, pool, ln, lns, NCH - 1)

        @block.vector
        def _(dve):
            ln_start(nc, ln, lns)
            nc.vector.memset(spare[:, 7:8], 0.0).then_inc(stored, 16)
            nc.vector.memset(cw[:, :, :], 0.0).then_inc(const_ready, 1)
            nc.vector.memset(spare[:, 0:1], 0.0).then_inc(relu_done, 4)
            nc.vector.memset(spare[:, 1:2], 0.0).then_inc(down_ready, 4)
            nc.vector.memset(spare[:, 2:3], 0.0).then_inc(added, 8)
            nc.vector.memset(spare[:, 3:4], 0.0).then_inc(h_lo_ready, 4)
            nc.vector.memset(spare[:, 8:9], 0.0).then_inc(logT_ready, 2)
            nc.vector.memset(spare[:, 9:10], 0.0).then_inc(log_turned, 2)
            dve.wait_ge(const_ready, 1)
            nc.vector.memset(cw[:, :, 15:16], 1.0).then_inc(const_ready, 1)
            nc.vector.memset(best[:, :, :], 0.0).then_inc(const_ready, 1)
            dve.wait_ge(const_ready, 3)
            nc.vector.memset(spare[:, 10:11], 0.0).then_inc(const_ready, 1)
            dve.wait_ge(loaded, ROUTER_LOADS)
            logits = P[:, 2, :].rearrange("p (t e) -> p t e", e=16)[:, :, 0:15]
            dve.wait_ge(log_turned, NCH + 2)
            nc.vector.tensor_reduce(top[:, :], logits, axis=AX.X, op=ALU.max).then_inc(route, 1)
            dve.wait_ge(route, 1)
            nc.vector.tensor_tensor(expd[:, :, :], logits, top[:, :].unsqueeze(2).to_broadcast([128, NT, 15]),
                                    ALU.subtract).then_inc(route, 1)
            dve.wait_ge(exp_ready, 1)
            nc.vector.tensor_reduce(total[:, :], expd[:, :, :], axis=AX.X, op=ALU.add).then_inc(route, 1)
            dve.wait_ge(route, 3)
            nc.vector.reciprocal(total[:, :], total[:, :]).then_inc(route, 1)
            dve.wait_ge(route, 4)
            nc.vector.tensor_tensor(probs[:, :, 0:15], expd[:, :, :],
                                    total[:, :].unsqueeze(2).to_broadcast([128, NT, 15]), ALU.mult).then_inc(route, 1)
            dve.wait_ge(route, 5)
            nc.vector.memset(spare[:, 4:5], 0.0)
            for t in range(NT):
                last = nc.vector.max(best[:, t, :], probs[:, t, 0:15])
            last.then_inc(route, 1)
            dve.wait_ge(route, 6)
            nc.vector.tensor_copy(chosen[:, :, 0:3], best[:, :, 0:3]).then_inc(route, 1)
            dve.wait_ge(route, 7)
            nc.vector.memset(spare[:, 5:6], 0.0)
            for t in range(NT):
                last = nc.vector.match_replace(rest[:, t, :], chosen[:, t, :], probs[:, t, :], 0.0)
            last.then_inc(route, 1)
            dve.wait_ge(route, 8)
            nc.vector.tensor_tensor(cw[:, :, 0:15], probs[:, :, 0:15], rest[:, :, 0:15],
                                    ALU.subtract).then_inc(cw_ready, 1)
            with nc.vector.Fori(0, NCH // 2) as j:
                for p in range(2):
                    c = j * 2 + p
                    dve.wait_ge(bias_ready, c + 1)
                    nc.vector.tensor_tensor(XN[:, bass.ds(c * 4, 4), :], P[:, 4 - 4 * p:8 - 4 * p, 0:D],
                                            XN[:, bass.ds(c * 4, 4), :], ALU.add).then_inc(bias_added, 1)
            dve.wait_ge(cw_ready, 1)
            dve.wait_ge(bias_added, NCH)

            def add(par, n, c, e, last_expert):
                for t in range(4):
                    dve.wait_ge(down_ready, n * 2 + 4 + t // 2 + 1)
                    tile = c * 4 + t
                    dst = ln.res[:, t, :] if last_expert else XN[:, tile, :]
                    nc.vector.scalar_tensor_tensor(dst, P[:, 4 + 2 * par + t // 2, (t % 2) * D:(t % 2) * D + D],
                                                   cw[:, tile, bass.ds(e, 1)], XN[:, tile, :],
                                                   ALU.mult, ALU.add).then_inc(added, 1)

            with nc.vector.Fori(0, NE - 1) as e:
                with nc.vector.Fori(0, NCH // 2) as j:
                    dve.wait_ge(added, e * 32 + j * 8 + 8)
                    add(0, e * NCH + j * 2, j * 2, e, False)
                    add(1, e * NCH + j * 2 + 1, j * 2 + 1, e, False)
            with nc.vector.Fori(0, NCH // 2) as j:
                for par in range(2):
                    c = j * 2 + par
                    dve.wait_ge(lns.done, (c + 1) * 4)
                    add(par, (NE - 1) * NCH + c, c, NE - 1, True)
                    dve.wait_ge(added, (NE - 1) * 32 + c * 4 + 12)
                    ln_dve(nc, dve, ln, lns, c, stored, 16)


def block_kernel(nc, T, out):
    bc_scratch = nc.dram_tensor("bc_scratch", [2 * NS, CH], FP32, kind="Internal").ap()
    ctx = ExitStack()
    with ctx:
        XN = ctx.enter_context(nc.sbuf_tensor("XN", [128, TOK // 128, D], FP32))
        ident = ctx.enter_context(nc.sbuf_tensor("ident", [128, 128], FP32))
        P = ctx.enter_context(nc.psum_tensor("P", [128, 8, CH], FP32))
        ident_loaded = ctx.enter_context(nc.semaphore("ident_loaded"))
        with nc.Block() as block:
            @block.sync
            def _(sync):
                sync.dma_start(ident[:, :], T["eye"]).then_inc(ident_loaded, 16)
                sync.wait_ge(ident_loaded, 16)
        mamba_phase(nc, XN, P, ident, T["x_tok"], T["x_feat"], T["m_w_in"], T["m_conv_w"], T["m_conv_b"],
                    T["m_w_x"], T["m_w_dt"], T["m_b_dt"], T["m_a_log"], T["m_w_out"], bc_scratch)
        XT = ctx.enter_context(nc.sbuf_tensor("XT", [128, 2, TOK], FP32))
        ffn_phase(nc, XN, XT, P, ident, T["f_w1"], T["f_b1"], T["f_w2"], T["f_b2"])
        attn_phase(nc, XN, XT, P, ident, T["a_wqk"], T["a_wv"], T["a_wo"], T["a_bo"], T["a_masks"])
        moe_phase(nc, XN, XT, P, ident, T["e_rw"], T["e_rb"], T["e_w"], T["e_b1"], T["e_b2"], T["e_pads"], out)


def _partitioned(a):
    return a.reshape((-1, 128) + a.shape[1:]).swapaxes(0, 1)


def _contraction_first(w):
    return _partitioned(w.T)


def _masks():
    r, c = np.arange(128)[:, None], np.arange(192)[None, :]
    band = (r <= c) & (c <= r + 64)
    allowed = [c <= r, band, band & (c >= 64), r <= c, band]
    return np.where(np.stack(allowed, 1), 0.0, -1e30).astype(np.float32)


def kernel(**inputs):
    import concourse.bacc as _bacc
    from concourse.bass_utils import run_bass_kernel_spmd as _run

    a = {k: np.asarray(v) for k, v in inputs.items()}
    x = a["L0_attn_x"].reshape(TOK, D)
    experts = {k: np.concatenate([a["L1_ffn_e" + k], a["L1_ffn_s" + k][None]]) for k in ("W1", "b1", "W2", "b2")}
    wo = np.zeros((4, 32, 4, D), np.float32)
    wo[:, :16] = a["L1_attn_Wo"].T.reshape(4, 4, 16, D).transpose(1, 2, 0, 3)
    wqk = np.stack([_contraction_first(a["L1_attn_" + w]).reshape(128, 2, 4, 64) for w in ("Wq", "Wk")],
                   3).reshape(128, 2, 512)
    router_w = np.zeros((D, 16), np.float32)
    router_w[:, :15] = a["L1_ffn_router_W"]
    router_b = np.zeros((16, 1), np.float32)
    router_b[:15, 0] = a["L1_ffn_router_b"]
    b2 = np.zeros((4, 32, D), np.float32)
    b2[:, :16] = experts["b2"]
    laid_out = {
        "eye": np.eye(128, dtype=np.float32),
        "x_tok": _partitioned(x),
        "x_feat": _contraction_first(x),
        "m_w_in": _contraction_first(a["L0_attn_W_in"]),
        "m_conv_w": _partitioned(a["L0_attn_conv_w"].reshape(512, 4)),
        "m_conv_b": _partitioned(a["L0_attn_conv_b"]),
        "m_w_x": _contraction_first(a["L0_attn_W_x"]),
        "m_w_dt": a["L0_attn_W_dt"].T,
        "m_b_dt": _partitioned(a["L0_attn_b_dt"]),
        "m_a_log": _partitioned(a["L0_attn_A_log"]),
        "m_w_out": _contraction_first(a["L0_attn_W_out"]),
        "f_w1": _contraction_first(a["L0_ffn_w1"]),
        "f_b1": _partitioned(a["L0_ffn_b1"]),
        "f_w2": _contraction_first(a["L0_ffn_w2"]),
        "f_b2": a["L0_ffn_b2"],
        "a_wqk": wqk,
        "a_wv": _contraction_first(a["L1_attn_Wv"]),
        "a_wo": wo.reshape(128, 4, D),
        "a_bo": a["L1_attn_bo"],
        "a_masks": _masks(),
        "e_rw": _partitioned(router_w),
        "e_rb": router_b,
        "e_w": np.concatenate([experts[k].reshape(16, 2, 128, D).transpose(0, 2, 1, 3) for k in ("W1", "W2")], 2),
        "e_b1": experts["b1"].reshape(16, 2, 128).transpose(0, 2, 1),
        "e_b2": b2.reshape(128, D),
        "e_pads": np.broadcast_to(-1.0 - np.arange(9, dtype=np.float32), (128, TOK // 128, 9)),
    }
    nc = _bacc.Bacc("TRN2", target_bir_lowering=False, num_devices=1)
    arrays = {"in_" + n: np.ascontiguousarray(v) for n, v in laid_out.items()}
    T = {n: nc.dram_tensor("in_" + n, v.shape, mybir.dt.from_np(v.dtype), kind="ExternalInput").ap()
         for n, v in laid_out.items()}
    out = nc.dram_tensor("out", (128, TOK // 128, D), FP32, kind="ExternalOutput").ap()
    block_kernel(nc, T, out)
    r = _run(nc, [arrays], core_ids=[0])
    return r.results[0]["out"].transpose(1, 0, 2).reshape(NB, SEQ, D)
```
